# Optimizing a Trainium2 kernel written in Bass

```python
import numpy as np
import jax
import jax.numpy as jnp

def _softmax(x, axis=-1):
    return jax.nn.softmax(x, axis=axis)

def _gelu(x):
    return jax.nn.gelu(x, approximate=True)

def _silu(x):
    return jax.nn.silu(x)

def _sigmoid(x):
    return jax.nn.sigmoid(x)

def _layernorm(x, axis=-1, eps=1e-05):
    m = jnp.mean(x, axis=axis, keepdims=True)
    v = jnp.var(x, axis=axis, keepdims=True)
    return (x - m) / jnp.sqrt(v + eps)

def _scatter_add(tgt, idx, src, axis=0):
    return tgt.at[idx].add(src)

def _segment_sum(src, seg, n):
    return jax.ops.segment_sum(src, seg, n)
kernel_name = 'mk_xattn_ffn_d4_seqx_r8_e6dd88'

def setup_inputs(seed: int=0):
    np.random.seed(seed)
    _w = jnp.asarray

    def _rec_inputs():
        import jax
        import jax.numpy as jnp
        _rk = jax.random.key(seed)
        x = -0.0003929 + 0.9999 * jax.random.normal(jax.random.fold_in(_rk, 1), (16, 128, 128), jnp.float32)
        _lenS = 128 - jax.random.randint(jax.random.fold_in(_rk, 7), (16,), 0, max(1, 128 // 4) + 1, jnp.int32)
        _lenS2 = 128 - jax.random.randint(jax.random.fold_in(_rk, 8), (16,), 0, max(1, 128 // 4) + 1, jnp.int32)
        _ctx_1024P = jax.random.normal(jax.random.fold_in(_rk, 11), (16, 16, 128), jnp.float32)
        _ctx_1024c = jax.random.dirichlet(jax.random.fold_in(_rk, 511), 0.3 * jnp.ones((16,), jnp.float32), (16, 128))
        _ctx_1024t = jnp.einsum('bsk,bkd->bsd', _ctx_1024c, _ctx_1024P)
        _ctx_1024t = _ctx_1024t * jax.lax.rsqrt(jnp.mean(jnp.square(_ctx_1024t)) + 1e-12) * 0.953939
        ctx_1024 = 2.81802e-05 + 1.00001 * (_ctx_1024t + 0.3 * jax.random.normal(jax.random.fold_in(_rk, 611), (16, 128, 128), jnp.float32))
        _validS = jnp.arange(128)[None, :] < _lenS[:, None]
        _validS2 = jnp.arange(128)[None, :] < _lenS2[:, None]
        _causal = jnp.tril(jnp.ones((128, 128), dtype=bool))
        mask_BxS2_bf1 = jnp.ones((16, 128), dtype=bool)
        mask_SxS2_ff0 = jnp.where(jnp.ones((128, 128), dtype=bool), 0.0, -1000000000.0).astype(jnp.float32)
        mask_BxS2_bf0 = jnp.logical_not(jnp.ones((16, 128), dtype=bool))
        return (x, ctx_1024, mask_BxS2_bf1, mask_SxS2_ff0, mask_BxS2_bf0)
    x, ctx_1024, mask_BxS2_bf1, mask_SxS2_ff0, mask_BxS2_bf0 = _rec_inputs()

    def _L0_xattn_setup():
        import jax, jax.numpy as jnp
        import numpy as np
        D_MODEL = 128
        NUM_HEADS = 16
        FOCUS = 3
        EPS = 1e-06

        def _focused_feature_map(x, scale):
            x = jax.nn.relu(x) + EPS
            x = x / scale
            x_norm = jnp.linalg.norm(x, axis=-1, keepdims=True)
            xp = x ** FOCUS
            return xp / jnp.linalg.norm(xp, axis=-1, keepdims=True) * x_norm
        key = jax.random.key(seed)
        ks = jax.random.split(key, 10)
        b, n, d = (4, 512, D_MODEL)
        s = 0.02
        return {'input_q': jax.random.normal(ks[0], (b, n, d), jnp.float32), 'input_k': jax.random.normal(ks[1], (b, n, d), jnp.float32), 'input_v': jax.random.normal(ks[2], (b, n, d), jnp.float32), 'Wq': jax.random.normal(ks[3], (d, d), jnp.float32) * s, 'bq': jnp.zeros((d,), jnp.float32), 'Wk': jax.random.normal(ks[4], (d, d), jnp.float32) * s, 'bk': jnp.zeros((d,), jnp.float32), 'Wv': jax.random.normal(ks[5], (d, d), jnp.float32) * s, 'bv': jnp.zeros((d,), jnp.float32), 'scale': jnp.zeros((1, 1, d), jnp.float32)}
    _L0_xattn_all = _L0_xattn_setup()
    _L0_xattn_in = {k: v for k, v in _L0_xattn_all.items() if k in ('Wq', 'bq', 'Wk', 'bk', 'Wv', 'bv', 'scale')}
    del _L0_xattn_all

    def _L0_ffn_setup():
        import jax, jax.numpy as jnp
        import numpy as np
        EMB = 128
        HID = 256
        HEADS = 16
        HEAD_DIM = EMB // HEADS
        EXPERTS = 8
        TOPK = 2
        EPS = 1e-05

        def layernorm(x, scale, shift):
            mean = jnp.mean(x, axis=-1, keepdims=True)
            var = jnp.mean((x - mean) ** 2, axis=-1, keepdims=True)
            return scale * (x - mean) / jnp.sqrt(var + EPS) + shift

        def attention(x, wq, wk, wv, wo, bo):
            b, t, _ = x.shape
            q = (x @ wq).reshape(b, t, HEADS, HEAD_DIM)
            k = (x @ wk).reshape(b, t, HEADS, HEAD_DIM)
            v = (x @ wv).reshape(b, t, HEADS, HEAD_DIM)
            scores = jnp.einsum('bqhd,bkhd->bhqk', q, k)
            mask = jnp.arange(t)[:, None] < jnp.arange(t)[None, :]
            scores = jnp.where(mask, -jnp.inf, scores)
            attn = jax.nn.softmax(scores / np.sqrt(HEAD_DIM), axis=-1)
            ctx = jnp.einsum('bhqk,bkhd->bqhd', attn, v).reshape(b, t, EMB)
            return ctx @ wo + bo

        def moe_ff(x, gate_w, w1, w2, w3):
            b, t, d = x.shape
            xf = x.reshape(b * t, d)
            scores = xf @ gate_w
            topk_scores, topk_idx = jax.lax.top_k(scores, TOPK)
            topk_probs = jax.nn.softmax(topk_scores, axis=-1)
            weight = jnp.sum(jax.nn.one_hot(topk_idx, EXPERTS, dtype=xf.dtype) * topk_probs[..., None], axis=1)
            h = jax.nn.silu(jnp.einsum('td,edh->eth', xf, w1)) * jnp.einsum('td,edh->eth', xf, w2)
            out_e = jnp.einsum('eth,ehd->etd', h, w3)
            out = jnp.einsum('etd,te->td', out_e, weight)
            return out.reshape(b, t, d)
        key = jax.random.key(seed)
        ks = jax.random.split(key, 12)
        s = lambda k, shape, fan: jax.random.normal(k, shape, jnp.float32) / np.sqrt(fan)
        return {'x': jax.random.normal(ks[0], (2, 256, EMB), jnp.float32), 'ln1_scale': jnp.ones((EMB,), jnp.float32), 'ln1_shift': jnp.zeros((EMB,), jnp.float32), 'wq': s(ks[1], (EMB, EMB), EMB), 'wk': s(ks[2], (EMB, EMB), EMB), 'wv': s(ks[3], (EMB, EMB), EMB), 'wo': s(ks[4], (EMB, EMB), EMB), 'bo': jnp.zeros((EMB,), jnp.float32), 'ln2_scale': jnp.ones((EMB,), jnp.float32), 'ln2_shift': jnp.zeros((EMB,), jnp.float32), 'gate_w': s(ks[5], (EMB, EXPERTS), EMB), 'w1': s(ks[6], (EXPERTS, EMB, HID), EMB), 'w2': s(ks[7], (EXPERTS, EMB, HID), EMB), 'w3': s(ks[8], (EXPERTS, HID, EMB), HID)}
    _L0_ffn_all = _L0_ffn_setup()
    _L0_ffn_in = {k: v for k, v in _L0_ffn_all.items() if k in ('ln1_scale', 'ln1_shift', 'wq', 'wk', 'wv', 'wo', 'bo', 'ln2_scale', 'ln2_shift', 'gate_w', 'w1', 'w2', 'w3')}
    del _L0_ffn_all

    def _L1_xattn_setup():
        import jax, jax.numpy as jnp
        import numpy as np
        D_MODEL = 128
        N_HEADS = 16
        HEAD_DIM = D_MODEL // N_HEADS
        key = jax.random.key(seed)
        ks = jax.random.split(key, 9)
        B, T, S, D = (4, 256, 64, D_MODEL)
        sc = 1.0 / np.sqrt(D)
        return {'x': jax.random.normal(ks[0], (B, T, D), dtype=jnp.float32), 'context': jax.random.normal(ks[1], (B, S, D), dtype=jnp.float32), 'context_mask': jnp.ones((B, S), dtype=bool), 'Wq': jax.random.normal(ks[2], (D, D), dtype=jnp.float32) * sc, 'bq': jnp.zeros((D,), dtype=jnp.float32), 'Wkv': jax.random.normal(ks[3], (D, 2 * D), dtype=jnp.float32) * sc, 'bkv': jnp.zeros((2 * D,), dtype=jnp.float32), 'Wp': jax.random.normal(ks[4], (D, D), dtype=jnp.float32) * sc, 'bp': jnp.zeros((D,), dtype=jnp.float32)}
    _L1_xattn_all = _L1_xattn_setup()
    _L1_xattn_in = {k: v for k, v in _L1_xattn_all.items() if k in ('Wq', 'bq', 'Wkv', 'bkv', 'Wp', 'bp')}
    del _L1_xattn_all

    def _L1_ffn_setup():
        import jax, jax.numpy as jnp
        import numpy as np
        D_MODEL = 128
        MLP_DIM = 512
        N_EXPERTS = 8
        B, T = (4, 128)
        key = jax.random.key(seed)
        ks = jax.random.split(key, 7)
        scale_in = (1.0 / D_MODEL) ** 0.5
        scale_out = (1.0 / MLP_DIM) ** 0.5
        bound_g = (1.0 / D_MODEL) ** 0.5
        w_gate = jax.random.uniform(ks[0], (D_MODEL, N_EXPERTS), minval=-bound_g, maxval=bound_g, dtype=jnp.float32)
        b_gate = jax.random.uniform(ks[1], (N_EXPERTS,), minval=-bound_g, maxval=bound_g, dtype=jnp.float32)
        W1 = jax.random.uniform(ks[2], (N_EXPERTS, D_MODEL, MLP_DIM), minval=-scale_in, maxval=scale_in, dtype=jnp.float32)
        b1 = jnp.zeros((N_EXPERTS, MLP_DIM), dtype=jnp.float32)
        W2 = jax.random.uniform(ks[3], (N_EXPERTS, MLP_DIM, D_MODEL), minval=-scale_out, maxval=scale_out, dtype=jnp.float32)
        b2 = jnp.zeros((N_EXPERTS, D_MODEL), dtype=jnp.float32)
        x = jax.random.normal(ks[4], (B, T, D_MODEL), dtype=jnp.float32)
        return {'x': x, 'w_gate': w_gate, 'b_gate': b_gate, 'W1': W1, 'b1': b1, 'W2': W2, 'b2': b2}
    _L1_ffn_all = _L1_ffn_setup()
    _L1_ffn_in = {k: v for k, v in _L1_ffn_all.items() if k in ('w_gate', 'b_gate', 'W1', 'b1', 'W2', 'b2')}
    del _L1_ffn_all

    def _L2_xattn_setup():
        import jax, jax.numpy as jnp
        import numpy as np
        EMBED_DIM = 128
        NUM_HEADS = 16
        HEAD_DIM = EMBED_DIM // NUM_HEADS
        SCALE = HEAD_DIM ** (-0.5)
        key = jax.random.key(seed)
        ks = jax.random.split(key, 12)
        B, T, S, C = (4, 256, 256, EMBED_DIM)
        inp = {'query': jax.random.normal(ks[0], (B, T, C), dtype=jnp.float32), 'key': jax.random.normal(ks[1], (B, S, C), dtype=jnp.float32), 'value': jax.random.normal(ks[2], (B, S, C), dtype=jnp.float32), 'attn_mask': jnp.zeros((T, S), dtype=jnp.float32), 'key_padding_mask': jnp.zeros((B, S), dtype=bool)}
        std = C ** (-0.5)
        for i, name in enumerate(['q', 'k', 'v', 'out']):
            inp[f'W{name}'] = jax.random.normal(ks[3 + i], (C, C), dtype=jnp.float32) * std
            inp[f'b{name}'] = jnp.zeros((C,), dtype=jnp.float32)
        return inp
    _L2_xattn_all = _L2_xattn_setup()
    _L2_xattn_in = {k: v for k, v in _L2_xattn_all.items() if k in ('Wq', 'bq', 'Wk', 'bk', 'Wv', 'bv', 'Wout', 'bout')}
    del _L2_xattn_all

    def _L2_ffn_setup():
        import jax, jax.numpy as jnp
        import numpy as np
        H, E, DFF = (128, 8, 512)
        key = jax.random.key(seed)
        ks = jax.random.split(key, 7)
        s = lambda *shape: 1.0 / np.sqrt(shape[-2] if len(shape) > 1 else shape[-1])
        x = jax.random.normal(ks[0], (2, 256, H), dtype=jnp.float32)
        Wr = jax.random.normal(ks[1], (H, E), dtype=jnp.float32) * (1.0 / np.sqrt(H))
        br = jnp.zeros((E,), dtype=jnp.float32)
        W1 = jax.random.normal(ks[2], (E, H, DFF), dtype=jnp.float32) * (1.0 / np.sqrt(H))
        b1 = jnp.zeros((E, DFF), dtype=jnp.float32)
        W2 = jax.random.normal(ks[3], (E, DFF, H), dtype=jnp.float32) * (1.0 / np.sqrt(DFF))
        b2 = jnp.zeros((E, H), dtype=jnp.float32)
        return {'x': x, 'Wr': Wr, 'br': br, 'W1': W1, 'b1': b1, 'W2': W2, 'b2': b2}
    _L2_ffn_all = _L2_ffn_setup()
    _L2_ffn_in = {k: v for k, v in _L2_ffn_all.items() if k in ('Wr', 'br', 'W1', 'b1', 'W2', 'b2')}
    del _L2_ffn_all

    def _L3_xattn_setup():
        import jax, jax.numpy as jnp
        import numpy as np
        N_HEADS = 16
        KQ_DIM = 64
        EMB_DIM = 128
        CTX_DIM = 128
        EPS = 1e-05

        def _layernorm(x, w, b):
            mu = jnp.mean(x, axis=-1, keepdims=True)
            var = jnp.mean(jnp.square(x - mu), axis=-1, keepdims=True)
            return (x - mu) * jax.lax.rsqrt(var + EPS) * w + b
        key = jax.random.key(seed)
        ks = jax.random.split(key, 10)
        B, SQ, SK = (2, 256, 256)
        inner = N_HEADS * KQ_DIM
        s_e = 1.0 / np.sqrt(EMB_DIM)
        s_c = 1.0 / np.sqrt(CTX_DIM)
        s_i = 1.0 / np.sqrt(inner)
        return {'emb': jax.random.normal(ks[0], (B, SQ, EMB_DIM), jnp.float32), 'context': jax.random.normal(ks[1], (B, SK, CTX_DIM), jnp.float32), 'Wq': jax.random.uniform(ks[2], (inner, EMB_DIM), jnp.float32, -s_e, s_e), 'Wk': jax.random.uniform(ks[3], (inner, CTX_DIM), jnp.float32, -s_c, s_c), 'Wv': jax.random.uniform(ks[4], (inner, CTX_DIM), jnp.float32, -s_c, s_c), 'Wu': jax.random.uniform(ks[5], (EMB_DIM, inner), jnp.float32, -s_i, s_i), 'bu': jax.random.uniform(ks[6], (EMB_DIM,), jnp.float32, -s_i, s_i), 'qn_w': jnp.ones((KQ_DIM,), jnp.float32), 'qn_b': jnp.zeros((KQ_DIM,), jnp.float32), 'kn_w': jnp.ones((KQ_DIM,), jnp.float32), 'kn_b': jnp.zeros((KQ_DIM,), jnp.float32)}
    _L3_xattn_all = _L3_xattn_setup()
    _L3_xattn_in = {k: v for k, v in _L3_xattn_all.items() if k in ('Wq', 'Wk', 'Wv', 'Wu', 'bu', 'qn_w', 'qn_b', 'kn_w', 'kn_b')}
    del _L3_xattn_all

    def _L3_ffn_setup():
        import jax, jax.numpy as jnp
        import numpy as np
        DIM = 128
        HIDDEN = 384
        SCALE = 1.0 / 127.0

        def _dequant(w_int, dtype):
            return w_int.astype(dtype) * jnp.asarray(SCALE, dtype)
        key = jax.random.key(seed)
        k_x, k_g, k_u, k_d = jax.random.split(key, 4)
        x = jax.random.normal(k_x, (4, 256, DIM), dtype=jnp.float32)
        w_gate = jax.random.randint(k_g, (HIDDEN, DIM), -127, 128, dtype=jnp.int32)
        w_up = jax.random.randint(k_u, (HIDDEN, DIM), -127, 128, dtype=jnp.int32)
        w_down = jax.random.randint(k_d, (DIM, HIDDEN), -127, 128, dtype=jnp.int32)
        return {'x': x, 'w_gate': w_gate, 'w_up': w_up, 'w_down': w_down}
    _L3_ffn_all = _L3_ffn_setup()
    _L3_ffn_in = {k: v for k, v in _L3_ffn_all.items() if k in ('w_gate', 'w_up', 'w_down')}
    del _L3_ffn_all
    return {'x': x, 'ctx_1024': ctx_1024, 'mask_BxS2_bf1': mask_BxS2_bf1, 'mask_SxS2_ff0': mask_SxS2_ff0, 'mask_BxS2_bf0': mask_BxS2_bf0, 'L0_xattn_Wq': _L0_xattn_in['Wq'], 'L0_xattn_bq': _L0_xattn_in['bq'], 'L0_xattn_Wk': _L0_xattn_in['Wk'], 'L0_xattn_bk': _L0_xattn_in['bk'], 'L0_xattn_Wv': _L0_xattn_in['Wv'], 'L0_xattn_bv': _L0_xattn_in['bv'], 'L0_xattn_scale': _L0_xattn_in['scale'], 'L0_ffn_ln1_scale': _L0_ffn_in['ln1_scale'], 'L0_ffn_ln1_shift': _L0_ffn_in['ln1_shift'], 'L0_ffn_wq': _L0_ffn_in['wq'], 'L0_ffn_wk': _L0_ffn_in['wk'], 'L0_ffn_wv': _L0_ffn_in['wv'], 'L0_ffn_wo': _L0_ffn_in['wo'], 'L0_ffn_bo': _L0_ffn_in['bo'], 'L0_ffn_ln2_scale': _L0_ffn_in['ln2_scale'], 'L0_ffn_ln2_shift': _L0_ffn_in['ln2_shift'], 'L0_ffn_gate_w': _L0_ffn_in['gate_w'], 'L0_ffn_w1': _L0_ffn_in['w1'], 'L0_ffn_w2': _L0_ffn_in['w2'], 'L0_ffn_w3': _L0_ffn_in['w3'], 'L1_xattn_Wq': _L1_xattn_in['Wq'], 'L1_xattn_bq': _L1_xattn_in['bq'], 'L1_xattn_Wkv': _L1_xattn_in['Wkv'], 'L1_xattn_bkv': _L1_xattn_in['bkv'], 'L1_xattn_Wp': _L1_xattn_in['Wp'], 'L1_xattn_bp': _L1_xattn_in['bp'], 'L1_ffn_w_gate': _L1_ffn_in['w_gate'], 'L1_ffn_b_gate': _L1_ffn_in['b_gate'], 'L1_ffn_W1': _L1_ffn_in['W1'], 'L1_ffn_b1': _L1_ffn_in['b1'], 'L1_ffn_W2': _L1_ffn_in['W2'], 'L1_ffn_b2': _L1_ffn_in['b2'], 'L2_xattn_Wq': _L2_xattn_in['Wq'], 'L2_xattn_bq': _L2_xattn_in['bq'], 'L2_xattn_Wk': _L2_xattn_in['Wk'], 'L2_xattn_bk': _L2_xattn_in['bk'], 'L2_xattn_Wv': _L2_xattn_in['Wv'], 'L2_xattn_bv': _L2_xattn_in['bv'], 'L2_xattn_Wout': _L2_xattn_in['Wout'], 'L2_xattn_bout': _L2_xattn_in['bout'], 'L2_ffn_Wr': _L2_ffn_in['Wr'], 'L2_ffn_br': _L2_ffn_in['br'], 'L2_ffn_W1': _L2_ffn_in['W1'], 'L2_ffn_b1': _L2_ffn_in['b1'], 'L2_ffn_W2': _L2_ffn_in['W2'], 'L2_ffn_b2': _L2_ffn_in['b2'], 'L3_xattn_Wq': _L3_xattn_in['Wq'], 'L3_xattn_Wk': _L3_xattn_in['Wk'], 'L3_xattn_Wv': _L3_xattn_in['Wv'], 'L3_xattn_Wu': _L3_xattn_in['Wu'], 'L3_xattn_bu': _L3_xattn_in['bu'], 'L3_xattn_qn_w': _L3_xattn_in['qn_w'], 'L3_xattn_qn_b': _L3_xattn_in['qn_b'], 'L3_xattn_kn_w': _L3_xattn_in['kn_w'], 'L3_xattn_kn_b': _L3_xattn_in['kn_b'], 'L3_ffn_w_gate': _L3_ffn_in['w_gate'], 'L3_ffn_w_up': _L3_ffn_in['w_up'], 'L3_ffn_w_down': _L3_ffn_in['w_down']}

def reference(x, ctx_1024, mask_BxS2_bf1, mask_SxS2_ff0, mask_BxS2_bf0, L0_xattn_Wq, L0_xattn_bq, L0_xattn_Wk, L0_xattn_bk, L0_xattn_Wv, L0_xattn_bv, L0_xattn_scale, L0_ffn_ln1_scale, L0_ffn_ln1_shift, L0_ffn_wq, L0_ffn_wk, L0_ffn_wv, L0_ffn_wo, L0_ffn_bo, L0_ffn_ln2_scale, L0_ffn_ln2_shift, L0_ffn_gate_w, L0_ffn_w1, L0_ffn_w2, L0_ffn_w3, L1_xattn_Wq, L1_xattn_bq, L1_xattn_Wkv, L1_xattn_bkv, L1_xattn_Wp, L1_xattn_bp, L1_ffn_w_gate, L1_ffn_b_gate, L1_ffn_W1, L1_ffn_b1, L1_ffn_W2, L1_ffn_b2, L2_xattn_Wq, L2_xattn_bq, L2_xattn_Wk, L2_xattn_bk, L2_xattn_Wv, L2_xattn_bv, L2_xattn_Wout, L2_xattn_bout, L2_ffn_Wr, L2_ffn_br, L2_ffn_W1, L2_ffn_b1, L2_ffn_W2, L2_ffn_b2, L3_xattn_Wq, L3_xattn_Wk, L3_xattn_Wv, L3_xattn_Wu, L3_xattn_bu, L3_xattn_qn_w, L3_xattn_qn_b, L3_xattn_kn_w, L3_xattn_kn_b, L3_ffn_w_gate, L3_ffn_w_up, L3_ffn_w_down):
    import jax
    import jax.numpy as jnp

    def _L0_xattn_ref(input_q, input_k, input_v, Wq, bq, Wk, bk, Wv, bv, scale):
        import jax, jax.numpy as jnp
        import numpy as np
        D_MODEL = 128
        NUM_HEADS = 16
        FOCUS = 3
        EPS = 1e-06

        def _focused_feature_map(x, scale):
            x = jax.nn.relu(x) + EPS
            x = x / scale
            x_norm = jnp.linalg.norm(x, axis=-1, keepdims=True)
            xp = x ** FOCUS
            return xp / jnp.linalg.norm(xp, axis=-1, keepdims=True) * x_norm
        b, n_q, d = input_q.shape
        h = NUM_HEADS
        c = d // h
        q = input_q @ Wq + bq
        k = input_k @ Wk + bk
        v = input_v @ Wv + bv
        sp = jax.nn.softplus(scale)
        q = _focused_feature_map(q, sp)
        k = _focused_feature_map(k, sp)
        q = q.reshape(b, n_q, h, c).transpose(0, 2, 1, 3)
        k = k.reshape(b, -1, h, c).transpose(0, 2, 1, 3)
        v = v.reshape(b, -1, h, c).transpose(0, 2, 1, 3)
        z = 1.0 / (jnp.einsum('bhic,bhc->bhi', q, k.sum(axis=2)) + EPS)
        kv = jnp.einsum('bhjc,bhjd->bhcd', k, v)
        x = jnp.einsum('bhic,bhcd->bhid', q, kv) * z[..., None]
        return x.transpose(0, 2, 1, 3).reshape(b, n_q, d)

    def _L0_ffn_ref(x, ln1_scale, ln1_shift, wq, wk, wv, wo, bo, ln2_scale, ln2_shift, gate_w, w1, w2, w3):
        import jax, jax.numpy as jnp
        import numpy as np
        EMB = 128
        HID = 256
        HEADS = 16
        HEAD_DIM = EMB // HEADS
        EXPERTS = 8
        TOPK = 2
        EPS = 1e-05

        def layernorm(x, scale, shift):
            mean = jnp.mean(x, axis=-1, keepdims=True)
            var = jnp.mean((x - mean) ** 2, axis=-1, keepdims=True)
            return scale * (x - mean) / jnp.sqrt(var + EPS) + shift

        def attention(x, wq, wk, wv, wo, bo):
            b, t, _ = x.shape
            q = (x @ wq).reshape(b, t, HEADS, HEAD_DIM)
            k = (x @ wk).reshape(b, t, HEADS, HEAD_DIM)
            v = (x @ wv).reshape(b, t, HEADS, HEAD_DIM)
            scores = jnp.einsum('bqhd,bkhd->bhqk', q, k)
            mask = jnp.arange(t)[:, None] < jnp.arange(t)[None, :]
            scores = jnp.where(mask, -jnp.inf, scores)
            attn = jax.nn.softmax(scores / np.sqrt(HEAD_DIM), axis=-1)
            ctx = jnp.einsum('bhqk,bkhd->bqhd', attn, v).reshape(b, t, EMB)
            return ctx @ wo + bo

        def moe_ff(x, gate_w, w1, w2, w3):
            b, t, d = x.shape
            xf = x.reshape(b * t, d)
            scores = xf @ gate_w
            topk_scores, topk_idx = jax.lax.top_k(scores, TOPK)
            topk_probs = jax.nn.softmax(topk_scores, axis=-1)
            weight = jnp.sum(jax.nn.one_hot(topk_idx, EXPERTS, dtype=xf.dtype) * topk_probs[..., None], axis=1)
            h = jax.nn.silu(jnp.einsum('td,edh->eth', xf, w1)) * jnp.einsum('td,edh->eth', xf, w2)
            out_e = jnp.einsum('eth,ehd->etd', h, w3)
            out = jnp.einsum('etd,te->td', out_e, weight)
            return out.reshape(b, t, d)
        h = layernorm(x, ln1_scale, ln1_shift)
        x = x + attention(h, wq, wk, wv, wo, bo)
        h = layernorm(x, ln2_scale, ln2_shift)
        x = x + moe_ff(h, gate_w, w1, w2, w3)
        return x

    def _L1_xattn_ref(x, context, context_mask, Wq, bq, Wkv, bkv, Wp, bp):
        import jax, jax.numpy as jnp
        import numpy as np
        D_MODEL = 128
        N_HEADS = 16
        HEAD_DIM = D_MODEL // N_HEADS
        B, T, D = x.shape
        S = context.shape[1]
        H, Hd = (N_HEADS, HEAD_DIM)
        q = (x @ Wq + bq).reshape(B, T, H, Hd).transpose(0, 2, 1, 3)
        kv = (context @ Wkv + bkv).reshape(B, S, 2, H, Hd)
        k = kv[:, :, 0].transpose(0, 2, 1, 3)
        v = kv[:, :, 1].transpose(0, 2, 1, 3)
        scores = jnp.einsum('bhtd,bhsd->bhts', q, k) / np.sqrt(Hd)
        neg_inf = jnp.finfo(scores.dtype).min
        scores = jnp.where(context_mask[:, None, None, :], scores, neg_inf)
        attn = jax.nn.softmax(scores, axis=-1)
        out = jnp.einsum('bhts,bhsd->bthd', attn, v).reshape(B, T, D)
        return out @ Wp + bp

    def _L1_ffn_ref(x, w_gate, b_gate, W1, b1, W2, b2):
        import jax, jax.numpy as jnp
        import numpy as np
        D_MODEL = 128
        MLP_DIM = 512
        N_EXPERTS = 8
        B, T = (4, 128)
        b, t, d = x.shape
        x_flat = x.reshape(b * t, d)
        logits = x_flat @ w_gate + b_gate
        probs = jax.nn.softmax(logits, axis=-1)
        route_p = jnp.max(probs, axis=-1)
        route_idx = jnp.argmax(probs, axis=-1)
        h = jnp.einsum('nd,edm->enm', x_flat, W1) + b1[:, None, :]
        h = jax.nn.relu(h)
        y = jnp.einsum('enm,emd->end', h, W2) + b2[:, None, :]
        n = b * t
        out = y[route_idx, jnp.arange(n)] * route_p[:, None]
        return out.reshape(b, t, d)

    def _L2_xattn_ref(query, key, value, attn_mask, key_padding_mask, Wq, bq, Wk, bk, Wv, bv, Wout, bout):
        import jax, jax.numpy as jnp
        import numpy as np
        EMBED_DIM = 128
        NUM_HEADS = 16
        HEAD_DIM = EMBED_DIM // NUM_HEADS
        SCALE = HEAD_DIM ** (-0.5)
        B, T, C = query.shape
        S = key.shape[1]
        H, D = (NUM_HEADS, HEAD_DIM)
        q = (query @ Wq.T + bq).reshape(B, T, H, D).transpose(0, 2, 1, 3)
        k = (key @ Wk.T + bk).reshape(B, S, H, D).transpose(0, 2, 1, 3)
        v = (value @ Wv.T + bv).reshape(B, S, H, D).transpose(0, 2, 1, 3)
        scores = jnp.einsum('bhtd,bhsd->bhts', q, k) * SCALE
        scores = scores + attn_mask[None, None, :, :]
        scores = jnp.where(key_padding_mask[:, None, None, :], -jnp.inf, scores)
        weights = jax.nn.softmax(scores, axis=-1)
        attn_out = jnp.einsum('bhts,bhsd->bhtd', weights, v)
        attn_out = attn_out.transpose(0, 2, 1, 3).reshape(B, T, C)
        return attn_out @ Wout.T + bout

    def _L2_ffn_ref(x, Wr, br, W1, b1, W2, b2):
        import jax, jax.numpy as jnp
        import numpy as np
        H, E, DFF = (128, 8, 512)
        B, S, Hd = x.shape
        n_exp = W1.shape[0]
        xt = x.reshape(-1, Hd)
        logits = xt @ Wr + br
        probs = jax.nn.softmax(logits, axis=-1)
        gate = jnp.max(probs, axis=-1)
        idx = jnp.argmax(probs, axis=-1)
        h1 = jnp.maximum(jnp.einsum('th,ehf->etf', xt, W1) + b1[:, None, :], 0.0)
        ye = jnp.einsum('etf,efh->eth', h1, W2) + b2[:, None, :]
        onehot = jax.nn.one_hot(idx, n_exp, dtype=xt.dtype)
        y = jnp.einsum('te,eth->th', onehot, ye) * gate[:, None]
        return y.reshape(B, S, Hd)

    def _L3_xattn_ref(emb, context, Wq, Wk, Wv, Wu, bu, qn_w, qn_b, kn_w, kn_b):
        import jax, jax.numpy as jnp
        import numpy as np
        N_HEADS = 16
        KQ_DIM = 64
        EMB_DIM = 128
        CTX_DIM = 128
        EPS = 1e-05

        def _layernorm(x, w, b):
            mu = jnp.mean(x, axis=-1, keepdims=True)
            var = jnp.mean(jnp.square(x - mu), axis=-1, keepdims=True)
            return (x - mu) * jax.lax.rsqrt(var + EPS) * w + b
        B, SQ, _ = emb.shape
        SK = context.shape[1]
        q = (emb @ Wq.T).reshape(B, SQ, N_HEADS, KQ_DIM).transpose(0, 2, 1, 3)
        k = (context @ Wk.T).reshape(B, SK, N_HEADS, KQ_DIM).transpose(0, 2, 1, 3)
        v = (context @ Wv.T).reshape(B, SK, N_HEADS, KQ_DIM).transpose(0, 2, 1, 3)
        q = _layernorm(q, qn_w, qn_b)
        k = _layernorm(k, kn_w, kn_b)
        scale = 1.0 / jnp.sqrt(jnp.asarray(KQ_DIM, emb.dtype))
        attn = jnp.einsum('bhqd,bhkd->bhqk', q, k) * scale
        attn = jax.nn.softmax(attn, axis=-1)
        out = jnp.einsum('bhqk,bhkd->bhqd', attn, v)
        out = out.transpose(0, 2, 1, 3).reshape(B, SQ, N_HEADS * KQ_DIM)
        return out @ Wu.T + bu

    def _L3_ffn_ref(x, w_gate, w_up, w_down):
        import jax, jax.numpy as jnp
        import numpy as np
        DIM = 128
        HIDDEN = 384
        SCALE = 1.0 / 127.0

        def _dequant(w_int, dtype):
            return w_int.astype(dtype) * jnp.asarray(SCALE, dtype)
        wg = _dequant(w_gate, x.dtype)
        wu = _dequant(w_up, x.dtype)
        wd = _dequant(w_down, x.dtype)
        gate = jnp.einsum('bsd,hd->bsh', x, wg)
        up = jnp.einsum('bsd,hd->bsh', x, wu)
        h = jax.nn.silu(gate) * up
        return jnp.einsum('bsh,dh->bsd', h, wd)
    x = x + _L0_xattn_ref(_layernorm(x, axis=-1), ctx_1024, ctx_1024, L0_xattn_Wq, L0_xattn_bq, L0_xattn_Wk, L0_xattn_bk, L0_xattn_Wv, L0_xattn_bv, L0_xattn_scale)
    x = x + _L0_ffn_ref(_layernorm(x, axis=-1), L0_ffn_ln1_scale, L0_ffn_ln1_shift, L0_ffn_wq, L0_ffn_wk, L0_ffn_wv, L0_ffn_wo, L0_ffn_bo, L0_ffn_ln2_scale, L0_ffn_ln2_shift, L0_ffn_gate_w, L0_ffn_w1, L0_ffn_w2, L0_ffn_w3)
    x = x + _L1_xattn_ref(_layernorm(x, axis=-1), ctx_1024, mask_BxS2_bf1, L1_xattn_Wq, L1_xattn_bq, L1_xattn_Wkv, L1_xattn_bkv, L1_xattn_Wp, L1_xattn_bp)
    x = x + _L1_ffn_ref(_layernorm(x, axis=-1), L1_ffn_w_gate, L1_ffn_b_gate, L1_ffn_W1, L1_ffn_b1, L1_ffn_W2, L1_ffn_b2)
    x = x + _L2_xattn_ref(_layernorm(x, axis=-1), ctx_1024, ctx_1024, mask_SxS2_ff0, mask_BxS2_bf0, L2_xattn_Wq, L2_xattn_bq, L2_xattn_Wk, L2_xattn_bk, L2_xattn_Wv, L2_xattn_bv, L2_xattn_Wout, L2_xattn_bout)
    x = x + _L2_ffn_ref(_layernorm(x, axis=-1), L2_ffn_Wr, L2_ffn_br, L2_ffn_W1, L2_ffn_b1, L2_ffn_W2, L2_ffn_b2)
    x = x + _L3_xattn_ref(_layernorm(x, axis=-1), ctx_1024, L3_xattn_Wq, L3_xattn_Wk, L3_xattn_Wv, L3_xattn_Wu, L3_xattn_bu, L3_xattn_qn_w, L3_xattn_qn_b, L3_xattn_kn_w, L3_xattn_kn_b)
    x = x + _L3_ffn_ref(_layernorm(x, axis=-1), L3_ffn_w_gate, L3_ffn_w_up, L3_ffn_w_down)
    return x

_drawn_inputs = setup_inputs


def setup_inputs(seed=0):
    import zlib

    import numpy as np

    out = dict(_drawn_inputs(seed))
    spreads = {'mask_SxS2_ff0': (0.0, 0.607),
     'L0_xattn_bq': (0.0, 0.1),
     'L0_xattn_bk': (0.0, 0.1),
     'L0_xattn_bv': (0.0, 0.1),
     'L0_xattn_scale': (0.0, 0.1),
     'L0_ffn_ln1_scale': (1.0, 0.2),
     'L0_ffn_ln1_shift': (0.0, 0.1),
     'L0_ffn_bo': (0.0, 0.1),
     'L0_ffn_ln2_scale': (1.0, 0.2),
     'L0_ffn_ln2_shift': (0.0, 0.1),
     'L1_xattn_bq': (0.0, 0.357),
     'L1_xattn_bkv': (0.0, 0.1),
     'L1_xattn_bp': (0.0, 0.1),
     'L1_ffn_b1': (0.0, 0.777),
     'L1_ffn_b2': (0.0, 0.281),
     'L2_xattn_bq': (0.0, 0.402),
     'L2_xattn_bk': (0.0, 0.8),
     'L2_xattn_bv': (0.0, 0.1),
     'L2_xattn_bout': (0.0, 0.1),
     'L2_ffn_br': (0.0, 0.1),
     'L2_ffn_b1': (0.0, 0.474),
     'L2_ffn_b2': (0.0, 0.32),
     'L3_xattn_qn_w': (1.0, 0.6),
     'L3_xattn_qn_b': (0.0, 0.8),
     'L3_xattn_kn_w': (1.0, 0.6),
     'L3_xattn_kn_b': (0.0, 0.8)}
    factors = {'L1_ffn_b_gate': 4.672, 'L3_xattn_bu': 5.019}
    for name, (base, spread) in spreads.items():
        noise = np.random.default_rng([zlib.crc32(name.encode()), seed]).standard_normal(out[name].shape)
        drawn = base * np.exp(spread * noise) if base else spread * noise
        out[name] = jnp.asarray(drawn.astype(out[name].dtype))
    for name, factor in factors.items():
        out[name] = (out[name] * factor).astype(out[name].dtype)
    return out
```

```python
from contextlib import ExitStack

import concourse.bass as bass
from concourse import mybir

F32 = mybir.dt.float32
BF16 = mybir.dt.bfloat16
I32 = mybir.dt.int32
U8 = mybir.dt.uint8
ALU = mybir.AluOpType
ACT = mybir.ActivationFunctionType
AX = mybir.AxisListType

B, T, D = 16, 128, 128
H, HD = 16, 8
G = 4
NG = H // G
HD3 = 64
E = 8
GB = 4
NT = GB * T
LN_EXP = "natural_log_exp_and_others"
NEG = -1.5 * 2.0 ** 127
EPS = 1e-5

COLS = ["ln1_s", "ln1_b", "ln2_s", "ln2_b", "bq1", "bk1", "bq2", "bk2", "qn_w", "qn_b", "kn_w", "kn_b"]
ROWS = [("bq0", D), ("bk0", D), ("bv0", D), ("scale0", D), ("bo", D), ("bv1", D), ("bp1", D), ("bv2", D),
        ("bout2", D), ("bu3", D), ("bg1", E), ("br2", E)]
ROW_AT = {}
_at = 0
for _n, _w in ROWS:
    ROW_AT[_n] = (_at, _w)
    _at += _w
NROW = _at
NCOL = len(COLS)


NGR = B // GB
FFN_COUNTS = {n: [NGR] * 4 for n in ("var_ready", "rstd_step", "rstd_ready", "stat_step", "xn_ready", "xT_ready", "xT_done")}
FFN_COUNTS.update({n: [NGR] * 3 + [0] for n in ("l_ready", "d_ready", "e_ready", "w_ready")})
FFN_COUNTS.update({n: [0, NGR, NGR, 0] for n in ("wT_ready", "wT_done")})
FFN_COUNTS.update({n: [NGR * 16, 0, 0, NGR * 3] for n in ("a_ready", "b_ready", "silu_done")})
FFN_COUNTS.update({"h_ready": [0, NGR * 32, NGR * 32, 0], "h_done": [NGR * 16, NGR * 32, NGR * 32, NGR * 3],
                   "gate_step": [NGR * 17, NGR * 8, NGR * 8, 0]})
FFN_COUNTS.update({n: [NGR * 8, NGR * 9, NGR * 9, NGR] for n in ("y_ready", "acc_done")})


class Names:
    pass


class From:

    def __init__(self, sem, base):
        self.sem, self.base = sem, base


def wait(eng, sem, value):
    if isinstance(sem, From):
        sem, value = sem.sem, value + sem.base
    if not (isinstance(value, int) and value <= 0):
        eng.wait_ge(sem, value)


class Chain:

    def __init__(self, eng, sem, k, per):
        self.eng, self.sem, self.base, self.per, self.n = eng, sem, k * per, per, 0
        if isinstance(sem, From):
            self.sem, self.base = sem.sem, k * per + sem.base

    def link(self, ins):
        self.n += 1
        ins.then_inc(self.sem, 1)
        self.eng.wait_ge(self.sem, self.base + self.n)

    def done(self):
        assert self.n == self.per, (self.n, self.per)


class Step:

    def __init__(self, i, c):
        self.i, self.c = i, c
        self.n, self.par, self.half = i * 2 + c, c % 2, i + c // 2

    def __add__(self, d):
        return Step(self.i, self.c + d)

    def static(self):
        return isinstance(self.i, int)

    def exists(self, count=B):
        return not self.static() or 0 <= self.c < count

    def within(self, count=B):
        return min(max(self.c, 0), count) if self.static() else self.n


def pipeline(eng, body, before, after):
    first = 2
    pairs = (B - before - first) // 2
    for c in range(-before, first):
        body(Step(0, c))
    with eng.Fori(0, pairs) as i:
        body(Step(i, first))
        body(Step(i, first + 1))
    for c in range(first + 2 * pairs, B + after):
        body(Step(0, c))


def batch(t, n):
    return t[:, n, :] if isinstance(n, int) else t[:, bass.ds(n, 1), :].rearrange("p a d -> p (a d)")



def attn_pe(nc, pe, K, lay):
    Wq, Wk, Wv, Wo = K.attn_w[lay]
    k0 = B * lay

    def transpose_x(s):
        k = s.n + k0
        wait(pe, K.xn_ready, k + 1)
        wait(pe, K.xT_done, k)
        wait(pe, K.oT_done, k0 + (s + -2).within())
        nc.tensor.transpose(K.pT[:, 0:T], K.xn[:, :], K.ident[:, :]).then_inc(K.xT_ready, 1)

    def project(s):
        k = s.n + k0
        if lay == 0:
            src = K.xT[:, s.par, :]
        else:
            src = K.ctx[:, s.par, :]
            pe.wait_ge(K.ctx_loaded[s.par], 16 * (s.half + 1 + (B // 2) * lay))
        wait(pe, K.xT_done, k + 1)
        wait(pe, K.qk_done, k)
        wait(pe, K.v_done, k)
        nc.tensor.matmul(K.pP[:, 0:T], Wq, K.xT[:, s.par, :], start=True, stop=True)
        nc.tensor.matmul(K.pP[:, T:2 * T], Wk, src, start=True, stop=True)
        nc.tensor.matmul(K.pP[:, 2 * T:3 * T], src, Wv, start=True, stop=True).then_inc(K.qkv_ready, 1)

    def row_scores(s, g):
        k = s.n + k0
        if g == 0:
            wait(pe, K.kblk_ready, k + 1)
        wait(pe, K.smax_done, 4 * k + g - 1)
        bank, r = K.pS[g % 2], slice(32 * g, 32 * g + 32)
        mm = nc.tensor.matmul(bank[:, :], K.qT[r, s.par, :], K.kblk[r, s.par, :, :].rearrange("p a k -> p (a k)"),
                              start=True, stop=False)
        if lay == 0:
            mm = nc.tensor.matmul(bank[:, :], K.identb[:, :], K.causal[:, :].unsqueeze(1).to_broadcast([T, G, T]),
                                  start=False, stop=True)
        else:
            if lay == 2:
                for part in range(3):
                    nc.tensor.matmul(bank[:, :], K.identb[:, :],
                                     K.amask[:, part, :].unsqueeze(1).to_broadcast([T, G, T]), start=False, stop=False)
            row = batch(K.prow[lay], s.n)
            mm = nc.tensor.matmul(bank[:, :], K.row0[:, :], row.unsqueeze(1).to_broadcast([T, G, T]),
                                  start=False, stop=True)
        mm.then_inc(K.s_ready, 1)

    def transpose_max(s):
        k = s.n + k0
        wait(pe, K.m3_ready, k + 1)
        wait(pe, K.mT_done, k)
        wait(pe, K.y_done, k0 + (s + -1).within())
        nc.tensor.transpose(K.pMb[:, 0:T], K.m3[:, :], K.identb[:, :]).then_inc(K.mT_ready, 1)

    def col_scores(s, g):
        k = s.n + k0
        if g == 0:
            wait(pe, K.mT_done, k + 1)
            wait(pe, K.qblk_ready, k + 1)
        wait(pe, K.exp_done, 4 * k + g - 1)
        bank, r = K.pC[g % 2], slice(32 * g, 32 * g + 32)
        nc.tensor.matmul(bank[:, :], K.kT[r, s.par, :], K.qblk[r, s.par, :, :].rearrange("p a k -> p (a k)"),
                         start=True, stop=False)
        if lay == 0:
            nc.tensor.matmul(bank[:, :], K.identb[:, :], K.causalT[:, :].unsqueeze(1).to_broadcast([T, G, T]),
                             start=False, stop=False)
        if lay == 2:
            for part in range(3):
                nc.tensor.matmul(bank[:, :], K.identb[:, :],
                                 K.amaskT[:, part, :].unsqueeze(1).to_broadcast([T, G, T]), start=False, stop=False)
        for a in range(G):
            mm = nc.tensor.matmul(bank[:, a * T:(a + 1) * T], K.sel[:, G * g + a, :], K.mT[:, :],
                                  start=False, stop=(a == G - 1))
        mm.then_inc(K.c_ready, 1)

    def probs_v(s, g):
        k = s.n + k0
        if g == 0:
            wait(pe, K.v_done, k + 1)
            wait(pe, K.on_ready, k)
        wait(pe, K.exp_done, 4 * k + g + 1)
        for a in range(G):
            h = G * g + a
            mm = nc.tensor.matmul(K.pO[:, h * (HD + 1):(h + 1) * (HD + 1)], K.pt[:, g % 2, a * T:(a + 1) * T],
                                  K.vaug[:, s.par, h, :], start=True, stop=True)
        mm.then_inc(K.pv_done, 1)

    def transpose_o(s):
        k = s.n + k0
        wait(pe, K.on_ready, k + 1)
        wait(pe, K.xT_done, k0 + (s + 3).within())
        wait(pe, K.oT_done, k)
        nc.tensor.transpose(K.pT[:, 0:T], K.on[:, :], K.ident[:, :]).then_inc(K.oT_ready, 1)

    def out_project(s):
        k = s.n + k0
        wait(pe, K.oT_done, k + 1)
        wait(pe, K.mT_done, k0 + (s + 2).within())
        wait(pe, K.y_done, k)
        nc.tensor.matmul(K.pM[:, 0:D], K.oT[:, :], Wo, start=True, stop=True).then_inc(K.y_ready, 1)

    pe.wait_ge(K.attn_w_loaded[lay], 64)

    def body(s):
        a, nx, pr = s + 1, s + 2, s + -1
        for g in range(NG):
            if s.exists():
                col_scores(s, g)
            if a.exists():
                row_scores(a, g)
            if g == 0:
                if pr.exists():
                    transpose_o(pr)
                if nx.exists():
                    transpose_x(nx)
            if g == 1 and pr.exists():
                out_project(pr)
            if g >= 1 and s.exists():
                probs_v(s, g - 1)
        if nx.exists():
            project(nx)
        if s.exists():
            probs_v(s, NG - 1)
        if a.exists():
            transpose_max(a)

    pipeline(pe, body, 3, 1)


def attn_act(nc, act, K, lay):
    k0 = B * lay

    def rstd(s):
        k = s.n + k0
        wait(act, K.var_ready, k + 1)
        c = Chain(act, K.rstd_step, k, 1)
        c.link(nc.scalar.activation(K.lnv[:, 0:1], K.mv[:, s.par, 1:2], ACT.Ln, bias=K.eps[:, :]))
        c.done()
        nc.scalar.activation(K.rs[:, s.par, 0:1], K.lnv[:, 0:1], ACT.Exp, scale=-0.5).then_inc(K.rstd_ready, 1)
        if lay == 0:
            wait(act, K.var2_ready, s.n + 1)
            c = Chain(act, K.rstd2_step, s.n, 1)
            c.link(nc.scalar.activation(K.lnv[:, 1:2], K.var2[:, :], ACT.Ln, bias=K.eps[:, :]))
            nc.scalar.activation(K.rs[:, s.par, 1:2], K.lnv[:, 1:2], ACT.Exp, scale=-0.5).then_inc(K.rstd2_ready, 1)

    def keep_xT(s):
        wait(act, K.xT_ready, s.n + k0 + 1)
        if lay == 0:
            op = nc.scalar.activation(K.xT[:, s.par, :], K.pT[:, 0:T], ACT.Identity, scale=K.col("ln1_s"),
                                      bias=K.col("ln1_b"))
        else:
            op = nc.scalar.copy(K.xT[:, s.par, :], K.pT[:, 0:T])
        op.then_inc(K.xT_done, 1)

    def keep_qk(s):
        wait(act, K.qkv_ready, s.n + k0 + 1)
        if lay == 0:
            nc.scalar.mul(K.qT[:, s.par, :], K.pP[:, 0:T], HD ** -0.5).then_inc(K.q_done, 1)
            nc.scalar.copy(K.kT[:, s.par, :], K.pP[:, T:2 * T]).then_inc(K.qk_done, 1)
        else:
            nc.scalar.activation(K.qT[:, s.par, :], K.pP[:, 0:T], ACT.Identity, scale=HD ** -0.5,
                                 bias=K.bqs[:, lay - 1:lay]).then_inc(K.q_done, 1)
            nc.scalar.activation(K.kT[:, s.par, :], K.pP[:, T:2 * T], ACT.Identity,
                                 bias=K.col(f"bk{lay}")).then_inc(K.qk_done, 1)

    def keep_mT(s):
        wait(act, K.mT_ready, s.n + k0 + 1)
        nc.scalar.copy(K.mT[:, :], K.pMb[:, 0:T]).then_inc(K.mT_done, 1)

    def exp(s, g):
        k = s.n + k0
        wait(act, K.c_ready, 4 * k + g + 1)
        wait(act, K.pv_done, 4 * k + g - 1)
        if lay and g == 0:
            wait(act, K.pc_ready, k - B + 1)
        bias = 0.0 if lay == 0 else K.pc[:, s.par, :]
        nc.scalar.activation(K.pt[:, g % 2, :], K.pC[g % 2][:, :], ACT.Exp, bias=bias).then_inc(K.exp_done, 1)

    def keep_oT(s):
        wait(act, K.oT_ready, s.n + k0 + 1)
        nc.scalar.copy(K.oT[:, :], K.pT[:, 0:T]).then_inc(K.oT_done, 1)

    if lay:
        act.wait_ge(K.consts_ready, K.n_consts)
    def body(s):
        a, nx, pr, st = s + 1, s + 2, s + -1, s + 3
        for g in range(NG):
            if s.exists():
                exp(s, g)
            if g == 0:
                if pr.exists():
                    keep_oT(pr)
                if nx.exists():
                    keep_xT(nx)
        if nx.exists():
            keep_qk(nx)
        if a.exists():
            keep_mT(a)
        if st.exists():
            rstd(st)

    pipeline(act, body, 3, 1)


def attn_dve(nc, dve, K, lay):
    k0 = B * lay

    def stats(s):
        k = s.n + k0
        c = Chain(dve, K.stat_step, k, 1)
        c.link(nc.vector.bn_stats(K.bn[:, :], batch(K.x, s.n)))
        nc.vector.memset(K.spare[:, :], 0.0)
        nc.vector.bn_aggr(K.mv[:, s.par, :], K.bn[:, :]).then_inc(K.var_ready, 1)
        if lay == 0:
            wait(dve, K.rstd_ready, k + 1)
            c = Chain(dve, K.var2_step, s.n, 1)
            c.link(nc.vector.tensor_tensor(K.var2a[:, :], K.mv[:, s.par, 1:2], K.rs[:, s.par, 0:1], ALU.mult))
            nc.vector.tensor_tensor(K.var2[:, :], K.var2a[:, :], K.rs[:, s.par, 0:1], ALU.mult).then_inc(K.var2_ready, 1)

    def normalise(s):
        k = s.n + k0
        wait(dve, K.rstd_ready, k + 1)
        wait(dve, K.xT_ready, k)
        if lay == 0:
            nc.vector.tensor_scalar(batch(K.x1, s.n), batch(K.x, s.n), K.mv[:, s.par, 0:1], K.rs[:, s.par, 0:1],
                                    ALU.subtract, ALU.mult).then_inc(K.x1_step, 1)
            wait(dve, K.rstd2_ready, s.n + 1)
            dve.wait_ge(K.x1_step, s.n + 1)
            nc.vector.tensor_scalar(K.xn[:, :], batch(K.x1, s.n), K.rs[:, s.par, 1:2], None,
                                    ALU.mult).then_inc(K.xn_ready, 1)
        else:
            nc.vector.tensor_scalar(K.xn[:, :], batch(K.x, s.n), K.mv[:, s.par, 0:1], K.rs[:, s.par, 0:1],
                                    ALU.subtract, ALU.mult).then_inc(K.xn_ready, 1)

    def keep_v(s):
        wait(dve, K.qk_done, s.n + k0 + 1)
        src = K.pP[:, 2 * T:3 * T].rearrange("p (h d) -> p h d", h=H)
        dst = K.vaug[:, s.par, :, 0:HD]
        if lay == 0:
            op = nc.vector.tensor_copy(dst, src)
        else:
            op = nc.vector.tensor_tensor(dst, src, K.row(f"bv{lay}").rearrange("p (h d) -> p h d", h=H), ALU.add)
        op.then_inc(K.v_done, 1)

    def row_max(s, g):
        wait(dve, K.s_ready, 4 * (s.n + k0) + g + 1)
        nc.vector.reduce_max(K.m[:, G * g:G * g + G], K.pS[g % 2][:, :].rearrange("p (a k) -> p a k", a=G),
                             AX.X).then_inc(K.smax_done, 1)

    def split_max(s):
        k = s.n + k0
        dve.wait_ge(K.smax_done, 4 * k + 4)
        c = Chain(dve, K.split_step, k, 3)
        c.link(nc.vector.tensor_scalar(K.m3[:, 0:H], K.m[:, :], -1.0, None, ALU.mult))
        c.link(nc.vector.scalar_tensor_tensor(K.mr[:, :], K.m[:, :], -1.0, K.m3[:, 0:H], ALU.mult, ALU.subtract))
        c.link(nc.vector.tensor_copy(K.m3[:, H:2 * H], K.mr[:, :]))
        c.done()
        nc.vector.tensor_tensor(K.m3[:, 2 * H:3 * H], K.mr[:, :], K.m3[:, H:2 * H],
                                ALU.subtract).then_inc(K.m3_ready, 1)

    def normalise_o(s):
        k = s.n + k0
        dve.wait_ge(K.pv_done, 4 * k + 4)
        po = K.pO[:, 0:H * (HD + 1)].rearrange("p (h d) -> p h d", h=H)
        c = Chain(dve, K.rec_step, k, 1)
        c.link(nc.vector.reciprocal(K.rec[:, :], po[:, :, HD]))
        nc.vector.tensor_tensor(K.on[:, :].rearrange("p (h d) -> p h d", h=H), po[:, :, 0:HD],
                                K.rec[:, :].unsqueeze(2).to_broadcast([T, H, HD]),
                                ALU.mult).then_inc(K.on_ready, 1)

    def residual(s):
        k = s.n + k0
        wait(dve, K.y_ready, k + 1)
        bias = K.row({0: "bo", 1: "bp1", 2: "bout2"}[lay])
        nc.vector.tensor_tensor(K.yb[:, :], K.pM[:, 0:D], bias, ALU.add).then_inc(K.y_done, 1)
        dve.wait_ge(K.y_done, k + 1)
        if lay == 0:
            c = Chain(dve, K.res_step, s.n, 1)
            c.link(nc.vector.tensor_tensor(batch(K.x1, s.n), batch(K.x1, s.n), K.yb[:, :], ALU.add))
            nc.vector.tensor_tensor(batch(K.x, s.n), batch(K.x, s.n), batch(K.x1, s.n), ALU.add).then_inc(K.x_done, 1)
        else:
            nc.vector.tensor_tensor(batch(K.x, s.n), batch(K.x, s.n), K.yb[:, :], ALU.add).then_inc(K.x_done, 1)

    def body(s):
        a, nx, pr, st = s + 1, s + 2, s + -1, s + 3
        if nx.exists():
            normalise(nx)
        for g in range(NG):
            if a.exists():
                row_max(a, g)
            if g == 1 and pr.exists():
                residual(pr)
        if a.exists():
            split_max(a)
        if s.exists():
            normalise_o(s)
        if nx.exists():
            keep_v(nx)
        if st.exists():
            stats(st)

    dve.wait_ge(K.x_done, K.x_before_attn[lay])
    pipeline(dve, body, 3, 1)


def attn_pool(nc, pool, K, lay):
    k0 = B * lay

    def body(s):
        nx = s + 2
        if not nx.exists():
            return
        k = nx.n + k0
        hm = K.hmask[:, :].unsqueeze(2).to_broadcast([D, G, T])
        wait(pool, K.qk_done, k + 1)
        if lay:
            nc.gpsimd.tensor_copy(K.pc[:, nx.par, :], batch(K.pcol[lay], nx.n)).then_inc(K.pc_ready, 1)
        nc.gpsimd.tensor_tensor(K.kblk[:, nx.par, :, :], K.kT[:, nx.par, :].unsqueeze(1).to_broadcast([D, G, T]), hm,
                                ALU.mult).then_inc(K.kblk_ready, 1)
        wait(pool, K.q_done, k + 1)
        nc.gpsimd.tensor_tensor(K.qblk[:, nx.par, :, :], K.qT[:, nx.par, :].unsqueeze(1).to_broadcast([D, G, T]), hm,
                                ALU.mult).then_inc(K.qblk_ready, 1)

    pipeline(pool, body, 3, 1)



def lin_pe(nc, pe, K):
    def transpose_x(s):
        wait(pe, K.lin_xn_ready, s.n + 1)
        wait(pe, K.lin_xT_done, s.n)
        nc.tensor.transpose(K.pT[:, 0:T], K.xn[:, :], K.ident[:, :]).then_inc(K.lin_xT_ready, 1)

    def project(s):
        wait(pe, K.lin_xT_done, s.n + 1)
        pe.wait_ge(K.ctx_loaded[s.par], 16 * (s.half + 1))
        wait(pe, K.lin_p_done, s.n)
        c = K.ctx[:, s.par, :]
        nc.tensor.matmul(K.pP[:, 0:D], K.xT[:, s.par, :], K.lin_w[:, 0, :], start=True, stop=True)
        nc.tensor.matmul(K.pP[:, D:2 * D], c, K.lin_w[:, 1, :], start=True, stop=True)
        nc.tensor.matmul(K.pP[:, 2 * D:3 * D], c, K.lin_w[:, 2, :], start=True, stop=True).then_inc(K.lin_p_ready, 1)

    def kv(s):
        wait(pe, K.lin_f_ready, s.n + 1)
        wait(pe, K.lin_qT_done, s.n)
        nc.tensor.transpose(K.pC[0][:, 0:T], K.feat[:, s.par, 0, :], K.ident[:, :]).then_inc(K.lin_qT_ready, 1)
        wait(pe, K.lin_kv_done, s.n)
        nc.tensor.matmul(K.pM[:, 0:D + 1], K.feat[:, s.par, 1, :], K.linv[:, s.par, :], start=True,
                         stop=True).then_inc(K.lin_kv_ready, 1)

    def out(s):
        wait(pe, K.lin_qT_done, s.n + 1)
        wait(pe, K.lin_kv_done, s.n + 1)
        wait(pe, K.lin_o_done, s.n)
        nc.tensor.matmul(K.pO[:, 0:D + H], K.lqT[:, :], K.kvblk[:, :], start=True, stop=True).then_inc(K.lin_o_ready, 1)

    pe.wait_ge(K.lin_w_loaded, 48)
    pe.wait_ge(K.consts_loaded, 16)

    def body(s):
        nx = s + 2
        if s.exists():
            kv(s)
        if nx.exists():
            transpose_x(nx)
        if s.exists():
            out(s)
        if nx.exists():
            project(nx)

    pipeline(pe, body, 3, 0)


def lin_act(nc, act, K):
    def rstd(s):
        wait(act, K.lin_var_ready, s.n + 1)
        c = Chain(act, K.lin_rstd_step, s.n, 1)
        c.link(nc.scalar.activation(K.lnv[:, 0:1], K.mv[:, s.par, 1:2], ACT.Ln, bias=K.eps[:, :]))
        nc.scalar.activation(K.rs[:, s.par, 0:1], K.lnv[:, 0:1], ACT.Exp, scale=-0.5).then_inc(K.lin_rstd_ready, 1)

    def keep_xT(s):
        wait(act, K.lin_xT_ready, s.n + 1)
        nc.scalar.copy(K.xT[:, s.par, :], K.pT[:, 0:T]).then_inc(K.lin_xT_done, 1)

    def keep_qT(s):
        wait(act, K.lin_qT_ready, s.n + 1)
        nc.scalar.copy(K.lqT[:, :], K.pC[0][:, 0:T]).then_inc(K.lin_qT_done, 1)

    def ratio(s):
        wait(act, K.lin_ratio_ready, s.n + 1)
        c = Chain(act, K.lin_root_step, s.n, 1)
        c.link(nc.scalar.activation(K.lnr[:, :], K.fr[:, :], ACT.Ln))
        nc.scalar.activation(K.froot[:, :], K.lnr[:, :], ACT.Exp, scale=0.5).then_inc(K.lin_root_ready, 1)

    def body(s):
        a, nx, st = s + 1, s + 2, s + 3
        if s.exists():
            keep_qT(s)
        if nx.exists():
            keep_xT(nx)
        if a.exists():
            ratio(a)
        if st.exists():
            rstd(st)

    pipeline(act, body, 3, 0)


def lin_dve(nc, dve, K):
    def stats(s):
        c = Chain(dve, K.lin_stat_step, s.n, 1)
        c.link(nc.vector.bn_stats(K.bn[:, :], batch(K.x, s.n)))
        nc.vector.memset(K.spare[:, :], 0.0)
        nc.vector.bn_aggr(K.mv[:, s.par, :], K.bn[:, :]).then_inc(K.lin_var_ready, 1)

    def normalise(s):
        wait(dve, K.lin_rstd_ready, s.n + 1)
        wait(dve, K.lin_xT_ready, s.n)
        nc.vector.tensor_scalar(K.xn[:, :], batch(K.x, s.n), K.mv[:, s.par, 0:1], K.rs[:, s.par, 0:1],
                                ALU.subtract, ALU.mult).then_inc(K.lin_xn_ready, 1)

    def features(s):
        wait(dve, K.lin_p_ready, s.n + 1)
        qk = K.pP[:, 0:2 * D].rearrange("p (a d) -> p a d", a=2)
        c = Chain(dve, K.lin_f_step, s.n, 12)
        two = [T, 2, D]
        c.link(nc.vector.tensor_tensor(K.ft[:, :, :], qk, K.row2("bq0", "bk0").rearrange("p (a d) -> p a d", a=2), ALU.add))
        nc.vector.tensor_tensor(K.linv[:, s.par, 0:D], K.pP[:, 2 * D:3 * D], K.row("bv0"), ALU.add).then_inc(K.lin_p_done, 1)
        c.link(nc.vector.tensor_scalar(K.ft[:, :, :], K.ft[:, :, :], 0.0, 1e-6, ALU.max, ALU.add))
        c.link(nc.vector.tensor_tensor(K.ft[:, :, :], K.ft[:, :, :], K.isp[:, :].unsqueeze(1).to_broadcast(two), ALU.mult))
        c.link(nc.vector.reduce_max(K.fm[:, :], K.ft[:, :, :], AX.X))
        c.link(nc.vector.reciprocal(K.fr[:, :], K.fm[:, :]))
        c.link(nc.vector.tensor_tensor(K.ft[:, :, :], K.ft[:, :, :], K.fr[:, :].unsqueeze(2).to_broadcast(two), ALU.mult))
        c.link(nc.vector.tensor_tensor(K.f2[:, :, :], K.ft[:, :, :], K.ft[:, :, :], ALU.mult))
        c.link(nc.vector.tensor_tensor(K.f3[:, :, :], K.f2[:, :, :], K.ft[:, :, :], ALU.mult))
        nc.vector.reduce_sum(K.fs[:, 0:2], K.f2[:, :, :], AX.X)
        c.link(nc.vector.tensor_tensor(K.ft[:, :, :], K.f3[:, :, :], K.f3[:, :, :], ALU.mult))
        c.link(nc.vector.reduce_sum(K.fs[:, 2:4], K.ft[:, :, :], AX.X))
        c.link(nc.vector.reciprocal(K.fs[:, 2:4], K.fs[:, 2:4]))
        nc.vector.tensor_tensor(K.fr[:, :], K.fs[:, 0:2], K.fs[:, 2:4], ALU.mult).then_inc(K.lin_ratio_ready, 1)
        wait(dve, K.lin_root_ready, s.n + 1)
        c.link(nc.vector.tensor_tensor(K.fr[:, :], K.froot[:, :], K.fm[:, :], ALU.mult))
        nc.vector.tensor_tensor(K.feat[:, s.par, :, :], K.f3[:, :, :], K.fr[:, :].unsqueeze(2).to_broadcast(two),
                                ALU.mult).then_inc(K.lin_f_ready, 1)
        c.done()

    def within_heads(s):
        wait(dve, K.lin_kv_ready, s.n + 1)
        nc.vector.tensor_tensor(K.kvblk[:, 0:D], K.pM[:, 0:D], K.blockmask[:, :], ALU.mult)
        nc.vector.tensor_scalar(K.kvblk[:, D:D + H], K.headmask[:, :], K.pM[:, D:D + 1], None,
                                ALU.mult).then_inc(K.lin_kv_done, 1)

    def residual(s):
        wait(dve, K.lin_o_ready, s.n + 1)
        c = Chain(dve, K.lin_o_step, s.n, 2)
        c.link(nc.vector.tensor_scalar(K.rec[:, :], K.pO[:, D:D + H], 1e-6, None, ALU.add))
        c.link(nc.vector.reciprocal(K.rec[:, :], K.rec[:, :]))
        nc.vector.tensor_tensor(K.yb[:, :].rearrange("p (h d) -> p h d", h=H),
                                K.pO[:, 0:D].rearrange("p (h d) -> p h d", h=H),
                                K.rec[:, :].unsqueeze(2).to_broadcast([T, H, HD]), ALU.mult).then_inc(K.lin_o_done, 1)
        dve.wait_ge(K.lin_o_done, s.n + 1)
        nc.vector.tensor_tensor(batch(K.x, s.n), batch(K.x, s.n), K.yb[:, :], ALU.add).then_inc(K.x_done, 1)

    dve.wait_ge(K.x_loaded, 16)

    def body(s):
        a, nx, st = s + 1, s + 2, s + 3
        if s.exists():
            within_heads(s)
        if nx.exists():
            normalise(nx)
        if a.exists():
            features(a)
        if s.exists():
            residual(s)
        if st.exists():
            stats(st)

    pipeline(dve, body, 3, 0)



def groups(eng, body):
    body(0, True)
    with eng.Fori(1, B // GB - 1) as g:
        body(g, True)
    body(B // GB - 1, False)


def ffn_pe(nc, pe, K, kind):
    F = K.ffn[kind]
    NE, HB = F.experts, F.blocks

    def transpose_x(g):
        wait(pe, F.xn_ready, g + 1)
        wait(pe, F.xT_done, g)
        for b in range(GB):
            mm = nc.tensor.transpose(K.pT[:, b * T:(b + 1) * T], K.xg[:, b, :], K.ident[:, :])
        mm.then_inc(F.xT_ready.sem, 1)

    def logits(g):
        wait(pe, F.xT_done, g + 1)
        if NE == 1:
            return
        wait(pe, F.w_ready, g)
        if kind:
            wait(pe, F.wT_done, g)
        for b in range(GB):
            mm = nc.tensor.matmul(K.pP[:, b * E:(b + 1) * E], K.xTg[:, b * T:(b + 1) * T], F.gate, start=True, stop=True)
        mm.then_inc(F.l_ready.sem, 1)

    def hidden(g, e):
        for hb in range(HB):
            v = e * HB + hb
            if kind in (1, 2):
                wait(pe, F.h_done, g * (NE * HB) + max(v - 3, 0))
                nc.tensor.matmul(K.pH[v % 4][:, :], F.w1[:, e, hb * T:(hb + 1) * T], K.xTg[:, :], start=True,
                                 stop=True).then_inc(F.h_ready.sem, 1)
            else:
                for q, w, free in ((0, F.w1, F.silu_done), (1, F.w2, F.h_done)):
                    wait(pe, free, g * (NE * HB) + max(v - 1, 0))
                    mm = nc.tensor.matmul(K.pH[2 * (v % 2) + q][:, :], w[:, e, hb * T:(hb + 1) * T], K.xTg[:, :],
                                          start=True, stop=True)
                    mm.then_inc((F.a_ready, F.b_ready)[q].sem, 1)

    def weights_T(g):
        wait(pe, F.w_ready, g + 1)
        for b in range(GB):
            mm = nc.tensor.transpose(K.pP[0:E, b * T:(b + 1) * T], K.wts[:, b, :], K.ident[:, :])
        mm.then_inc(F.wT_ready.sem, 1)

    def down(g, e):
        wait(pe, F.h_done, g * (NE * HB) + (e + 1) * HB)
        wait(pe, F.acc_done, g * F.ys + max(e - 1, 0))
        bank = K.pY[e % 2]
        for b in range(GB):
            for hb in range(HB):
                mm = nc.tensor.matmul(bank[:, b * T:(b + 1) * T], K.hT[:, e % 2, hb, b * T:(b + 1) * T],
                                      F.w3[:, e, hb, :], start=(hb == 0), stop=(hb == HB - 1))
        mm.then_inc(F.y_ready.sem, 1)

    def down_bias(g):
        wait(pe, F.wT_done, g + 1)
        wait(pe, F.acc_done, g * F.ys + NE - 1)
        for b in range(GB):
            mm = nc.tensor.matmul(K.pY[0][:, b * T:(b + 1) * T], K.wT[:, b * T:(b + 1) * T], F.b2, start=True, stop=True)
        mm.then_inc(F.y_ready.sem, 1)

    for sem, count in F.loaded:
        pe.wait_ge(sem, count)
    transpose_x(0)
    logits(0)

    def body(g, more):
        hidden(g, 0)
        for e in range(NE):
            if e + 1 < NE:
                hidden(g, e + 1)
            if e == 0 and kind in (1, 2):
                weights_T(g)
            if e == NE - 1 and more:
                transpose_x(g + 1)
            down(g, e)
        if kind in (1, 2):
            down_bias(g)
        if more:
            logits(g + 1)

    groups(pe, body)


def ffn_act(nc, act, K, kind):
    F = K.ffn[kind]
    NE, HB = F.experts, F.blocks

    def rstd(g):
        wait(act, F.var_ready, g + 1)
        c = Chain(act, F.rstd_step, g, 1)
        c.link(nc.scalar.activation(K.lng[:, :], K.mvg[:, :, 1], ACT.Ln, bias=K.eps[:, :]))
        nc.scalar.activation(K.rsg[:, :], K.lng[:, :], ACT.Exp, scale=-0.5).then_inc(F.rstd_ready.sem, 1)

    def keep_xT(g):
        wait(act, F.xT_ready, g + 1)
        if kind == 0:
            op = nc.scalar.activation(K.xTg[:, :], K.pT[:, :], ACT.Identity, scale=K.col("ln2_s"), bias=K.col("ln2_b"))
        else:
            op = nc.scalar.copy(K.xTg[:, :], K.pT[:, :])
        op.then_inc(F.xT_done.sem, 1)

    def gate_exp(g):
        wait(act, F.d_ready, g + 1)
        n = GB if kind == 0 else GB * E
        nc.scalar.activation(K.ge[:, 0:n], K.gd[:, 0:n], ACT.Exp).then_inc(F.e_ready.sem, 1)

    def keep_wT(g):
        wait(act, F.wT_ready, g + 1)
        nc.scalar.copy(K.wT[:, :], K.pP[0:E, :]).then_inc(F.wT_done.sem, 1)

    def hidden(g, e):
        for hb in range(HB):
            v = e * HB + hb
            u = g * (NE * HB) + v
            if kind in (1, 2):
                wait(act, F.h_ready, u + 1)
                if hb == 0:
                    wait(act, F.y_ready, g * F.ys + max(e - 1, 0))
                nc.scalar.activation(K.hT[:, e % 2, hb, :], K.pH[v % 4][:, :], ACT.Relu,
                                     bias=F.b1[:, v:v + 1]).then_inc(F.h_done.sem, 1)
            else:
                wait(act, F.a_ready, u + 1)
                wait(act, F.h_done, g * (NE * HB) + max(v - 1, 0))
                nc.scalar.activation(K.silu[:, v % 2, :], K.pH[2 * (v % 2)][:, :], ACT.Silu,
                                     scale=F.scale).then_inc(F.silu_done.sem, 1)

    act.preload_act_table_set(LN_EXP)
    rstd(0)
    keep_xT(0)

    def body(g, more):
        if NE > 1:
            gate_exp(g)
        for e in range(NE):
            hidden(g, e)
            if e == 1 and kind in (1, 2):
                keep_wT(g)
        if more:
            if kind in (0, 3):
                act.preload_act_table_set(LN_EXP)
            rstd(g + 1)
            keep_xT(g + 1)

    groups(act, body)
    if kind in (0, 3):
        act.preload_act_table_set(LN_EXP)


def ffn_dve(nc, dve, K, kind):
    F = K.ffn[kind]
    NE, HB = F.experts, F.blocks
    src = K.x1 if kind == 0 else K.x
    f4 = [T, GB, E]

    def stats(g):
        c = Chain(dve, F.stat_step, g, 1)
        for b in range(GB):
            op = nc.vector.bn_stats(K.bng[:, b, :], batch(src, g * GB + b))
        c.link(op)
        nc.vector.memset(K.spare[:, :], 0.0)
        for b in range(GB):
            op = nc.vector.bn_aggr(K.mvg[:, b, :], K.bng[:, b, :])
        op.then_inc(F.var_ready.sem, 1)

    def normalise(g):
        wait(dve, F.rstd_ready, g + 1)
        wait(dve, F.xT_ready, g)
        for b in range(GB):
            op = nc.vector.tensor_scalar(K.xg[:, b, :], batch(src, g * GB + b), K.mvg[:, b, 0:1], K.rsg[:, b:b + 1],
                                         ALU.subtract, ALU.mult)
        op.then_inc(F.xn_ready.sem, 1)

    def first_max(c, onehot):
        c.link(nc.vector.reduce_max(K.gm[:, :], K.gl[:, :, :], AX.X))
        c.link(nc.vector.tensor_tensor(onehot, K.gl[:, :, :], K.gm[:, :].unsqueeze(2).to_broadcast(f4), ALU.is_equal))
        c.link(nc.vector.tensor_tensor(onehot, onehot, K.desc[:, :].unsqueeze(1).to_broadcast(f4), ALU.mult))
        c.link(nc.vector.reduce_max(K.gi[:, :], onehot, AX.X))
        c.link(nc.vector.tensor_tensor(onehot, onehot, K.gi[:, :].unsqueeze(2).to_broadcast(f4), ALU.is_equal))

    def gating(g):
        wait(dve, F.l_ready, g + 1)
        pl = K.pP[:, 0:GB * E].rearrange("p (b e) -> p b e", b=GB)
        c = Chain(dve, F.gate_step, g, 17 if kind == 0 else 8)
        if kind == 0:
            c.link(nc.vector.tensor_copy(K.gl[:, :, :], pl))
            first_max(c, K.g1[:, :, :])
            c.link(nc.vector.tensor_copy(K.gm1[:, :], K.gm[:, :]))
            c.link(nc.vector.scalar_tensor_tensor(K.gl[:, :, :], K.g1[:, :, :], NEG, K.gl[:, :, :], ALU.mult, ALU.add))
            first_max(c, K.g2[:, :, :])
            nc.vector.tensor_tensor(K.gd[:, 0:GB], K.gm[:, :], K.gm1[:, :], ALU.subtract).then_inc(F.d_ready.sem, 1)
            wait(dve, F.e_ready, g + 1)
            c.link(nc.vector.tensor_scalar(K.gs[:, :], K.ge[:, 0:GB], 1.0, None, ALU.add))
            c.link(nc.vector.reciprocal(K.gs[:, :], K.gs[:, :]))
            c.link(nc.vector.tensor_tensor(K.g2[:, :, :], K.g2[:, :, :], K.ge[:, 0:GB].unsqueeze(2).to_broadcast(f4), ALU.mult))
            c.link(nc.vector.tensor_tensor(K.g2[:, :, :], K.g2[:, :, :], K.g1[:, :, :], ALU.add))
            nc.vector.tensor_tensor(K.wts[:, :, :], K.g2[:, :, :], K.gs[:, :].unsqueeze(2).to_broadcast(f4),
                                    ALU.mult).then_inc(F.w_ready.sem, 1)
        else:
            bg = K.row({1: "bg1", 2: "br2"}[kind]).unsqueeze(1).to_broadcast(f4)
            c.link(nc.vector.tensor_tensor(K.gl[:, :, :], pl, bg, ALU.add))
            first_max(c, K.g1[:, :, :])
            nc.vector.tensor_tensor(K.gd[:, :].rearrange("p (b e) -> p b e", b=GB), K.gl[:, :, :],
                                    K.gm[:, :].unsqueeze(2).to_broadcast(f4), ALU.subtract).then_inc(F.d_ready.sem, 1)
            wait(dve, F.e_ready, g + 1)
            c.link(nc.vector.reduce_sum(K.gs[:, :], K.ge[:, :].rearrange("p (b e) -> p b e", b=GB), AX.X))
            c.link(nc.vector.reciprocal(K.gs[:, :], K.gs[:, :]))
            nc.vector.tensor_tensor(K.wts[:, :, :], K.g1[:, :, :], K.gs[:, :].unsqueeze(2).to_broadcast(f4),
                                    ALU.mult).then_inc(F.w_ready.sem, 1)
        c.done()
        wait(dve, F.w_ready, g + 1)

    def product(g, e):
        for hb in range(HB):
            v = e * HB + hb
            u = g * (NE * HB) + v
            wait(dve, F.silu_done, u + 1)
            wait(dve, F.b_ready, u + 1)
            if hb == 0:
                wait(dve, F.y_ready, g * F.ys + max(e - 1, 0))
            if F.scale == 1.0:
                op = nc.vector.tensor_tensor(K.hT[:, e % 2, hb, :], K.silu[:, v % 2, :], K.pH[2 * (v % 2) + 1][:, :],
                                             ALU.mult)
            else:
                op = nc.vector.scalar_tensor_tensor(K.hT[:, e % 2, hb, :], K.pH[2 * (v % 2) + 1][:, :], F.scale,
                                                    K.silu[:, v % 2, :], ALU.mult, ALU.mult)
            op.then_inc(F.h_done.sem, 1)

    def add_up(g, e):
        y = g * F.ys + e
        wait(dve, F.y_ready, y + 1)
        wait(dve, F.acc_done, y)
        bank = K.pY[e % 2]
        for b in range(GB):
            xb = batch(K.x, g * GB + b)
            if NE > 1 and e < NE:
                op = nc.vector.scalar_tensor_tensor(xb, bank[:, b * T:(b + 1) * T], K.wts[:, b, e:e + 1], xb,
                                                    ALU.mult, ALU.add)
            else:
                op = nc.vector.tensor_tensor(xb, bank[:, b * T:(b + 1) * T], xb, ALU.add)
        op.then_inc(F.acc_done.sem, 1)

    dve.wait_ge(K.x_done, K.x_before_ffn[kind])
    stats(0)
    normalise(0)

    def body(g, more):
        if NE > 1:
            gating(g)
        for e in range(NE):
            if kind in (0, 3):
                product(g, e)
            if e == max(NE - 2, 0) and more:
                stats(g + 1)
            if e:
                add_up(g, e - 1)
        if more:
            normalise(g + 1)
        add_up(g, NE - 1)
        if kind in (1, 2):
            add_up(g, NE)

    groups(dve, body)
    wait(dve, F.acc_done, (B // GB) * F.ys)
    dve.sem_inc(K.x_done, 1)



class Uses:

    ORDER = [("oT0", -1), ("oT1", -1), ("y", -1), ("xT", 2), ("Q0", 2), ("Q1", 2), ("K0", 2), ("K1", 2), ("m", 1),
             ("V0", 2), ("V1", 2), ("QT0", 2), ("QT1", 2), ("KT0", 2), ("KT1", 2)]

    def __init__(self):
        self.total, self.looped = 0, None

    def of(self, s):
        n = len(self.ORDER)
        if s.static():
            if self.looped is not None:
                self.total, self.looped = self.looped + n * 2 * ((B - 3 - 2) // 2), None
            start = self.total
        else:
            if self.looped is None:
                self.looped = self.total
            base = self.looped + n * (s.c - 2)
            start = s.i * (2 * n) + base
        names = [name for name, d in self.ORDER if (s + d).exists()]
        at = {name: start + j for j, name in enumerate(names)}
        even = self.total if s.static() else base
        self.bank = {name: (even + j) % 2 for j, name in enumerate(names)}
        if s.static():
            self.total += len(names)
        self.at, self.start = at, start
        return at


def attn3_pe(nc, pe, K):
    uses = Uses()

    def free(name):
        wait(pe, K.a_done, uses.at[name] - 1)
        return K.pA[uses.bank[name]]

    def transpose_x(s):
        wait(pe, K.l3_xn_ready, s.n + 1)
        nc.tensor.transpose(free("xT")[:, 0:T], K.xn[:, :], K.ident[:, :]).then_inc(K.a_ready, 1)

    def project(s, which):
        if which == 0:
            wait(pe, K.a_done, uses.at["xT"] + 1)
            pe.wait_ge(K.ctx_loaded[s.par], 16 * (s.half + 1 + (B // 2) * 3))
        src = K.xT[:, s.par, :] if which == 0 else K.ctx[:, s.par, :]
        for half in range(2):
            op = nc.tensor.matmul(free(f"{'QKV'[which]}{half}")[:, :], src,
                                  K.w3qkv[:, which, half * 512:(half + 1) * 512], start=True, stop=True)
            op.then_inc(K.a_ready, 1)

    def transpose_qk(s, which):
        wait(pe, (K.q3n_ready, K.k3n_ready)[which], s.n + 1)
        for half in range(2):
            bank = free(f"{'QK'[which]}T{half}")
            for j in range(4):
                jj = half * 4 + j
                op = nc.tensor.transpose(bank[:, j * T:(j + 1) * T], K.qk3n[:, which, jj * T:(jj + 1) * T], K.ident[:, :])
            op.then_inc(K.a_ready, 1)

    def row_scores(s, u):
        if u == 0:
            wait(pe, K.a_done, uses.start)
        wait(pe, K.s3_done, 4 * s.n + u - 1)
        r = slice(64 * (u % 2), 64 * (u % 2) + 64)
        for a in range(4):
            j = 4 * (u // 2) + a
            op = nc.tensor.matmul(K.pS[u % 2][:, a * T:(a + 1) * T], K.q3T[r, s.par, j, :], K.k3T[r, s.par, j, :],
                                  start=True, stop=True)
        op.then_inc(K.s3_ready, 1)

    def transpose_max(s):
        wait(pe, K.m33_ready, s.n + 1)
        nc.tensor.transpose(free("m")[:, :].bitcast(BF16)[:, 0:T], K.m3[:, :], K.identb[:, :]).then_inc(K.a_ready, 1)

    def col_scores(s, u):
        if u == 0:
            wait(pe, K.a_done, uses.start - (6 if (s + 1).exists() else 0))
        wait(pe, K.exp3_done, 4 * s.n + u - 1)
        r = slice(64 * (u % 2), 64 * (u % 2) + 64)
        bank = K.pC[u % 2]
        for a in range(4):
            j = 4 * (u // 2) + a
            nc.tensor.matmul(bank[:, a * T:(a + 1) * T], K.k3T[r, s.par, j, :], K.q3T[r, s.par, j, :],
                             start=(a == 0), stop=False, skip_group_check=True)
        for a in range(4):
            h = 2 * (4 * (u // 2) + a) + u % 2
            op = nc.tensor.matmul(bank[:, a * T:(a + 1) * T], K.sel[:, h, :], K.mT[:, :], start=False, stop=(a == 3),
                                  skip_group_check=True)
        op.then_inc(K.c3_ready, 1)

    def probs_v(s, u):
        wait(pe, K.exp3_done, 4 * s.n + u + 1)
        wait(pe, K.on3_done, 4 * s.n + u - 1)
        for a in range(4):
            h = 2 * (4 * (u // 2) + a) + u % 2
            op = nc.tensor.matmul(K.pO3[u % 2][:, a * (HD3 + 1):(a + 1) * (HD3 + 1)], K.pt[:, u % 2, a * T:(a + 1) * T],
                                  K.v3[:, s.par, h, :], start=True, stop=True)
        op.then_inc(K.pv3_done, 1)

    def transpose_o(s):
        wait(pe, K.on3_done, 4 * s.n + 4)
        for half in range(2):
            bank = free(f"oT{half}")
            for j in range(4):
                jj = half * 4 + j
                op = nc.tensor.transpose(bank[:, j * T:(j + 1) * T], K.on3[:, jj * T:(jj + 1) * T], K.ident[:, :])
            op.then_inc(K.a_ready, 1)

    def out_project(s):
        wait(pe, K.a_done, uses.at["oT1"] + 1)
        bank = free("y")
        for j in range(8):
            op = nc.tensor.matmul(bank[:, 0:D], K.o3T[:, j, :], K.wu[:, j, :], start=(j == 0), stop=(j == 7))
        op.then_inc(K.a_ready, 1)

    pe.wait_ge(K.w3_loaded, 64)
    pe.wait_ge(K.w3_centred, 2)

    def body(s):
        uses.of(s)
        a, nx, pr = s + 1, s + 2, s + -1
        for u in range(4):
            if s.exists():
                col_scores(s, u)
            if a.exists():
                row_scores(a, u)
            if u == 0 and pr.exists():
                transpose_o(pr)
            if u >= 1 and s.exists():
                probs_v(s, u - 1)
            if u == 1:
                if pr.exists():
                    out_project(pr)
                if nx.exists():
                    transpose_x(nx)
            if u == 2 and nx.exists():
                project(nx, 0)
                project(nx, 1)
        if s.exists():
            probs_v(s, 3)
        if a.exists():
            transpose_max(a)
        if nx.exists():
            project(nx, 2)
            transpose_qk(nx, 0)
            transpose_qk(nx, 1)

    pipeline(pe, body, 3, 1)


def attn3_act(nc, act, K):
    uses = Uses()

    def taken(name):
        wait(act, K.a_ready, uses.at[name] + 1)
        return K.pA[uses.bank[name]]

    def rstd(s):
        wait(act, K.l3_var_ready, s.n + 1)
        c = Chain(act, K.l3_rstd_step, s.n, 1)
        c.link(nc.scalar.activation(K.lnv[:, 0:1], K.mv[:, s.par, 1:2], ACT.Ln, bias=K.eps[:, :]))
        nc.scalar.activation(K.rs[:, s.par, 0:1], K.lnv[:, 0:1], ACT.Exp, scale=-0.5).then_inc(K.l3_rstd_ready, 1)

    def keep_qk(s, which):
        if which == 0:
            wait(act, K.k3n_ready, s.n)
        for half in range(2):
            nc.scalar.copy(K.qk3[:, which, half * 512:(half + 1) * 512],
                           taken(f"{'QK'[which]}{half}")[:, :]).then_inc(K.a_done, 1)

    def keep_v(s):
        for half in range(2):
            nc.scalar.copy(K.v3[:, s.par, half * 8:(half + 1) * 8, 0:HD3],
                           taken(f"V{half}")[:, :].rearrange("p (h d) -> p h d", h=8)).then_inc(K.a_done, 1)

    def head_rstd(s):
        wait(act, K.ss_ready, s.n + 1)
        c = Chain(act, K.l3_hr_step, s.n, 1)
        c.link(nc.scalar.activation(K.lnh[:, :], K.ss[:, :], ACT.Ln, bias=K.eps[:, :], scale=1.0 / HD3))
        nc.scalar.activation(K.rh[:, :], K.lnh[:, :], ACT.Exp, scale=-0.5).then_inc(K.rh_ready, 1)

    def keep_qkT(s, which):
        dst = (K.q3T, K.k3T)[which]
        w, b = ((K.qn8[:, 0:1], K.qn8[:, 1:2]), (K.col("kn_w"), K.col("kn_b")))[which]
        for half in range(2):
            nc.scalar.activation(dst[:, s.par, half * 4:(half + 1) * 4, :].rearrange("p a q -> p (a q)"),
                                 taken(f"{'QK'[which]}T{half}")[:, :], ACT.Identity, scale=w, bias=b).then_inc(K.a_done, 1)

    def exp(s, u):
        wait(act, K.c3_ready, 4 * s.n + u + 1)
        wait(act, K.pv3_done, 4 * s.n + u - 1)
        nc.scalar.activation(K.pt[:, u % 2, :], K.pC[u % 2][:, :], ACT.Exp).then_inc(K.exp3_done, 1)

    def keep_oT(s):
        for half in range(2):
            nc.scalar.copy(K.o3T[:, half * 4:(half + 1) * 4, :].rearrange("p a q -> p (a q)"),
                           taken(f"oT{half}")[:, :]).then_inc(K.a_done, 1)

    def body(s):
        uses.of(s)
        a, nx, pr, st = s + 1, s + 2, s + -1, s + 3
        for u in range(4):
            if s.exists():
                exp(s, u)
            if u == 0 and pr.exists():
                keep_oT(pr)
            if u == 1:
                if pr.exists():
                    wait(act, K.x3_done, pr.n)
                    nc.scalar.copy(K.yb[:, :], taken("y")[:, 0:D]).then_inc(K.a_done, 1)
                if nx.exists():
                    nc.scalar.copy(K.xT[:, nx.par, :], taken("xT")[:, 0:T]).then_inc(K.a_done, 1)
            if u == 2 and nx.exists():
                keep_qk(nx, 0)
                keep_qk(nx, 1)
        if a.exists():
            nc.scalar.copy(K.mT[:, :], taken("m")[:, :].bitcast(BF16)[:, 0:T]).then_inc(K.a_done, 1)
        if nx.exists():
            keep_v(nx)
            head_rstd(nx)
            keep_qkT(nx, 0)
            keep_qkT(nx, 1)
        if st.exists():
            rstd(st)

    pipeline(act, body, 3, 1)


def attn3_dve(nc, dve, K):
    uses = Uses()

    def stats(s):
        c = Chain(dve, K.l3_stat_step, s.n, 1)
        c.link(nc.vector.bn_stats(K.bn[:, :], batch(K.x, s.n)))
        nc.vector.memset(K.spare[:, :], 0.0)
        nc.vector.bn_aggr(K.mv[:, s.par, :], K.bn[:, :]).then_inc(K.l3_var_ready, 1)

    def normalise(s):
        wait(dve, K.l3_rstd_ready, s.n + 1)
        nc.vector.tensor_scalar(K.xn[:, :], batch(K.x, s.n), K.mv[:, s.par, 0:1], K.rs[:, s.par, 0:1],
                                ALU.subtract, ALU.mult).then_inc(K.l3_xn_ready, 1)

    def row_max(s, u):
        wait(dve, K.s3_ready, 4 * s.n + u + 1)
        out = K.m[:, :].rearrange("p (j a b) -> p j a b", j=2, a=4)[:, u // 2, :, u % 2]
        nc.vector.reduce_max(out, K.pS[u % 2][:, :].rearrange("p (a k) -> p a k", a=4), AX.X).then_inc(K.s3_done, 1)

    def split_max(s):
        dve.wait_ge(K.s3_done, 4 * s.n + 4)
        c = Chain(dve, K.l3_split_step, s.n, 3)
        c.link(nc.vector.tensor_scalar(K.m3[:, 0:H], K.m[:, :], -1.0, None, ALU.mult))
        c.link(nc.vector.scalar_tensor_tensor(K.mr[:, :], K.m[:, :], -1.0, K.m3[:, 0:H], ALU.mult, ALU.subtract))
        c.link(nc.vector.tensor_copy(K.m3[:, H:2 * H], K.mr[:, :]))
        nc.vector.tensor_tensor(K.m3[:, 2 * H:3 * H], K.mr[:, :], K.m3[:, H:2 * H],
                                ALU.subtract).then_inc(K.m33_ready, 1)

    def normalise_o(s, u):
        wait(dve, K.pv3_done, 4 * s.n + u + 1)
        po = K.pO3[u % 2][:, 0:4 * (HD3 + 1)].rearrange("p (a d) -> p a d", a=4)
        out = K.on3[:, :].rearrange("p (j a b d) -> p j a b d", j=2, a=4, b=2)[:, u // 2, :, u % 2, :]
        c = Chain(dve, K.l3_rec_step, 4 * s.n + u, 1)
        rec = K.rec[:, 4 * (u % 2):4 * (u % 2) + 4]
        c.link(nc.vector.reciprocal(rec, po[:, :, HD3]))
        nc.vector.tensor_tensor(out, po[:, :, 0:HD3], rec.unsqueeze(2).to_broadcast([T, 4, HD3]),
                                ALU.mult).then_inc(K.on3_done, 1)

    def squares(s):
        wait(dve, K.sq_ready, s.n + 1)
        nc.vector.reduce_sum(K.ss[:, :], K.sq3[:, :, :].rearrange("p w (h d) -> p (w h) d", d=HD3),
                             AX.X).then_inc(K.ss_ready, 1)

    def head_norm(s, which):
        if which == 0:
            wait(dve, K.rh_ready, s.n + 1)
        op = nc.vector.tensor_tensor(K.qk3n[:, which, :].rearrange("p (h d) -> p h d", h=H),
                                     K.qk3[:, which, :].rearrange("p (h d) -> p h d", h=H),
                                     K.rh[:, which * H:(which + 1) * H].unsqueeze(2).to_broadcast([T, H, HD3]), ALU.mult)
        op.then_inc((K.q3n_ready, K.k3n_ready)[which], 1)

    def residual(s):
        wait(dve, K.a_done, uses.at["y"] + 1)
        c = Chain(dve, K.l3_res_step, s.n, 1)
        c.link(nc.vector.tensor_tensor(K.y3[:, :], K.yb[:, :], K.row("bu3"), ALU.add))
        nc.vector.tensor_tensor(batch(K.x, s.n), batch(K.x, s.n), K.y3[:, :], ALU.add).then_inc(K.x3_done, 1)

    dve.wait_ge(K.x_done, K.x_before_attn[3])

    def body(s):
        uses.of(s)
        a, nx, pr, st = s + 1, s + 2, s + -1, s + 3
        if nx.exists():
            normalise(nx)
        for u in range(4):
            if a.exists():
                row_max(a, u)
            if u >= 1 and s.exists():
                normalise_o(s, u - 1)
            if u == 2 and pr.exists():
                residual(pr)
        if a.exists():
            split_max(a)
        if s.exists():
            normalise_o(s, 3)
        if nx.exists():
            squares(nx)
            head_norm(nx, 0)
            head_norm(nx, 1)
        if st.exists():
            stats(st)

    pipeline(dve, body, 3, 1)
    dve.wait_ge(K.x3_done, B)
    dve.sem_inc(K.x_done, 1)


def attn3_pool(nc, pool, K):
    uses = Uses()

    def body(s):
        uses.of(s)
        if (s + 2).exists():
            wait(pool, K.a_done, uses.at["K1"] + 1)
            nc.gpsimd.tensor_tensor(K.sq3[:, :, :], K.qk3[:, :, :], K.qk3[:, :, :], ALU.mult).then_inc(K.sq_ready, 1)

    pipeline(pool, body, 3, 1)



CONSTS = [("ident", T), ("blockmask", T), ("headmask", H), ("hmask", G), ("desc", E), ("selc", H), ("causal", T),
          ("causalT", T), ("row0", T)]
NCONST = sum(w for _, w in CONSTS)
CONST_AT = {}
_at = 0
for _n, _w in CONSTS:
    CONST_AT[_n] = slice(_at, _at + _w)
    _at += _w


def setup_dve(nc, dve, K):
    def const(name):
        return K.consts[:, CONST_AT[name]]

    nc.vector.memset(K.eps[:, :], EPS)
    nc.vector.memset(K.vaug[:, :, :, :], 1.0)
    nc.vector.memset(K.linv[:, :, :], 1.0)
    nc.vector.memset(K.m3[:, :], 0.0)
    nc.vector.memset(K.prow[1][:, :, :], 0.0).then_inc(K.set_step, 1)
    dve.wait_ge(K.consts_loaded, 16)
    nc.vector.tensor_copy(K.identb[:, :], const("ident"))
    nc.vector.tensor_copy(K.causal[:, :], const("causal"))
    nc.vector.tensor_copy(K.causalT[:, :], const("causalT"))
    nc.vector.tensor_copy(K.row0[:, :], const("row0"))
    nc.vector.tensor_copy(K.sel[:, :, :], const("selc").unsqueeze(2).to_broadcast([T, H, T]))
    dve.wait_ge(K.rows_loaded, 16)
    dve.wait_ge(K.cols_loaded, 16)
    dve.wait_ge(K.masks_loaded, 64)
    for n in (1, 2):
        nc.vector.tensor_scalar(K.bqs[:, n - 1:n], K.col(f"bq{n}"), HD ** -0.5, None, ALU.mult)
    nc.vector.tensor_scalar(K.qn8[:, 0:1], K.col("qn_w"), HD3 ** -0.5, None, ALU.mult)
    nc.vector.tensor_scalar(K.qn8[:, 1:2], K.col("qn_b"), HD3 ** -0.5, None, ALU.mult)
    nc.vector.tensor_scalar(K.pcol[1][:, :, 0], K.mcol[:, 0, :], 1.0, -NEG, ALU.subtract, ALU.mult)
    nc.vector.tensor_scalar(K.pcol[2][:, :, 0], K.mcol[:, 1, :], NEG, 2.0, ALU.mult, ALU.mult)
    dve.wait_ge(K.set_step, 1)
    nc.vector.tensor_scalar(K.prow[1][0:1, :, :].rearrange("p b k -> p (b k)"), K.mrow[0:1, 0, :], 1.0, -NEG,
                            ALU.subtract, ALU.mult)
    def part(out, a, b):
        K.parts += 1
        nc.vector.tensor_tensor(out, a, b, ALU.subtract).then_inc(K.part_step, 1)
        dve.wait_ge(K.part_step, K.parts)
    K.parts = 0
    for src, dst in ((K.amf[:, 0, :], K.amask), (K.amf[:, 1, :], K.amaskT)):
        for step, op in enumerate((lambda: nc.vector.tensor_scalar(src, src, NEG, None, ALU.max),
                                   lambda: nc.vector.tensor_copy(dst[:, 0, :], src))):
            K.parts += 1
            op().then_inc(K.part_step, 1)
            dve.wait_ge(K.part_step, K.parts)
        part(src, src, dst[:, 0, :])
        K.parts += 1
        nc.vector.tensor_copy(dst[:, 1, :], src).then_inc(K.part_step, 1)
        dve.wait_ge(K.part_step, K.parts)
        part(dst[:, 2, :], src, dst[:, 1, :])
    z, t = K.row("scale0"), K.sp
    c = Chain(dve, K.sp_step, 0, 11)
    c.link(nc.vector.tensor_scalar(t[:, 0, :], z, -1.0, None, ALU.mult))
    c.link(nc.vector.tensor_tensor(t[:, 0, :], t[:, 0, :], z, ALU.min))
    dve.sem_inc(K.spz_ready, 1)
    dve.wait_ge(K.spe_ready, 1)
    c.link(nc.vector.tensor_scalar(t[:, 2, :], t[:, 1, :], 1.0, None, ALU.add))
    dve.sem_inc(K.spu_ready, 1)
    c.link(nc.vector.tensor_scalar(t[:, 3, :], t[:, 2, :], 1.0, None, ALU.is_equal))
    c.link(nc.vector.scalar_tensor_tensor(t[:, 4, :], t[:, 2, :], 1.0, t[:, 3, :], ALU.subtract, ALU.add))
    c.link(nc.vector.reciprocal(t[:, 4, :], t[:, 4, :]))
    dve.wait_ge(K.spl_ready, 1)
    c.link(nc.vector.tensor_tensor(t[:, 5, :], t[:, 5, :], t[:, 3, :], ALU.add))
    c.link(nc.vector.tensor_tensor(t[:, 5, :], t[:, 5, :], t[:, 1, :], ALU.mult))
    c.link(nc.vector.tensor_tensor(t[:, 5, :], t[:, 5, :], t[:, 4, :], ALU.mult))
    c.link(nc.vector.scalar_tensor_tensor(t[:, 5, :], z, 0.0, t[:, 5, :], ALU.max, ALU.add))
    c.link(nc.vector.reciprocal(K.isp[:, :], t[:, 5, :]))
    dve.sem_inc(K.consts_ready, 1)


def setup_act(nc, act, K):
    act.preload_act_table_set(LN_EXP)
    act.wait_ge(K.spz_ready, 1)
    nc.scalar.activation(K.sp[:, 1, :], K.sp[:, 0, :], ACT.Exp).then_inc(K.spe_ready, 1)
    act.wait_ge(K.spu_ready, 1)
    nc.scalar.activation(K.sp[:, 5, :], K.sp[:, 2, :], ACT.Ln).then_inc(K.spl_ready, 1)


def before_layer2(nc, dve, K):
    nc.vector.tensor_scalar(K.prow[2][0:1, :, :].rearrange("p b k -> p (b k)"), K.mrow[0:1, 1, :], NEG, 2.0,
                            ALU.mult, ALU.mult).then_inc(K.prow2_ready, 1)


def before_layer3(nc, dve, K):
    for n, w in enumerate((K.w3qkv[:, 0, :], K.w3qkv[:, 1, :])):
        if n == 0:
            dve.wait_ge(K.w3_loaded, 64)
        heads = w.rearrange("p (h d) -> p h d", h=H)
        c = Chain(dve, K.centre_step, n, 2)
        c.link(nc.vector.reduce_sum(K.rec[:, :], heads, AX.X))
        c.link(nc.vector.tensor_scalar(K.rec[:, :], K.rec[:, :], -1.0 / HD3, None, ALU.mult))
        nc.vector.tensor_tensor(heads, heads, K.rec[:, :].unsqueeze(2).to_broadcast([T, H, HD3]),
                                ALU.add).then_inc(K.w3_centred, 1)
        dve.wait_ge(K.w3_centred, n + 1)
    nc.vector.memset(K.v3[:, :, :, HD3:HD3 + 1], 1.0)
    dve.wait_ge(K.int_loaded, 48)
    nc.vector.tensor_scalar(K.wint[:, :], K.wint[:, :].bitcast(I32), 1.0 / 127.0, None, ALU.mult).then_inc(K.deq_ready, 1)


def build(nc, a, out):
    ctx = ExitStack()
    with ctx:
        def sb(name, shape, dt=F32):
            return ctx.enter_context(nc.sbuf_tensor(name, shape, dt))

        K = Names()
        K.x = sb("x", [T, B, D])
        K.lin_w = sb("lin_w", [D, 3, D])
        K.wsmall = [sb(f"attn_w{n}", [D, 4, D]) for n in range(3)]
        K.attn_w = [[w[:, n, :] for n in range(4)] for w in K.wsmall]
        early = sb("early", [128, 8192])
        w0_1 = early[:, 0:2048].rearrange("p (e n) -> p e n", e=E)
        w0_2 = early[:, 2048:4096].rearrange("p (e n) -> p e n", e=E)
        w0_3 = early[:, 4096:6144].rearrange("p (e h n) -> p e h n", e=E, h=2)
        K.x1 = early[:, 6144:8192].rearrange("p (b d) -> p b d", b=B)
        K.qk3 = early[:, 0:2048].rearrange("p (w n) -> p w n", w=2)
        K.qk3n = early[:, 2048:4096].rearrange("p (w n) -> p w n", w=2)
        K.sq3 = early[:, 4096:6144].rearrange("p (w n) -> p w n", w=2)
        qkT = early[:, 6144:8192].rearrange("p (c j q) -> p c j q", c=2, j=8)
        w1_1 = sb("w1_1", [128, E * 512])
        late = w1_1[:, :]
        K.q3T = qkT
        K.k3T = late[:, 0:2048].rearrange("p (c j q) -> p c j q", c=2, j=8)
        K.on3 = late[:, 2048:3072]
        K.o3T = late[:, 3072:4096].rearrange("p (j q) -> p j q", j=8)
        w1_2 = sb("w1_2", [128, E, 4, D])
        w2_1 = sb("w2_1", [128, E * 512])
        w2_2 = sb("w2_2", [128, E, 4, D])
        gates = sb("gates", [D, 3, E])
        b1s = sb("b1s", [128, 2, E * 4])
        b2s = sb("b2s", [E, 2, D])
        K.w3qkv = sb("w3qkv", [D, 3, H * HD3])
        K.wu = sb("wu", [128, 8, D])
        K.wint = sb("wint", [128, 9 * 128])
        K.v3 = sb("v3", [T, 2, H, HD3 + 1])
        K.rows, K.cols = sb("rows", [128, NROW]), sb("cols", [128, NCOL])
        K.row = lambda name: K.rows[:, ROW_AT[name][0]:ROW_AT[name][0] + ROW_AT[name][1]]
        K.row2 = lambda one, two: K.rows[:, ROW_AT[one][0]:ROW_AT[two][0] + ROW_AT[two][1]]
        K.col = lambda name: K.cols[:, COLS.index(name):COLS.index(name) + 1]
        K.consts = sb("consts", [128, NCONST])
        K.ident, K.blockmask = K.consts[:, CONST_AT["ident"]], K.consts[:, CONST_AT["blockmask"]]
        K.headmask, K.hmask = K.consts[:, CONST_AT["headmask"]], K.consts[:, CONST_AT["hmask"]]
        K.desc = K.consts[:, CONST_AT["desc"]]
        K.identb, K.causal = sb("identb", [T, T], BF16), sb("causalb", [T, T], BF16)
        K.causalT, K.row0 = sb("causalTb", [T, T], BF16), sb("row0b", [T, T], BF16)
        K.sel = sb("sel", [T, H, T], BF16)
        K.eps, K.bqs, K.qn8 = sb("eps", [128, 1]), sb("bqs", [D, 2]), sb("qn8", [128, 2])
        prow = sb("prow", [128, B, T], BF16)
        K.prow = {1: prow, 2: prow}
        K.pcol = {1: sb("pcol1", [T, B, 1]), 2: sb("pcol2", [T, B, 1])}
        K.spare, K.pc = sb("spare", [T, 1]), sb("pc", [T, 2, 1])
        K.mcol, K.mrow = sb("mcol", [T, 2, B], U8), sb("mrow", [1, 2, B * T], U8)
        K.amf = sb("amf", [T, 2, T])
        K.amask, K.amaskT = sb("amask", [T, 3, T], BF16), sb("amaskT", [T, 3, T], BF16)
        shared = sb("shared", [128, 2 * 4 * NT])
        K.sp, K.isp = shared[:, 2048:2816].rearrange("p (a d) -> p a d", a=6), sb("isp", [128, D])
        K.ctx, K.xT = sb("ctx", [D, 2, T]), sb("xT", [D, 2, T])
        K.xn, K.qT, K.kT = sb("xn", [T, D]), sb("qT", [D, 2, T]), sb("kT", [D, 2, T])
        K.kblk = shared[:, 0:1024].rearrange("p (c a k) -> p c a k", c=2, a=G)
        K.qblk = shared[:, 1024:2048].rearrange("p (c a k) -> p c a k", c=2, a=G)
        K.vaug, K.pt = sb("vaug", [T, 2, H, HD + 1]), shared[:, 2048:3072].rearrange("p (c n) -> p c n", c=2)
        K.m, K.m3, K.mr, K.mT = sb("m", [T, H]), sb("m3", [T, T], BF16), sb("mr", [T, H]), sb("mT", [T, T], BF16)
        K.rec, K.on, K.oT, K.yb = sb("rec", [T, H]), sb("on", [T, D]), sb("oT", [D, T]), sb("yb", [T, D])
        K.y3 = sb("y3", [T, D])
        K.bn, K.mv, K.rs = sb("bn", [T, 6]), sb("mv", [T, 2, 2]), sb("rs", [T, 2, 2])
        K.lnv, K.var2, K.var2a = sb("lnv", [T, 2]), sb("var2", [T, 1]), sb("var2a", [T, 1])
        K.ss, K.lnh, K.rh = sb("ss", [T, 2 * H]), sb("lnh", [T, 2 * H]), sb("rh", [T, 2 * H])
        K.ft, K.f2, K.f3 = (shared[:, n:n + 256].rearrange("p (a d) -> p a d", a=2) for n in (0, 256, 512))
        K.fm, K.fr, K.fs, K.lnr, K.froot = sb("fm", [T, 2]), sb("fr", [T, 2]), sb("fs", [T, 4]), sb("lnr", [T, 2]), sb("froot", [T, 2])
        K.feat, K.linv = shared[:, 1024:1536].rearrange("p (c a d) -> p c a d", c=2, a=2), sb("linv", [T, 2, D + 1])
        K.lqT, K.kvblk = sb("lqT", [D, T]), sb("kvblk", [D, D + H])
        K.xg, K.xTg = sb("xg", [T, GB, D]), sb("xTg", [D, NT])
        K.hT = shared[:, :].rearrange("p (c h n) -> p c h n", c=2, h=4)
        K.silu = sb("silu", [128, 2, NT])
        K.bng, K.mvg, K.lng, K.rsg = sb("bng", [T, GB, 6]), sb("mvg", [T, GB, 2]), sb("lng", [T, GB]), sb("rsg", [T, GB])
        K.gl, K.g1, K.g2, K.wts = (sb(n, [T, GB, E]) for n in ("gl", "g1", "g2", "wts"))
        K.gm, K.gm1, K.gi, K.gs = (sb(n, [T, GB]) for n in ("gm", "gm1", "gi", "gs"))
        K.gd, K.ge = sb("gd", [T, GB * E]), sb("ge", [T, GB * E])
        K.wT = sb("wT", [E, NT])

        bank = [ctx.enter_context(nc.psum_tensor(f"bank{n}", [128, 512], F32)) for n in range(8)]
        K.pT, K.pP, K.pO, K.pM = bank[0], bank[1], bank[6], bank[7]
        K.pS, K.pC, K.pH, K.pY, K.pA, K.pO3 = bank[2:4], bank[4:6], bank[2:6], bank[6:8], bank[0:2], bank[6:8]
        K.pMb = bank[7][:, :].bitcast(BF16)

        def sem(name):
            return ctx.enter_context(nc.semaphore(name))

        def sems(names):
            return [sem(name) for name in names.split()]

        K.a_done, K.a_ready, K.c3_ready, K.c_ready, K.centre_step = sems(
            "a_done a_ready c3_ready c_ready centre_step")
        K.cols_loaded, K.consts_loaded, K.consts_ready, K.deq_ready, K.exp3_done = sems(
            "cols_loaded consts_loaded consts_ready deq_ready exp3_done")
        K.exp_done, K.int_loaded, K.k3n_ready, K.kblk_ready, K.l3_hr_step = sems(
            "exp_done int_loaded k3n_ready kblk_ready l3_hr_step")
        K.l3_rec_step, K.l3_res_step, K.l3_rstd_ready, K.l3_rstd_step, K.l3_split_step = sems(
            "l3_rec_step l3_res_step l3_rstd_ready l3_rstd_step l3_split_step")
        K.l3_stat_step, K.l3_var_ready, K.l3_xn_ready, K.lin_f_ready, K.lin_f_step = sems(
            "l3_stat_step l3_var_ready l3_xn_ready lin_f_ready lin_f_step")
        K.lin_kv_done, K.lin_kv_ready, K.lin_o_done, K.lin_o_ready, K.lin_o_step = sems(
            "lin_kv_done lin_kv_ready lin_o_done lin_o_ready lin_o_step")
        K.lin_p_done, K.lin_p_ready, K.lin_qT_done, K.lin_qT_ready, K.lin_ratio_ready = sems(
            "lin_p_done lin_p_ready lin_qT_done lin_qT_ready lin_ratio_ready")
        K.lin_root_ready, K.lin_root_step, K.lin_rstd_ready, K.lin_rstd_step, K.lin_stat_step = sems(
            "lin_root_ready lin_root_step lin_rstd_ready lin_rstd_step lin_stat_step")
        K.lin_var_ready, K.lin_w_loaded, K.lin_xT_done, K.lin_xT_ready, K.lin_xn_ready = sems(
            "lin_var_ready lin_w_loaded lin_xT_done lin_xT_ready lin_xn_ready")
        K.m33_ready, K.m3_ready, K.mT_done, K.mT_ready, K.masks_loaded = sems(
            "m33_ready m3_ready mT_done mT_ready masks_loaded")
        K.oT_done, K.oT_ready, K.on3_done, K.on_ready, K.out_done = sems(
            "oT_done oT_ready on3_done on_ready out_done")
        K.part_step, K.pc_ready, K.prow2_ready, K.pv3_done, K.pv_done = sems(
            "part_step pc_ready prow2_ready pv3_done pv_done")
        K.q3n_ready, K.q_done, K.qblk_ready, K.qk_done, K.qkv_ready = sems(
            "q3n_ready q_done qblk_ready qk_done qkv_ready")
        K.rec_step, K.res_step, K.rh_ready, K.rows_loaded, K.rstd2_ready = sems(
            "rec_step res_step rh_ready rows_loaded rstd2_ready")
        K.rstd2_step, K.rstd_ready, K.rstd_step, K.s3_done, K.s3_ready = sems(
            "rstd2_step rstd_ready rstd_step s3_done s3_ready")
        K.s_ready, K.set_step, K.smax_done, K.sp_step, K.spe_ready = sems(
            "s_ready set_step smax_done sp_step spe_ready")
        K.spl_ready, K.split_step, K.spu_ready, K.spz_ready, K.sq_ready = sems(
            "spl_ready split_step spu_ready spz_ready sq_ready")
        K.ss_ready, K.stat_step, K.v_done, K.var2_ready, K.var2_step = sems(
            "ss_ready stat_step v_done var2_ready var2_step")
        K.var_ready, K.w3_centred, K.w3_loaded, K.x1_step, K.x3_done = sems(
            "var_ready w3_centred w3_loaded x1_step x3_done")
        K.xT_done, K.xT_ready, K.x_done, K.x_loaded, K.xn_ready = sems(
            "xT_done xT_ready x_done x_loaded xn_ready")
        K.y_done, K.y_ready = sems(
            "y_done y_ready")
        K.ctx_loaded = [ctx.enter_context(nc.semaphore(f"ctx_loaded{n}")) for n in range(2)]
        K.attn_w_loaded = [ctx.enter_context(nc.semaphore(f"attn_w_loaded{n}")) for n in range(3)]
        ffn_sems = {n: ctx.enter_context(nc.semaphore(f"ffn_{n}")) for n in FFN_COUNTS}
        K.ffn = {}
        for kind in range(4):
            F = Names()
            F.scale, F.w_loaded = 1.0, sem(f"ffn_w_loaded{kind}")
            at = {n: From(h, sum(FFN_COUNTS[n][:kind])) for n, h in ffn_sems.items()}
            F.var_ready, F.rstd_step, F.rstd_ready, F.stat_step, F.xn_ready, F.xT_ready, F.xT_done = (
                at[n] for n in "var_ready rstd_step rstd_ready stat_step xn_ready xT_ready xT_done".split())
            F.l_ready, F.d_ready, F.e_ready, F.w_ready, F.wT_ready, F.wT_done, F.a_ready = (
                at[n] for n in "l_ready d_ready e_ready w_ready wT_ready wT_done a_ready".split())
            F.b_ready, F.silu_done, F.h_ready, F.h_done, F.gate_step, F.y_ready, F.acc_done = (
                at[n] for n in "b_ready silu_done h_ready h_done gate_step y_ready acc_done".split())
            F.experts, F.blocks = (E, E, E, 1)[kind], (2, 4, 4, 3)[kind]
            F.ys = F.experts + (kind in (1, 2))
            K.ffn[kind] = F
        F0, F1, F2, F3 = (K.ffn[n] for n in range(4))
        F0.w1, F0.w2, F0.w3, F0.gate = w0_1, w0_2, w0_3, gates[:, 0, :]
        for n, F, w, w2 in ((1, F1, w1_1, w1_2), (2, F2, w2_1, w2_2)):
            F.w1, F.w3 = w[:, :].rearrange("p (e n) -> p e n", e=E), w2
            F.gate, F.b1, F.b2 = gates[:, n, :], b1s[:, n - 1, :], b2s[:, n - 1, :]
        F3.w1 = K.wint[:, 0:384].unsqueeze(1)
        F3.w2 = K.wint[:, 384:768].unsqueeze(1)
        F3.w3 = K.wint[:, 768:1152].rearrange("p (e h n) -> p e h n", e=1, h=3)
        F0.loaded, F1.loaded, F2.loaded = [(F0.w_loaded, 64)], [(F1.w_loaded, 80)], [(F2.w_loaded, 80)]
        F3.loaded = [(K.deq_ready, 1)]
        K.x_before_attn = {0: 16, 1: 33, 2: 50, 3: 67}
        K.x_before_ffn = {0: 32, 1: 49, 2: 66, 3: 68}
        K.n_consts = 1

        block = ctx.enter_context(nc.Block())

        @block.sync
        def _(sp):
            sp.dma_start(K.x[:, :, :], a["x"]).then_inc(K.x_loaded, 16)
            sp.dma_start(K.consts[:, :], a["consts"]).then_inc(K.consts_loaded, 16)
            sp.dma_start(K.rows[:, :], a["rows"].partition_broadcast(128)).then_inc(K.rows_loaded, 16)
            sp.dma_start(K.cols[:, :], a["cols"]).then_inc(K.cols_loaded, 16)
            sp.dma_start(K.mcol[:, :, :].bitcast(I32), a["mcol"]).then_inc(K.masks_loaded, 16)
            sp.dma_start(K.mrow[:, :, :].bitcast(I32), a["mrow"]).then_inc(K.masks_loaded, 16)
            sp.dma_start(K.amf[:, :, :], a["amf"]).then_inc(K.masks_loaded, 32)
            ctxT = a["ctxT"]

            def load_ctx(s):
                src = ctxT[s.n] if s.static() else ctxT[bass.ds(s.n, 1)].rearrange("a d t -> d (a t)")
                sp.dma_start(K.ctx[:, s.par, :], src).then_inc(K.ctx_loaded[s.par], 16)

            def lin(s):
                if s.c >= 2 or not s.static():
                    wait(sp, K.lin_p_ready, s.n - 1)
                load_ctx(s)

            pipeline(sp, lin, 0, 0)
            for lay in (1, 2):
                def attn(s):
                    wait(sp, K.qkv_ready, s.n + B * lay - 1)
                    load_ctx(s)
                sp.wait_ge(K.lin_p_ready, B)
                pipeline(sp, attn, 0, 0)
            sp.wait_ge(K.qkv_ready, 3 * B)
            uses = Uses()

            def attn3(s):
                uses.of(s)
                if s.exists() or s.c < 0:
                    wait(sp, K.a_ready, uses.start)
                if (s + 3).exists():
                    load_ctx(s + 3)

            pipeline(sp, attn3, 3, 1)
            for g in range(B // GB):
                wait(sp, K.ffn[3].acc_done, g + 1)
                sp.dma_start(out.rearrange("b t d -> t b d")[:, g * GB:(g + 1) * GB, :],
                             K.x[:, g * GB:(g + 1) * GB, :]).then_inc(K.out_done, 16)
            sp.wait_ge(K.out_done, 16 * (B // GB))

        @block.scalar
        def _(act):
            act.dma_start(K.lin_w[:, :, :], a["lin_w"]).then_inc(K.lin_w_loaded, 48)
            act.dma_start(K.wsmall[0][:, :, :], a["attn_w"][0]).then_inc(K.attn_w_loaded[0], 64)
            act.dma_start(gates[:, :, :], a["gates"]).then_inc(F0.w_loaded, 16)
            act.dma_start(w0_1, a["w0_1"].rearrange("e d h -> d e h")).then_inc(F0.w_loaded, 16)
            act.dma_start(w0_2, a["w0_2"].rearrange("e d h -> d e h")).then_inc(F0.w_loaded, 16)
            act.dma_start(w0_3, a["w0_3"]).then_inc(F0.w_loaded, 16)
            for n, F, w, w2, aw, aw2 in ((1, F1, w1_1, w1_2, a["w1_1"], a["w1_2"]), (2, F2, w2_1, w2_2, a["w2_1"], a["w2_2"])):
                act.dma_start(K.wsmall[n][:, :, :], a["attn_w"][n]).then_inc(K.attn_w_loaded[n], 64)
                act.dma_start(F.w1, aw.rearrange("e d h -> d e h")).then_inc(F.w_loaded, 16)
                act.dma_start(w2[:, :, :, :], aw2).then_inc(F.w_loaded, 16)
                act.dma_start(b1s[:, n - 1, :], a["b1s"][n - 1]).then_inc(F.w_loaded, 16)
                act.dma_start(b2s[:, n - 1, :], a["b2s"][n - 1]).then_inc(F.w_loaded, 32)
            act.dma_start(K.w3qkv[:, :, :], a["w3qkv"]).then_inc(K.w3_loaded, 48)
            act.dma_start(K.wu[:, :, :], a["wu"]).then_inc(K.w3_loaded, 16)
            act.dma_start(K.wint[:, :].bitcast(I32), a["wint"]).then_inc(K.int_loaded, 48)
            setup_act(nc, act, K)
            lin_act(nc, act, K)
            for lay in range(3):
                attn_act(nc, act, K, lay)
                ffn_act(nc, act, K, lay)
            attn3_act(nc, act, K)
            ffn_act(nc, act, K, 3)

        @block.vector
        def _(dve):
            setup_dve(nc, dve, K)
            lin_dve(nc, dve, K)
            for lay in range(3):
                if lay == 2:
                    before_layer2(nc, dve, K)
                attn_dve(nc, dve, K, lay)
                ffn_dve(nc, dve, K, lay)
            before_layer3(nc, dve, K)
            attn3_dve(nc, dve, K)
            ffn_dve(nc, dve, K, 3)

        @block.tensor
        def _(pe):
            lin_pe(nc, pe, K)
            for lay in range(3):
                if lay == 2:
                    pe.wait_ge(K.prow2_ready, 1)
                attn_pe(nc, pe, K, lay)
                ffn_pe(nc, pe, K, lay)
            attn3_pe(nc, pe, K)
            ffn_pe(nc, pe, K, 3)

        @block.gpsimd
        def _(pool):
            for lay in range(3):
                attn_pool(nc, pool, K, lay)
            attn3_pool(nc, pool, K)


INPUTS = ["x", "ctxT", "lin_w", "attn_w", "gates", "w0_1", "w0_2", "w0_3", "w1_1", "w1_2", "w2_1", "w2_2", "b1s", "b2s",
          "w3qkv", "wu", "wint", "rows", "cols", "consts", "mcol", "mrow", "amf"]


def constants(np):
    p, c = np.arange(128)[:, None], np.arange(128)[None, :]
    r16 = np.arange(16)[None, :]
    parts = {
        "ident": p == c, "blockmask": p // HD == c // HD, "headmask": p // HD == r16,
        "hmask": p % 32 // HD == np.arange(G)[None, :], "desc": np.zeros((128, 1)) + (E - np.arange(E)[None, :]),
        "selc": (p % H == r16) & (p < 3 * H), "causal": (c > p) * NEG, "causalT": (p > c) * NEG, "row0": (p == 0) & (c >= 0),
    }
    return np.concatenate([np.asarray(parts[n], np.float32) for n, _ in CONSTS], axis=1)


def lay_out(np, v):
    f = {n: np.ascontiguousarray(a) for n, a in v.items()}
    d = {"x": f["x"].transpose(1, 0, 2), "ctxT": f["ctx_1024"].transpose(0, 2, 1)}
    d["lin_w"] = np.stack([f[f"L0_xattn_W{n}"] for n in "qkv"], 1)
    kv = f["L1_xattn_Wkv"]
    d["attn_w"] = np.stack([
        np.stack([f["L0_ffn_wq"], f["L0_ffn_wk"], f["L0_ffn_wv"], f["L0_ffn_wo"]], 1),
        np.stack([f["L1_xattn_Wq"], kv[:, :D], kv[:, D:], f["L1_xattn_Wp"]], 1),
        np.stack([f[f"L2_xattn_W{n}"].T for n in ("q", "k", "v", "out")], 1)])
    d["gates"] = np.stack([f["L0_ffn_gate_w"], f["L1_ffn_w_gate"], f["L2_ffn_Wr"]], 1)
    d["w0_1"], d["w0_2"], d["w0_3"] = f["L0_ffn_w1"], f["L0_ffn_w2"], f["L0_ffn_w3"]
    d["w1_1"], d["w1_2"], d["w2_1"], d["w2_2"] = f["L1_ffn_W1"], f["L1_ffn_W2"], f["L2_ffn_W1"], f["L2_ffn_W2"]
    for n in ("w0_3", "w1_2", "w2_2"):
        d[n] = d[n].reshape(E, -1, 128, D).transpose(2, 0, 1, 3)
    d["b1s"] = np.stack([f[f"L{n}_ffn_b1"].reshape(E * 4, 128).T for n in (1, 2)])
    d["b2s"] = np.stack([f[f"L{n}_ffn_b2"] for n in (1, 2)])
    d["w3qkv"] = np.stack([f[f"L3_xattn_W{n}"].T for n in "qkv"], 1)
    d["wu"] = f["L3_xattn_Wu"].T.reshape(8, 128, D).transpose(1, 0, 2)
    down = f["L3_ffn_w_down"].T.reshape(3, 128, D).transpose(1, 0, 2).reshape(128, 3 * D)
    d["wint"] = np.concatenate([f["L3_ffn_w_gate"].T, f["L3_ffn_w_up"].T, down], 1)
    bkv = f["L1_xattn_bkv"]
    rows = {"bq0": "L0_xattn_bq", "bk0": "L0_xattn_bk", "bv0": "L0_xattn_bv", "scale0": "L0_xattn_scale", "bo": "L0_ffn_bo",
            "bp1": "L1_xattn_bp", "bv2": "L2_xattn_bv", "bout2": "L2_xattn_bout", "bu3": "L3_xattn_bu",
            "bg1": "L1_ffn_b_gate", "br2": "L2_ffn_br"}
    d["rows"] = np.concatenate([bkv[D:] if n == "bv1" else f[rows[n]].reshape(-1) for n, _ in ROWS])
    twice = lambda n: np.concatenate([f[n], f[n]])
    d["cols"] = np.stack([f["L0_ffn_ln1_scale"], f["L0_ffn_ln1_shift"], f["L0_ffn_ln2_scale"], f["L0_ffn_ln2_shift"],
                          f["L1_xattn_bq"], bkv[:D], f["L2_xattn_bq"], f["L2_xattn_bk"], twice("L3_xattn_qn_w"),
                          twice("L3_xattn_qn_b"), twice("L3_xattn_kn_w"), twice("L3_xattn_kn_b")], 1)
    d["consts"] = constants(np)
    m1, m2 = (f[n].view(np.uint8) for n in ("mask_BxS2_bf1", "mask_BxS2_bf0"))
    d["mcol"] = np.ascontiguousarray(np.stack([m1.T, m2.T], 1)).view(np.int32)
    d["mrow"] = np.stack([m1.reshape(-1), m2.reshape(-1)])[None].view(np.int32)
    d["amf"] = np.stack([f["mask_SxS2_ff0"], f["mask_SxS2_ff0"].T], 1)
    return {n: np.ascontiguousarray(d[n]) for n in INPUTS}


def kernel(**inputs):
    import numpy as np
    import concourse.bacc as bacc
    from concourse.bass_utils import run_bass_kernel_spmd

    nc = bacc.Bacc("TRN2", target_bir_lowering=False, num_devices=1)
    arrays = lay_out(np, inputs)
    a = {n: nc.dram_tensor(f"in_{n}", v.shape, mybir.dt.from_np(v.dtype), kind="ExternalInput").ap()
         for n, v in arrays.items()}
    out = nc.dram_tensor("out_x", (B, T, D), F32, kind="ExternalOutput").ap()
    build(nc, a, out)
    r = run_bass_kernel_spmd(nc, [{f"in_{n}": v for n, v in arrays.items()}], core_ids=[0])
    return r.results[0]["out_x"]
```

```python
from contextlib import ExitStack

import concourse.bass as bass
from concourse import mybir

F32 = mybir.dt.float32
BF16 = mybir.dt.bfloat16
I32 = mybir.dt.int32
U8 = mybir.dt.uint8
ALU = mybir.AluOpType
ACT = mybir.ActivationFunctionType
AX = mybir.AxisListType

B, T, D = 16, 128, 128
H, HD = 16, 8
G = 4
NG = H // G
HD3 = 64
E = 8
GB = 4
NT = GB * T
LN_EXP = "natural_log_exp_and_others"
NEG = -1.5 * 2.0 ** 127
EPS = 1e-5

COLS = ["ln1_s", "ln1_b", "ln2_s", "ln2_b", "qn_w", "qn_b", "kn_w", "kn_b"]
ROWS = [("bq0", D), ("bk0", D), ("bv0", D), ("scale0", D), ("bo", D), ("bq1", D), ("bk1", D), ("bv1", D), ("bp1", D),
        ("bq2", D), ("bk2", D), ("bv2", D),
        ("bout2", D), ("bu3", D), ("bg1", E), ("br2", E)]
ROW_AT = {}
_at = 0
for _n, _w in ROWS:
    ROW_AT[_n] = (_at, _w)
    _at += _w
NROW = _at
NCOL = len(COLS)


NGR = B // GB
FFN_COUNTS = {n: [NGR] * 4 for n in ("var_ready", "rstd_step", "rstd_ready", "stat_step", "xn_ready", "xT_ready", "xT_done")}
FFN_COUNTS.update({n: [NGR] * 3 + [0] for n in ("l_ready", "d_ready", "e_ready", "w_ready")})
FFN_COUNTS.update({n: [0, NGR, NGR, 0] for n in ("wT_ready", "wT_done")})
FFN_COUNTS.update({n: [NGR * 16, 0, 0, NGR * 3] for n in ("a_ready", "b_ready", "silu_done")})
FFN_COUNTS.update({"h_ready": [0, NGR * 32, NGR * 32, 0], "h_done": [NGR * 16, NGR * 32, NGR * 32, NGR * 3],
                   "gate_step": [NGR * 17, NGR * 8, NGR * 8, 0]})
FFN_COUNTS.update({n: [NGR * 8, NGR * 9, NGR * 9, NGR] for n in ("y_ready", "acc_done")})


class Names:
    pass


class From:

    def __init__(self, sem, base):
        self.sem, self.base = sem, base


def wait(eng, sem, value):
    if isinstance(sem, From):
        sem, value = sem.sem, value + sem.base
    if not (isinstance(value, int) and value <= 0):
        eng.wait_ge(sem, value)


class Chain:

    def __init__(self, eng, sem, k, per):
        self.eng, self.sem, self.base, self.per, self.n = eng, sem, k * per, per, 0
        if isinstance(sem, From):
            self.sem, self.base = sem.sem, k * per + sem.base

    def link(self, ins):
        self.n += 1
        ins.then_inc(self.sem, 1)
        self.eng.wait_ge(self.sem, self.base + self.n)

    def done(self):
        assert self.n == self.per, (self.n, self.per)


class Step:

    def __init__(self, i, c):
        self.i, self.c = i, c
        self.n, self.par, self.half = i * 2 + c, c % 2, i + c // 2

    def __add__(self, d):
        return Step(self.i, self.c + d)

    def static(self):
        return isinstance(self.i, int)

    def exists(self, count=B):
        return not self.static() or 0 <= self.c < count

    def within(self, count=B):
        return min(max(self.c, 0), count) if self.static() else self.n


def pipeline(eng, body, before, after):
    first = 2
    pairs = (B - before - first) // 2
    for c in range(-before, first):
        body(Step(0, c))
    with eng.Fori(0, pairs) as i:
        body(Step(i, first))
        body(Step(i, first + 1))
    for c in range(first + 2 * pairs, B + after):
        body(Step(0, c))


def batch(t, n):
    return t[:, n, :] if isinstance(n, int) else t[:, bass.ds(n, 1), :].rearrange("p a d -> p (a d)")



def unit_head(u, a):
    return 2 * (4 * (u // 2) + a) + u % 2


def unit_max(K, u):
    return K.m[:, :].rearrange("p (j a b) -> p j a b", j=2, a=4)[:, u // 2, :, u % 2]


def attn_pe(nc, pe, K, lay):
    W, Wo = K.wsmall[lay], K.wsmall[lay][:, 3, :]
    k0 = B * lay

    def transpose_x(s):
        k = s.n + k0
        wait(pe, K.xn_ready, k + 1)
        wait(pe, K.kt_done, k)
        wait(pe, K.oT_done, k0 + (s + -2).within())
        nc.tensor.transpose(K.pT[:, 0:T], K.xn[:, :], K.ident[:, :]).then_inc(K.xT_ready, 1)

    def project(s):
        k = s.n + k0
        wait(pe, K.xT_done, k + 1)
        wait(pe, K.qt_done, k)
        x = K.xT[:, s.par, :]
        if lay == 0:
            mm = nc.tensor.matmul(K.pP[:, 0:3 * D], x, W[:, 0:3, :].rearrange("p a d -> p (a d)"), start=True, stop=True)
        else:
            pe.wait_ge(K.ctx_loaded[s.par], 16 * (s.half + 1 + (B // 2) * lay))
            nc.tensor.matmul(K.pP[:, 0:D], x, W[:, 0, :], start=True, stop=True)
            mm = nc.tensor.matmul(K.pP[:, D:3 * D], K.ctx[:, s.par, :], W[:, 1:3, :].rearrange("p a d -> p (a d)"),
                                  start=True, stop=True)
        mm.then_inc(K.qkv_ready, 1)

    def transpose_q(s):
        wait(pe, K.qs_ready, s.n + k0 + 1)
        for j in range(H // 2):
            mm = nc.tensor.transpose(K.pPb[:, j * T:(j + 1) * T], K.qs[:, j * 128:(j + 1) * 128], K.identb[:, :])
        mm.then_inc(K.qt_ready, 1)

    def transpose_k(s):
        wait(pe, K.ks_ready, s.n + k0 + 1)
        for j in range(H // 2):
            mm = nc.tensor.transpose(K.pTb[:, j * T:(j + 1) * T], K.ks[:, j * 128:(j + 1) * 128], K.identb[:, :])
        mm.then_inc(K.kt_ready, 1)

    def mask(bank, causal, parts):
        masks = [causal[:, :]] if lay == 0 else [parts[:, part, :] for part in range(3)]
        for n, m in enumerate(masks):
            nc.tensor.matmul(bank[:, :], K.identb[:, :], m.unsqueeze(1).to_broadcast([T, G, T]), start=(n == 0),
                             stop=False, skip_group_check=True)

    def row_scores(s, u):
        k = s.n + k0
        if u == 0:
            wait(pe, K.qt_done, k + 1)
            wait(pe, K.kt_done, k + 1)
        wait(pe, K.smax_done, 4 * k + u - 1)
        bank, r = K.pS[u % 2], slice(64 * (u % 2), 64 * (u % 2) + 64)
        if lay != 1:
            mask(bank, K.causal, K.amask)
        for a in range(G):
            j = G * (u // 2) + a
            mm = nc.tensor.matmul(bank[:, a * T:(a + 1) * T], K.qt[r, s.par, j, :], K.kt[r, s.par, j, :],
                                  start=(lay == 1 and a == 0), stop=(a == G - 1), skip_group_check=True)
        mm.then_inc(K.s_ready, 1)

    def transpose_max(s):
        k = s.n + k0
        wait(pe, K.m3_ready, k + 1)
        wait(pe, K.mT_done, k)
        wait(pe, K.y_done, k0 + (s + -1).within())
        nc.tensor.transpose(K.pMb[:, 0:T], K.m3[:, :], K.identb[:, :]).then_inc(K.mT_ready, 1)

    def col_scores(s, u):
        k = s.n + k0
        wait(pe, K.exp_done, 4 * k + u - 1)
        bank, r = K.pC[u % 2], slice(64 * (u % 2), 64 * (u % 2) + 64)
        if lay != 1:
            mask(bank, K.causalT, K.amaskT)
        for a in range(G):
            j = G * (u // 2) + a
            nc.tensor.matmul(bank[:, a * T:(a + 1) * T], K.kt[r, s.par, j, :], K.qt[r, s.par, j, :],
                             start=(lay == 1 and a == 0), stop=False, skip_group_check=True)
        if u == 0:
            wait(pe, K.mT_done, k + 1)
        for a in range(G):
            mm = nc.tensor.matmul(bank[:, a * T:(a + 1) * T], K.sel[:, unit_head(u, a), :], K.mT[:, :],
                                  start=False, stop=(a == G - 1), skip_group_check=True)
        mm.then_inc(K.c_ready, 1)

    def probs_v(s, u):
        k = s.n + k0
        if u == 0:
            wait(pe, K.v_done, k + 1)
            wait(pe, K.on_ready, k)
        wait(pe, K.exp_done, 4 * k + u + 1)
        for a in range(G):
            h = unit_head(u, a)
            mm = nc.tensor.matmul(K.pO[:, h * (HD + 1):(h + 1) * (HD + 1)], K.pt[:, u % 2, a * T:(a + 1) * T],
                                  K.vaug[:, s.par, h, :], start=True, stop=True)
        mm.then_inc(K.pv_done, 1)

    def transpose_o(s):
        k = s.n + k0
        wait(pe, K.on_ready, k + 1)
        wait(pe, K.kt_done, k0 + (s + 3).within())
        nc.tensor.transpose(K.pT[:, 0:T], K.on[:, :], K.ident[:, :]).then_inc(K.oT_ready, 1)

    def out_project(s):
        k = s.n + k0
        wait(pe, K.oT_done, k + 1)
        wait(pe, K.mT_done, k0 + (s + 2).within())
        wait(pe, K.y_done, k)
        nc.tensor.matmul(K.pM[:, 0:D], K.oT[:, :], Wo, start=True, stop=True).then_inc(K.y_ready, 1)

    pe.wait_ge(K.attn_w_loaded[lay], 64)

    def body(s):
        a, nx, pr = s + 1, s + 2, s + -1
        for u in range(4):
            if s.exists():
                col_scores(s, u)
            if a.exists():
                row_scores(a, u)
            if u == 0:
                if pr.exists():
                    transpose_o(pr)
                if nx.exists():
                    transpose_x(nx)
            if u == 1:
                if pr.exists():
                    out_project(pr)
                if nx.exists():
                    project(nx)
            if u >= 1 and s.exists():
                probs_v(s, u - 1)
        if nx.exists():
            transpose_q(nx)
            transpose_k(nx)
        if s.exists():
            probs_v(s, 3)
        if a.exists():
            transpose_max(a)

    pipeline(pe, body, 3, 1)


def attn_act(nc, act, K, lay):
    k0 = B * lay

    def rstd(s):
        k = s.n + k0
        wait(act, K.var_ready, k + 1)
        c = Chain(act, K.rstd_step, k, 1)
        c.link(nc.scalar.activation(K.lnv[:, 0:1], K.mv[:, s.par, 1:2], ACT.Ln, bias=K.eps[:, :]))
        c.done()
        nc.scalar.activation(K.rs[:, s.par, 0:1], K.lnv[:, 0:1], ACT.Exp, scale=-0.5).then_inc(K.rstd_ready, 1)
        if lay == 0:
            wait(act, K.var2_ready, s.n + 1)
            c = Chain(act, K.rstd2_step, s.n, 1)
            c.link(nc.scalar.activation(K.lnv[:, 1:2], K.var2[:, :], ACT.Ln, bias=K.eps[:, :]))
            nc.scalar.activation(K.rs[:, s.par, 1:2], K.lnv[:, 1:2], ACT.Exp, scale=-0.5).then_inc(K.rstd2_ready, 1)

    def keep_xT(s):
        wait(act, K.xT_ready, s.n + k0 + 1)
        if lay == 0:
            op = nc.scalar.activation(K.xT[:, s.par, :], K.pT[:, 0:T], ACT.Identity, scale=K.col("ln1_s"),
                                      bias=K.col("ln1_b"))
        else:
            op = nc.scalar.copy(K.xT[:, s.par, :], K.pT[:, 0:T])
        op.then_inc(K.xT_done, 1)

    def keep_qT(s):
        wait(act, K.qt_ready, s.n + k0 + 1)
        nc.scalar.copy(K.qt[:, s.par, :, :].rearrange("p j q -> p (j q)"), K.pPb[:, 0:8 * T]).then_inc(K.qt_done, 1)

    def keep_mT(s):
        wait(act, K.mT_ready, s.n + k0 + 1)
        nc.scalar.copy(K.mT[:, :], K.pMb[:, 0:T]).then_inc(K.mT_done, 1)

    def exp(s, u):
        k = s.n + k0
        wait(act, K.c_ready, 4 * k + u + 1)
        wait(act, K.pv_done, 4 * k + u - 1)
        nc.scalar.activation(K.pt[:, u % 2, :], K.pC[u % 2][:, :], ACT.Exp).then_inc(K.exp_done, 1)

    def keep_oT(s):
        wait(act, K.oT_ready, s.n + k0 + 1)
        nc.scalar.copy(K.oT[:, :], K.pT[:, 0:T]).then_inc(K.oT_done, 1)

    def body(s):
        a, nx, pr, st = s + 1, s + 2, s + -1, s + 3
        for u in range(4):
            if s.exists():
                exp(s, u)
            if u == 0:
                if pr.exists():
                    keep_oT(pr)
                if nx.exists():
                    keep_xT(nx)
        if nx.exists():
            keep_qT(nx)
        if a.exists():
            keep_mT(a)
        if st.exists():
            rstd(st)

    pipeline(act, body, 3, 1)


def split(c, engine, copy, parts, x, first, second, third):
    heads = x.rearrange("p (h d) -> p h d", h=H)
    c.link(copy(first, heads.unsqueeze(2).to_broadcast([T, H, 3, HD])))
    c.link(engine.tensor_tensor(heads, heads, first[:, :, 0, :], ALU.subtract))
    c.link(copy(second, heads.unsqueeze(2).to_broadcast([T, H, 2, HD])))
    engine.tensor_tensor(third, heads, second[:, :, 0, :], ALU.subtract).then_inc(parts, 1)


def attn_dve(nc, dve, K, lay):
    k0 = B * lay

    def stats(s):
        k = s.n + k0
        c = Chain(dve, K.stat_step, k, 1)
        c.link(nc.vector.bn_stats(K.bn[:, :], batch(K.x, s.n)))
        nc.vector.memset(K.spare[:, :], 0.0)
        nc.vector.bn_aggr(K.mv[:, s.par, :], K.bn[:, :]).then_inc(K.var_ready, 1)
        if lay == 0:
            wait(dve, K.rstd_ready, k + 1)
            c = Chain(dve, K.var2_step, s.n, 1)
            c.link(nc.vector.tensor_tensor(K.var2a[:, :], K.mv[:, s.par, 1:2], K.rs[:, s.par, 0:1], ALU.mult))
            nc.vector.tensor_tensor(K.var2[:, :], K.var2a[:, :], K.rs[:, s.par, 0:1], ALU.mult).then_inc(K.var2_ready, 1)

    def normalise(s):
        k = s.n + k0
        wait(dve, K.rstd_ready, k + 1)
        wait(dve, K.xT_ready, k)
        if lay == 0:
            nc.vector.tensor_scalar(batch(K.x1, s.n), batch(K.x, s.n), K.mv[:, s.par, 0:1], K.rs[:, s.par, 0:1],
                                    ALU.subtract, ALU.mult).then_inc(K.x1_step, 1)
            wait(dve, K.rstd2_ready, s.n + 1)
            dve.wait_ge(K.x1_step, s.n + 1)
            nc.vector.tensor_scalar(K.xn[:, :], batch(K.x1, s.n), K.rs[:, s.par, 1:2], None,
                                    ALU.mult).then_inc(K.xn_ready, 1)
        else:
            nc.vector.tensor_scalar(K.xn[:, :], batch(K.x, s.n), K.mv[:, s.par, 0:1], K.rs[:, s.par, 0:1],
                                    ALU.subtract, ALU.mult).then_inc(K.xn_ready, 1)

    def keep_qkv(s):
        k = s.n + k0
        wait(dve, K.qkv_ready, k + 1)
        wait(dve, K.v_done, k)
        if lay == 0:
            nc.vector.tensor_copy(K.qkv[:, D:3 * D], K.pP[:, D:3 * D]).then_inc(K.kv_done, 1)
            nc.vector.tensor_scalar(K.qkv[:, 0:D], K.pP[:, 0:D], HD ** -0.5, None, ALU.mult).then_inc(K.q_done, 1)
        else:
            nc.vector.tensor_tensor(K.qkv[:, D:3 * D], K.pP[:, D:3 * D], K.row2(f"bk{lay}", f"bv{lay}"),
                                    ALU.add).then_inc(K.kv_done, 1)
            nc.vector.scalar_tensor_tensor(K.qkv[:, 0:D], K.pP[:, 0:D], HD ** -0.5, K.bqs[:, lay - 1, :], ALU.mult,
                                           ALU.add).then_inc(K.q_done, 1)

    def split_q(s):
        k = s.n + k0
        dve.wait_ge(K.q_done, k + 1)
        wait(dve, K.qt_ready, k)
        q = K.qs[:, :].rearrange("p (h b d) -> p h b d", h=H, b=8)
        c = Chain(dve, K.qsplit_step, k, 3)
        split(c, nc.vector, nc.vector.tensor_copy, K.qs_ready, K.qkv[:, 0:D], q[:, :, 3:6, :], q[:, :, 0:2, :], q[:, :, 2, :])
        c.done()

    def keep_kT(s):
        wait(dve, K.kt_ready, s.n + k0 + 1)
        nc.vector.tensor_copy(K.kt[:, s.par, :, :].rearrange("p j q -> p (j q)"), K.pTb[:, 0:8 * T]).then_inc(K.kt_done, 1)

    def row_max(s, u):
        wait(dve, K.s_ready, 4 * (s.n + k0) + u + 1)
        nc.vector.reduce_max(unit_max(K, u), K.pS[u % 2][:, :].rearrange("p (a k) -> p a k", a=G),
                             AX.X).then_inc(K.smax_done, 1)

    def split_max(s):
        k = s.n + k0
        dve.wait_ge(K.smax_done, 4 * k + 4)
        c = Chain(dve, K.split_step, k, 3)
        c.link(nc.vector.tensor_scalar(K.m3[:, 0:H], K.m[:, :], -1.0, None, ALU.mult))
        c.link(nc.vector.scalar_tensor_tensor(K.mr[:, :], K.m[:, :], -1.0, K.m3[:, 0:H], ALU.mult, ALU.subtract))
        c.link(nc.vector.tensor_copy(K.m3[:, H:2 * H], K.mr[:, :]))
        c.done()
        nc.vector.tensor_tensor(K.m3[:, 2 * H:3 * H], K.mr[:, :], K.m3[:, H:2 * H],
                                ALU.subtract).then_inc(K.m3_ready, 1)

    def normalise_o(s):
        k = s.n + k0
        dve.wait_ge(K.pv_done, 4 * k + 4)
        wait(dve, K.oT_ready, k)
        po = K.pO[:, 0:H * (HD + 1)].rearrange("p (h d) -> p h d", h=H)
        c = Chain(dve, K.rec_step, k, 1)
        c.link(nc.vector.reciprocal(K.rec[:, :], po[:, :, HD]))
        nc.vector.tensor_tensor(K.on[:, :].rearrange("p (h d) -> p h d", h=H), po[:, :, 0:HD],
                                K.rec[:, :].unsqueeze(2).to_broadcast([T, H, HD]),
                                ALU.mult).then_inc(K.on_ready, 1)

    def residual(s):
        k = s.n + k0
        wait(dve, K.y_ready, k + 1)
        bias = K.row({0: "bo", 1: "bp1", 2: "bout2"}[lay])
        nc.vector.tensor_tensor(K.yb[:, :], K.pM[:, 0:D], bias, ALU.add).then_inc(K.y_done, 1)
        dve.wait_ge(K.y_done, k + 1)
        if lay == 0:
            c = Chain(dve, K.res_step, s.n, 1)
            c.link(nc.vector.tensor_tensor(batch(K.x1, s.n), batch(K.x1, s.n), K.yb[:, :], ALU.add))
            nc.vector.tensor_tensor(batch(K.x, s.n), batch(K.x, s.n), batch(K.x1, s.n), ALU.add).then_inc(K.x_done, 1)
        else:
            nc.vector.tensor_tensor(batch(K.x, s.n), batch(K.x, s.n), K.yb[:, :], ALU.add).then_inc(K.x_done, 1)

    def body(s):
        a, nx, pr, st = s + 1, s + 2, s + -1, s + 3
        if nx.exists():
            normalise(nx)
        for u in range(4):
            if a.exists():
                row_max(a, u)
            if u == 1 and nx.exists():
                keep_qkv(nx)
                split_q(nx)
            if u == 1 and pr.exists():
                residual(pr)
        if a.exists():
            split_max(a)
        if nx.exists():
            keep_kT(nx)
        if s.exists():
            normalise_o(s)
        if st.exists():
            stats(st)

    dve.wait_ge(K.x_done, K.x_before_attn[lay])
    pipeline(dve, body, 3, 1)


def attn_pool(nc, pool, K, lay):
    k0 = B * lay

    def copy(out, x):
        one = K.one[:, :]
        while len(one.shape) < len(x.shape):
            one = one.unsqueeze(1)
        return nc.gpsimd.tensor_tensor(out, x, one.to_broadcast(list(x.shape)), ALU.mult)

    def body(s):
        nx = s + 2
        if not nx.exists():
            return
        k = nx.n + k0
        wait(pool, K.kv_done, k + 1)
        wait(pool, K.kt_ready, k)
        if lay:
            nc.gpsimd.tensor_copy(K.ks[:, :].rearrange("p (h c) -> p h c", h=H)[:, :, 6 * HD],
                                  batch(K.pcol[lay], nx.n).to_broadcast([T, H]))
        kb = K.ks[:, :].rearrange("p (h b w d) -> p h b w d", h=H, b=4, w=2)
        c = Chain(pool, K.ksplit_step, k, 3)
        split(c, nc.gpsimd, copy, K.ks_ready, K.qkv[:, D:2 * D], kb[:, :, 0:3, 0, :], kb[:, :, 0:2, 1, :], kb[:, :, 2, 1, :])
        wait(pool, K.pv_done, 4 * (k - 1))
        copy(K.vaug[:, nx.par, :, 0:HD], K.qkv[:, 2 * D:3 * D].rearrange("p (h d) -> p h d", h=H)).then_inc(K.v_done, 1)

    pipeline(pool, body, 3, 1)



def lin_pe(nc, pe, K):
    def transpose_x(s):
        wait(pe, K.lin_xn_ready, s.n + 1)
        wait(pe, K.lin_xT_done, s.n)
        nc.tensor.transpose(K.pT[:, 0:T], K.xn[:, :], K.ident[:, :]).then_inc(K.lin_xT_ready, 1)

    def project(s):
        wait(pe, K.lin_xT_done, s.n + 1)
        pe.wait_ge(K.ctx_loaded[s.par], 16 * (s.half + 1))
        wait(pe, K.lin_p_done, s.n)
        c = K.ctx[:, s.par, :]
        nc.tensor.matmul(K.pP[:, 0:D], K.xT[:, s.par, :], K.lin_w[:, 0, :], start=True, stop=True)
        nc.tensor.matmul(K.pP[:, D:2 * D], c, K.lin_w[:, 1, :], start=True, stop=True)
        nc.tensor.matmul(K.pP[:, 2 * D:3 * D], c, K.lin_w[:, 2, :], start=True, stop=True).then_inc(K.lin_p_ready, 1)

    def kv(s):
        wait(pe, K.lin_f_ready, s.n + 1)
        wait(pe, K.lin_qT_done, s.n)
        nc.tensor.transpose(K.pC[0][:, 0:T], K.feat[:, s.par, 0, :], K.ident[:, :]).then_inc(K.lin_qT_ready, 1)
        wait(pe, K.lin_kv_done, s.n)
        nc.tensor.matmul(K.pM[:, 0:D + 1], K.feat[:, s.par, 1, :], K.linv[:, s.par, :], start=True,
                         stop=True).then_inc(K.lin_kv_ready, 1)

    def out(s):
        wait(pe, K.lin_qT_done, s.n + 1)
        wait(pe, K.lin_kv_done, s.n + 1)
        wait(pe, K.lin_o_done, s.n)
        nc.tensor.matmul(K.pO[:, 0:D + H], K.lqT[:, :], K.kvblk[:, :], start=True, stop=True).then_inc(K.lin_o_ready, 1)

    pe.wait_ge(K.lin_w_loaded, 48)
    pe.wait_ge(K.consts_loaded, 16)

    def body(s):
        nx = s + 2
        if s.exists():
            kv(s)
        if nx.exists():
            transpose_x(nx)
        if s.exists():
            out(s)
        if nx.exists():
            project(nx)

    pipeline(pe, body, 3, 0)


def lin_act(nc, act, K):
    def rstd(s):
        wait(act, K.lin_var_ready, s.n + 1)
        c = Chain(act, K.lin_rstd_step, s.n, 1)
        c.link(nc.scalar.activation(K.lnv[:, 0:1], K.mv[:, s.par, 1:2], ACT.Ln, bias=K.eps[:, :]))
        nc.scalar.activation(K.rs[:, s.par, 0:1], K.lnv[:, 0:1], ACT.Exp, scale=-0.5).then_inc(K.lin_rstd_ready, 1)

    def keep_xT(s):
        wait(act, K.lin_xT_ready, s.n + 1)
        nc.scalar.copy(K.xT[:, s.par, :], K.pT[:, 0:T]).then_inc(K.lin_xT_done, 1)

    def keep_qT(s):
        wait(act, K.lin_qT_ready, s.n + 1)
        nc.scalar.copy(K.lqT[:, :], K.pC[0][:, 0:T]).then_inc(K.lin_qT_done, 1)

    def ratio(s):
        wait(act, K.lin_ratio_ready, s.n + 1)
        c = Chain(act, K.lin_root_step, s.n, 1)
        c.link(nc.scalar.activation(K.lnr[:, :], K.fr[:, :], ACT.Ln))
        nc.scalar.activation(K.froot[:, :], K.lnr[:, :], ACT.Exp, scale=0.5).then_inc(K.lin_root_ready, 1)

    def body(s):
        a, nx, st = s + 1, s + 2, s + 3
        if s.exists():
            keep_qT(s)
        if nx.exists():
            keep_xT(nx)
        if a.exists():
            ratio(a)
        if st.exists():
            rstd(st)

    pipeline(act, body, 3, 0)


def lin_dve(nc, dve, K):
    def stats(s):
        c = Chain(dve, K.lin_stat_step, s.n, 1)
        c.link(nc.vector.bn_stats(K.bn[:, :], batch(K.x, s.n)))
        nc.vector.memset(K.spare[:, :], 0.0)
        nc.vector.bn_aggr(K.mv[:, s.par, :], K.bn[:, :]).then_inc(K.lin_var_ready, 1)

    def normalise(s):
        wait(dve, K.lin_rstd_ready, s.n + 1)
        wait(dve, K.lin_xT_ready, s.n)
        nc.vector.tensor_scalar(K.xn[:, :], batch(K.x, s.n), K.mv[:, s.par, 0:1], K.rs[:, s.par, 0:1],
                                ALU.subtract, ALU.mult).then_inc(K.lin_xn_ready, 1)

    def features(s):
        wait(dve, K.lin_p_ready, s.n + 1)
        qk = K.pP[:, 0:2 * D].rearrange("p (a d) -> p a d", a=2)
        c = Chain(dve, K.lin_f_step, s.n, 12)
        two = [T, 2, D]
        c.link(nc.vector.tensor_tensor(K.ft[:, :, :], qk, K.row2("bq0", "bk0").rearrange("p (a d) -> p a d", a=2), ALU.add))
        nc.vector.tensor_tensor(K.linv[:, s.par, 0:D], K.pP[:, 2 * D:3 * D], K.row("bv0"), ALU.add).then_inc(K.lin_p_done, 1)
        c.link(nc.vector.tensor_scalar(K.ft[:, :, :], K.ft[:, :, :], 0.0, 1e-6, ALU.max, ALU.add))
        c.link(nc.vector.tensor_tensor(K.ft[:, :, :], K.ft[:, :, :], K.isp[:, :].unsqueeze(1).to_broadcast(two), ALU.mult))
        c.link(nc.vector.reduce_max(K.fm[:, :], K.ft[:, :, :], AX.X))
        c.link(nc.vector.reciprocal(K.fr[:, :], K.fm[:, :]))
        c.link(nc.vector.tensor_tensor(K.ft[:, :, :], K.ft[:, :, :], K.fr[:, :].unsqueeze(2).to_broadcast(two), ALU.mult))
        c.link(nc.vector.tensor_tensor(K.f2[:, :, :], K.ft[:, :, :], K.ft[:, :, :], ALU.mult))
        c.link(nc.vector.tensor_tensor(K.f3[:, :, :], K.f2[:, :, :], K.ft[:, :, :], ALU.mult))
        nc.vector.reduce_sum(K.fs[:, 0:2], K.f2[:, :, :], AX.X)
        c.link(nc.vector.tensor_tensor(K.ft[:, :, :], K.f3[:, :, :], K.f3[:, :, :], ALU.mult))
        c.link(nc.vector.reduce_sum(K.fs[:, 2:4], K.ft[:, :, :], AX.X))
        c.link(nc.vector.reciprocal(K.fs[:, 2:4], K.fs[:, 2:4]))
        nc.vector.tensor_tensor(K.fr[:, :], K.fs[:, 0:2], K.fs[:, 2:4], ALU.mult).then_inc(K.lin_ratio_ready, 1)
        wait(dve, K.lin_root_ready, s.n + 1)
        c.link(nc.vector.tensor_tensor(K.fr[:, :], K.froot[:, :], K.fm[:, :], ALU.mult))
        nc.vector.tensor_tensor(K.feat[:, s.par, :, :], K.f3[:, :, :], K.fr[:, :].unsqueeze(2).to_broadcast(two),
                                ALU.mult).then_inc(K.lin_f_ready, 1)
        c.done()

    def within_heads(s):
        wait(dve, K.lin_kv_ready, s.n + 1)
        nc.vector.tensor_tensor(K.kvblk[:, 0:D], K.pM[:, 0:D], K.blockmask[:, :], ALU.mult)
        nc.vector.tensor_scalar(K.kvblk[:, D:D + H], K.headmask[:, :], K.pM[:, D:D + 1], None,
                                ALU.mult).then_inc(K.lin_kv_done, 1)

    def residual(s):
        wait(dve, K.lin_o_ready, s.n + 1)
        c = Chain(dve, K.lin_o_step, s.n, 2)
        c.link(nc.vector.tensor_scalar(K.rec[:, :], K.pO[:, D:D + H], 1e-6, None, ALU.add))
        c.link(nc.vector.reciprocal(K.rec[:, :], K.rec[:, :]))
        nc.vector.tensor_tensor(K.yb[:, :].rearrange("p (h d) -> p h d", h=H),
                                K.pO[:, 0:D].rearrange("p (h d) -> p h d", h=H),
                                K.rec[:, :].unsqueeze(2).to_broadcast([T, H, HD]), ALU.mult).then_inc(K.lin_o_done, 1)
        dve.wait_ge(K.lin_o_done, s.n + 1)
        nc.vector.tensor_tensor(batch(K.x, s.n), batch(K.x, s.n), K.yb[:, :], ALU.add).then_inc(K.x_done, 1)

    dve.wait_ge(K.x_loaded, 16)

    def body(s):
        a, nx, st = s + 1, s + 2, s + 3
        if s.exists():
            within_heads(s)
        if nx.exists():
            normalise(nx)
        if a.exists():
            features(a)
        if s.exists():
            residual(s)
        if st.exists():
            stats(st)

    pipeline(dve, body, 3, 0)



def groups(eng, body):
    body(0, True)
    with eng.Fori(1, B // GB - 1) as g:
        body(g, True)
    body(B // GB - 1, False)


def ffn_pe(nc, pe, K, kind):
    F = K.ffn[kind]
    NE, HB = F.experts, F.blocks

    def transpose_x(g):
        wait(pe, F.xn_ready, g + 1)
        wait(pe, F.xT_done, g)
        for b in range(GB):
            mm = nc.tensor.transpose(K.pT[:, b * T:(b + 1) * T], K.xg[:, b, :], K.ident[:, :])
        mm.then_inc(F.xT_ready.sem, 1)

    def logits(g):
        wait(pe, F.xT_done, g + 1)
        if NE == 1:
            return
        wait(pe, F.w_ready, g)
        if kind:
            wait(pe, F.wT_done, g)
        for b in range(GB):
            mm = nc.tensor.matmul(K.pP[:, b * E:(b + 1) * E], K.xTg[:, b * T:(b + 1) * T], F.gate, start=True, stop=True)
        mm.then_inc(F.l_ready.sem, 1)

    def hidden(g, e):
        for hb in range(HB):
            v = e * HB + hb
            if kind in (1, 2):
                wait(pe, F.h_done, g * (NE * HB) + max(v - 3, 0))
                nc.tensor.matmul(K.pH[v % 4][:, :], F.w1[:, e, hb * T:(hb + 1) * T], K.xTg[:, :], start=True,
                                 stop=True).then_inc(F.h_ready.sem, 1)
            else:
                for q, w, free in ((0, F.w1, F.silu_done), (1, F.w2, F.h_done)):
                    wait(pe, free, g * (NE * HB) + max(v - 1, 0))
                    mm = nc.tensor.matmul(K.pH[2 * (v % 2) + q][:, :], w[:, e, hb * T:(hb + 1) * T], K.xTg[:, :],
                                          start=True, stop=True)
                    mm.then_inc((F.a_ready, F.b_ready)[q].sem, 1)

    def weights_T(g):
        wait(pe, F.w_ready, g + 1)
        for b in range(GB):
            mm = nc.tensor.transpose(K.pP[0:E, b * T:(b + 1) * T], K.wts[:, b, :], K.ident[:, :])
        mm.then_inc(F.wT_ready.sem, 1)

    def down(g, e):
        wait(pe, F.h_done, g * (NE * HB) + (e + 1) * HB)
        wait(pe, F.acc_done, g * F.ys + max(e - 1, 0))
        bank = K.pY[e % 2]
        for b in range(GB):
            for hb in range(HB):
                mm = nc.tensor.matmul(bank[:, b * T:(b + 1) * T], K.hT[:, e % 2, hb, b * T:(b + 1) * T],
                                      F.w3[:, e, hb, :], start=(hb == 0), stop=(hb == HB - 1))
        mm.then_inc(F.y_ready.sem, 1)

    def down_bias(g):
        wait(pe, F.wT_done, g + 1)
        wait(pe, F.acc_done, g * F.ys + NE - 1)
        for b in range(GB):
            mm = nc.tensor.matmul(K.pY[0][:, b * T:(b + 1) * T], K.wT[:, b * T:(b + 1) * T], F.b2, start=True, stop=True)
        mm.then_inc(F.y_ready.sem, 1)

    for sem, count in F.loaded:
        pe.wait_ge(sem, count)
    transpose_x(0)
    logits(0)

    def body(g, more):
        hidden(g, 0)
        for e in range(NE):
            if e + 1 < NE:
                hidden(g, e + 1)
            if e == 0 and kind in (1, 2):
                weights_T(g)
            if e == NE - 1 and more:
                transpose_x(g + 1)
            down(g, e)
        if kind in (1, 2):
            down_bias(g)
        if more:
            logits(g + 1)

    groups(pe, body)


def ffn_act(nc, act, K, kind):
    F = K.ffn[kind]
    NE, HB = F.experts, F.blocks

    def rstd(g):
        wait(act, F.var_ready, g + 1)
        c = Chain(act, F.rstd_step, g, 1)
        c.link(nc.scalar.activation(K.lng[:, :], K.mvg[:, :, 1], ACT.Ln, bias=K.eps[:, :]))
        nc.scalar.activation(K.rsg[:, :], K.lng[:, :], ACT.Exp, scale=-0.5).then_inc(F.rstd_ready.sem, 1)

    def keep_xT(g):
        wait(act, F.xT_ready, g + 1)
        if kind == 0:
            op = nc.scalar.activation(K.xTg[:, :], K.pT[:, :], ACT.Identity, scale=K.col("ln2_s"), bias=K.col("ln2_b"))
        else:
            op = nc.scalar.copy(K.xTg[:, :], K.pT[:, :])
        op.then_inc(F.xT_done.sem, 1)

    def gate_exp(g):
        wait(act, F.d_ready, g + 1)
        n = GB if kind == 0 else GB * E
        nc.scalar.activation(K.ge[:, 0:n], K.gd[:, 0:n], ACT.Exp).then_inc(F.e_ready.sem, 1)

    def keep_wT(g):
        wait(act, F.wT_ready, g + 1)
        nc.scalar.copy(K.wT[:, :], K.pP[0:E, :]).then_inc(F.wT_done.sem, 1)

    def hidden(g, e):
        for hb in range(HB):
            v = e * HB + hb
            u = g * (NE * HB) + v
            if kind in (1, 2):
                wait(act, F.h_ready, u + 1)
                if hb == 0:
                    wait(act, F.y_ready, g * F.ys + max(e - 1, 0))
                nc.scalar.activation(K.hT[:, e % 2, hb, :], K.pH[v % 4][:, :], ACT.Relu,
                                     bias=F.b1[:, v:v + 1]).then_inc(F.h_done.sem, 1)
            else:
                wait(act, F.a_ready, u + 1)
                wait(act, F.h_done, g * (NE * HB) + max(v - 1, 0))
                nc.scalar.activation(K.silu[:, v % 2, :], K.pH[2 * (v % 2)][:, :], ACT.Silu,
                                     scale=F.scale).then_inc(F.silu_done.sem, 1)

    act.preload_act_table_set(LN_EXP)
    rstd(0)
    keep_xT(0)

    def body(g, more):
        if NE > 1:
            gate_exp(g)
        for e in range(NE):
            hidden(g, e)
            if e == 1 and kind in (1, 2):
                keep_wT(g)
        if more:
            if kind in (0, 3):
                act.preload_act_table_set(LN_EXP)
            rstd(g + 1)
            keep_xT(g + 1)

    groups(act, body)
    if kind in (0, 3):
        act.preload_act_table_set(LN_EXP)


def ffn_dve(nc, dve, K, kind):
    F = K.ffn[kind]
    NE, HB = F.experts, F.blocks
    src = K.x1 if kind == 0 else K.x
    f4 = [T, GB, E]

    def stats(g):
        c = Chain(dve, F.stat_step, g, 1)
        for b in range(GB):
            op = nc.vector.bn_stats(K.bng[:, b, :], batch(src, g * GB + b))
        c.link(op)
        nc.vector.memset(K.spare[:, :], 0.0)
        for b in range(GB):
            op = nc.vector.bn_aggr(K.mvg[:, b, :], K.bng[:, b, :])
        op.then_inc(F.var_ready.sem, 1)

    def normalise(g):
        wait(dve, F.rstd_ready, g + 1)
        wait(dve, F.xT_ready, g)
        for b in range(GB):
            op = nc.vector.tensor_scalar(K.xg[:, b, :], batch(src, g * GB + b), K.mvg[:, b, 0:1], K.rsg[:, b:b + 1],
                                         ALU.subtract, ALU.mult)
        op.then_inc(F.xn_ready.sem, 1)

    def first_max(c, onehot):
        c.link(nc.vector.reduce_max(K.gm[:, :], K.gl[:, :, :], AX.X))
        c.link(nc.vector.tensor_tensor(onehot, K.gl[:, :, :], K.gm[:, :].unsqueeze(2).to_broadcast(f4), ALU.is_equal))
        c.link(nc.vector.tensor_tensor(onehot, onehot, K.desc[:, :].unsqueeze(1).to_broadcast(f4), ALU.mult))
        c.link(nc.vector.reduce_max(K.gi[:, :], onehot, AX.X))
        c.link(nc.vector.tensor_tensor(onehot, onehot, K.gi[:, :].unsqueeze(2).to_broadcast(f4), ALU.is_equal))

    def gating(g):
        wait(dve, F.l_ready, g + 1)
        pl = K.pP[:, 0:GB * E].rearrange("p (b e) -> p b e", b=GB)
        c = Chain(dve, F.gate_step, g, 17 if kind == 0 else 8)
        if kind == 0:
            c.link(nc.vector.tensor_copy(K.gl[:, :, :], pl))
            first_max(c, K.g1[:, :, :])
            c.link(nc.vector.tensor_copy(K.gm1[:, :], K.gm[:, :]))
            c.link(nc.vector.scalar_tensor_tensor(K.gl[:, :, :], K.g1[:, :, :], NEG, K.gl[:, :, :], ALU.mult, ALU.add))
            first_max(c, K.g2[:, :, :])
            nc.vector.tensor_tensor(K.gd[:, 0:GB], K.gm[:, :], K.gm1[:, :], ALU.subtract).then_inc(F.d_ready.sem, 1)
            wait(dve, F.e_ready, g + 1)
            c.link(nc.vector.tensor_scalar(K.gs[:, :], K.ge[:, 0:GB], 1.0, None, ALU.add))
            c.link(nc.vector.reciprocal(K.gs[:, :], K.gs[:, :]))
            c.link(nc.vector.tensor_tensor(K.g2[:, :, :], K.g2[:, :, :], K.ge[:, 0:GB].unsqueeze(2).to_broadcast(f4), ALU.mult))
            c.link(nc.vector.tensor_tensor(K.g2[:, :, :], K.g2[:, :, :], K.g1[:, :, :], ALU.add))
            nc.vector.tensor_tensor(K.wts[:, :, :], K.g2[:, :, :], K.gs[:, :].unsqueeze(2).to_broadcast(f4),
                                    ALU.mult).then_inc(F.w_ready.sem, 1)
        else:
            bg = K.row({1: "bg1", 2: "br2"}[kind]).unsqueeze(1).to_broadcast(f4)
            c.link(nc.vector.tensor_tensor(K.gl[:, :, :], pl, bg, ALU.add))
            first_max(c, K.g1[:, :, :])
            nc.vector.tensor_tensor(K.gd[:, :].rearrange("p (b e) -> p b e", b=GB), K.gl[:, :, :],
                                    K.gm[:, :].unsqueeze(2).to_broadcast(f4), ALU.subtract).then_inc(F.d_ready.sem, 1)
            wait(dve, F.e_ready, g + 1)
            c.link(nc.vector.reduce_sum(K.gs[:, :], K.ge[:, :].rearrange("p (b e) -> p b e", b=GB), AX.X))
            c.link(nc.vector.reciprocal(K.gs[:, :], K.gs[:, :]))
            nc.vector.tensor_tensor(K.wts[:, :, :], K.g1[:, :, :], K.gs[:, :].unsqueeze(2).to_broadcast(f4),
                                    ALU.mult).then_inc(F.w_ready.sem, 1)
        c.done()
        wait(dve, F.w_ready, g + 1)

    def product(g, e):
        for hb in range(HB):
            v = e * HB + hb
            u = g * (NE * HB) + v
            wait(dve, F.silu_done, u + 1)
            wait(dve, F.b_ready, u + 1)
            if hb == 0:
                wait(dve, F.y_ready, g * F.ys + max(e - 1, 0))
            if F.scale == 1.0:
                op = nc.vector.tensor_tensor(K.hT[:, e % 2, hb, :], K.silu[:, v % 2, :], K.pH[2 * (v % 2) + 1][:, :],
                                             ALU.mult)
            else:
                op = nc.vector.scalar_tensor_tensor(K.hT[:, e % 2, hb, :], K.pH[2 * (v % 2) + 1][:, :], F.scale,
                                                    K.silu[:, v % 2, :], ALU.mult, ALU.mult)
            op.then_inc(F.h_done.sem, 1)

    def add_up(g, e):
        y = g * F.ys + e
        wait(dve, F.y_ready, y + 1)
        wait(dve, F.acc_done, y)
        bank = K.pY[e % 2]
        for b in range(GB):
            xb = batch(K.x, g * GB + b)
            if NE > 1 and e < NE:
                op = nc.vector.scalar_tensor_tensor(xb, bank[:, b * T:(b + 1) * T], K.wts[:, b, e:e + 1], xb,
                                                    ALU.mult, ALU.add)
            else:
                op = nc.vector.tensor_tensor(xb, bank[:, b * T:(b + 1) * T], xb, ALU.add)
        op.then_inc(F.acc_done.sem, 1)

    dve.wait_ge(K.x_done, K.x_before_ffn[kind])
    stats(0)
    normalise(0)

    def body(g, more):
        if NE > 1:
            gating(g)
        for e in range(NE):
            if kind in (0, 3):
                product(g, e)
            if e == max(NE - 2, 0) and more:
                stats(g + 1)
            if e:
                add_up(g, e - 1)
        if more:
            normalise(g + 1)
        add_up(g, NE - 1)
        if kind in (1, 2):
            add_up(g, NE)

    groups(dve, body)
    wait(dve, F.acc_done, (B // GB) * F.ys)
    dve.sem_inc(K.x_done, 1)



class Uses:

    ORDER = [("oT0", -1), ("oT1", -1), ("y", -1), ("xT", 2), ("Q0", 2), ("Q1", 2), ("K0", 2), ("K1", 2), ("m", 1),
             ("V0", 2), ("V1", 2), ("QT0", 2), ("QT1", 2), ("KT0", 2), ("KT1", 2)]

    def __init__(self):
        self.total, self.looped = 0, None

    def of(self, s):
        n = len(self.ORDER)
        if s.static():
            if self.looped is not None:
                self.total, self.looped = self.looped + n * 2 * ((B - 3 - 2) // 2), None
            start = self.total
        else:
            if self.looped is None:
                self.looped = self.total
            base = self.looped + n * (s.c - 2)
            start = s.i * (2 * n) + base
        names = [name for name, d in self.ORDER if (s + d).exists()]
        at = {name: start + j for j, name in enumerate(names)}
        even = self.total if s.static() else base
        self.bank = {name: (even + j) % 2 for j, name in enumerate(names)}
        if s.static():
            self.total += len(names)
        self.at, self.start = at, start
        return at


def attn3_pe(nc, pe, K):
    uses = Uses()

    def free(name):
        wait(pe, K.a_done, uses.at[name] - 1)
        return K.pA[uses.bank[name]]

    def transpose_x(s):
        wait(pe, K.l3_xn_ready, s.n + 1)
        nc.tensor.transpose(free("xT")[:, 0:T], K.xn[:, :], K.ident[:, :]).then_inc(K.a_ready, 1)

    def project(s, which):
        if which == 0:
            wait(pe, K.a_done, uses.at["xT"] + 1)
            pe.wait_ge(K.ctx_loaded[s.par], 16 * (s.half + 1 + (B // 2) * 3))
        src = K.xT[:, s.par, :] if which == 0 else K.ctx[:, s.par, :]
        for half in range(2):
            op = nc.tensor.matmul(free(f"{'QKV'[which]}{half}")[:, :], src,
                                  K.w3qkv[:, which, half * 512:(half + 1) * 512], start=True, stop=True)
            op.then_inc(K.a_ready, 1)

    def transpose_qk(s, which):
        wait(pe, (K.q3n_ready, K.k3n_ready)[which], s.n + 1)
        for half in range(2):
            bank = free(f"{'QK'[which]}T{half}")
            for j in range(4):
                jj = half * 4 + j
                op = nc.tensor.transpose(bank[:, j * T:(j + 1) * T], K.qk3n[:, which, jj * T:(jj + 1) * T], K.ident[:, :])
            op.then_inc(K.a_ready, 1)

    def row_scores(s, u):
        if u == 0:
            wait(pe, K.a_done, uses.start)
        wait(pe, K.s3_done, 4 * s.n + u - 1)
        r = slice(64 * (u % 2), 64 * (u % 2) + 64)
        for a in range(4):
            j = 4 * (u // 2) + a
            op = nc.tensor.matmul(K.pS[u % 2][:, a * T:(a + 1) * T], K.q3T[r, s.par, j, :], K.k3T[r, s.par, j, :],
                                  start=True, stop=True)
        op.then_inc(K.s3_ready, 1)

    def transpose_max(s):
        wait(pe, K.m33_ready, s.n + 1)
        nc.tensor.transpose(free("m")[:, :].bitcast(BF16)[:, 0:T], K.m3[:, :], K.identb[:, :]).then_inc(K.a_ready, 1)

    def col_scores(s, u):
        if u == 0:
            wait(pe, K.a_done, uses.start - (6 if (s + 1).exists() else 0))
        wait(pe, K.exp3_done, 4 * s.n + u - 1)
        r = slice(64 * (u % 2), 64 * (u % 2) + 64)
        bank = K.pC[u % 2]
        for a in range(4):
            j = 4 * (u // 2) + a
            nc.tensor.matmul(bank[:, a * T:(a + 1) * T], K.k3T[r, s.par, j, :], K.q3T[r, s.par, j, :],
                             start=(a == 0), stop=False, skip_group_check=True)
        for a in range(4):
            h = 2 * (4 * (u // 2) + a) + u % 2
            op = nc.tensor.matmul(bank[:, a * T:(a + 1) * T], K.sel[:, h, :], K.mT[:, :], start=False, stop=(a == 3),
                                  skip_group_check=True)
        op.then_inc(K.c3_ready, 1)

    def probs_v(s, u):
        wait(pe, K.exp3_done, 4 * s.n + u + 1)
        wait(pe, K.on3_done, 4 * s.n + u - 1)
        for a in range(4):
            h = 2 * (4 * (u // 2) + a) + u % 2
            op = nc.tensor.matmul(K.pO3[u % 2][:, a * (HD3 + 1):(a + 1) * (HD3 + 1)], K.pt[:, u % 2, a * T:(a + 1) * T],
                                  K.v3[:, s.par, h, :], start=True, stop=True)
        op.then_inc(K.pv3_done, 1)

    def transpose_o(s):
        wait(pe, K.on3_done, 4 * s.n + 4)
        for half in range(2):
            bank = free(f"oT{half}")
            for j in range(4):
                jj = half * 4 + j
                op = nc.tensor.transpose(bank[:, j * T:(j + 1) * T], K.on3[:, jj * T:(jj + 1) * T], K.ident[:, :])
            op.then_inc(K.a_ready, 1)

    def out_project(s):
        wait(pe, K.a_done, uses.at["oT1"] + 1)
        bank = free("y")
        for j in range(8):
            op = nc.tensor.matmul(bank[:, 0:D], K.o3T[:, j, :], K.wu[:, j, :], start=(j == 0), stop=(j == 7))
        op.then_inc(K.a_ready, 1)

    pe.wait_ge(K.w3_loaded, 64)
    pe.wait_ge(K.w3_centred, 2)

    def body(s):
        uses.of(s)
        a, nx, pr = s + 1, s + 2, s + -1
        for u in range(4):
            if s.exists():
                col_scores(s, u)
            if a.exists():
                row_scores(a, u)
            if u == 0 and pr.exists():
                transpose_o(pr)
            if u >= 1 and s.exists():
                probs_v(s, u - 1)
            if u == 1:
                if pr.exists():
                    out_project(pr)
                if nx.exists():
                    transpose_x(nx)
            if u == 2 and nx.exists():
                project(nx, 0)
                project(nx, 1)
        if s.exists():
            probs_v(s, 3)
        if a.exists():
            transpose_max(a)
        if nx.exists():
            project(nx, 2)
            transpose_qk(nx, 0)
            transpose_qk(nx, 1)

    pipeline(pe, body, 3, 1)


def attn3_act(nc, act, K):
    uses = Uses()

    def taken(name):
        wait(act, K.a_ready, uses.at[name] + 1)
        return K.pA[uses.bank[name]]

    def rstd(s):
        wait(act, K.l3_var_ready, s.n + 1)
        c = Chain(act, K.l3_rstd_step, s.n, 1)
        c.link(nc.scalar.activation(K.lnv[:, 0:1], K.mv[:, s.par, 1:2], ACT.Ln, bias=K.eps[:, :]))
        nc.scalar.activation(K.rs[:, s.par, 0:1], K.lnv[:, 0:1], ACT.Exp, scale=-0.5).then_inc(K.l3_rstd_ready, 1)

    def keep_qk(s, which):
        if which == 0:
            wait(act, K.k3n_ready, s.n)
        for half in range(2):
            nc.scalar.copy(K.qk3[:, which, half * 512:(half + 1) * 512],
                           taken(f"{'QK'[which]}{half}")[:, :]).then_inc(K.a_done, 1)

    def keep_v(s):
        for half in range(2):
            nc.scalar.copy(K.v3[:, s.par, half * 8:(half + 1) * 8, 0:HD3],
                           taken(f"V{half}")[:, :].rearrange("p (h d) -> p h d", h=8)).then_inc(K.a_done, 1)

    def head_rstd(s):
        wait(act, K.ss_ready, s.n + 1)
        c = Chain(act, K.l3_hr_step, s.n, 1)
        c.link(nc.scalar.activation(K.lnh[:, :], K.ss[:, :], ACT.Ln, bias=K.eps[:, :], scale=1.0 / HD3))
        nc.scalar.activation(K.rh[:, :], K.lnh[:, :], ACT.Exp, scale=-0.5).then_inc(K.rh_ready, 1)

    def keep_qkT(s, which):
        dst = (K.q3T, K.k3T)[which]
        w, b = ((K.qn8[:, 0:1], K.qn8[:, 1:2]), (K.col("kn_w"), K.col("kn_b")))[which]
        for half in range(2):
            nc.scalar.activation(dst[:, s.par, half * 4:(half + 1) * 4, :].rearrange("p a q -> p (a q)"),
                                 taken(f"{'QK'[which]}T{half}")[:, :], ACT.Identity, scale=w, bias=b).then_inc(K.a_done, 1)

    def exp(s, u):
        wait(act, K.c3_ready, 4 * s.n + u + 1)
        wait(act, K.pv3_done, 4 * s.n + u - 1)
        nc.scalar.activation(K.pt[:, u % 2, :], K.pC[u % 2][:, :], ACT.Exp).then_inc(K.exp3_done, 1)

    def keep_oT(s):
        for half in range(2):
            nc.scalar.copy(K.o3T[:, half * 4:(half + 1) * 4, :].rearrange("p a q -> p (a q)"),
                           taken(f"oT{half}")[:, :]).then_inc(K.a_done, 1)

    def body(s):
        uses.of(s)
        a, nx, pr, st = s + 1, s + 2, s + -1, s + 3
        for u in range(4):
            if s.exists():
                exp(s, u)
            if u == 0 and pr.exists():
                keep_oT(pr)
            if u == 1:
                if pr.exists():
                    wait(act, K.x3_done, pr.n)
                    nc.scalar.copy(K.yb[:, :], taken("y")[:, 0:D]).then_inc(K.a_done, 1)
                if nx.exists():
                    nc.scalar.copy(K.xT[:, nx.par, :], taken("xT")[:, 0:T]).then_inc(K.a_done, 1)
            if u == 2 and nx.exists():
                keep_qk(nx, 0)
                keep_qk(nx, 1)
        if a.exists():
            nc.scalar.copy(K.mT[:, :], taken("m")[:, :].bitcast(BF16)[:, 0:T]).then_inc(K.a_done, 1)
        if nx.exists():
            keep_v(nx)
            head_rstd(nx)
            keep_qkT(nx, 0)
            keep_qkT(nx, 1)
        if st.exists():
            rstd(st)

    pipeline(act, body, 3, 1)


def attn3_dve(nc, dve, K):
    uses = Uses()

    def stats(s):
        c = Chain(dve, K.l3_stat_step, s.n, 1)
        c.link(nc.vector.bn_stats(K.bn[:, :], batch(K.x, s.n)))
        nc.vector.memset(K.spare[:, :], 0.0)
        nc.vector.bn_aggr(K.mv[:, s.par, :], K.bn[:, :]).then_inc(K.l3_var_ready, 1)

    def normalise(s):
        wait(dve, K.l3_rstd_ready, s.n + 1)
        nc.vector.tensor_scalar(K.xn[:, :], batch(K.x, s.n), K.mv[:, s.par, 0:1], K.rs[:, s.par, 0:1],
                                ALU.subtract, ALU.mult).then_inc(K.l3_xn_ready, 1)

    def row_max(s, u):
        wait(dve, K.s3_ready, 4 * s.n + u + 1)
        out = K.m[:, :].rearrange("p (j a b) -> p j a b", j=2, a=4)[:, u // 2, :, u % 2]
        nc.vector.reduce_max(out, K.pS[u % 2][:, :].rearrange("p (a k) -> p a k", a=4), AX.X).then_inc(K.s3_done, 1)

    def split_max(s):
        dve.wait_ge(K.s3_done, 4 * s.n + 4)
        c = Chain(dve, K.l3_split_step, s.n, 3)
        c.link(nc.vector.tensor_scalar(K.m3[:, 0:H], K.m[:, :], -1.0, None, ALU.mult))
        c.link(nc.vector.scalar_tensor_tensor(K.mr[:, :], K.m[:, :], -1.0, K.m3[:, 0:H], ALU.mult, ALU.subtract))
        c.link(nc.vector.tensor_copy(K.m3[:, H:2 * H], K.mr[:, :]))
        nc.vector.tensor_tensor(K.m3[:, 2 * H:3 * H], K.mr[:, :], K.m3[:, H:2 * H],
                                ALU.subtract).then_inc(K.m33_ready, 1)

    def normalise_o(s, u):
        wait(dve, K.pv3_done, 4 * s.n + u + 1)
        po = K.pO3[u % 2][:, 0:4 * (HD3 + 1)].rearrange("p (a d) -> p a d", a=4)
        out = K.on3[:, :].rearrange("p (j a b d) -> p j a b d", j=2, a=4, b=2)[:, u // 2, :, u % 2, :]
        c = Chain(dve, K.l3_rec_step, 4 * s.n + u, 1)
        rec = K.rec[:, 4 * (u % 2):4 * (u % 2) + 4]
        c.link(nc.vector.reciprocal(rec, po[:, :, HD3]))
        nc.vector.tensor_tensor(out, po[:, :, 0:HD3], rec.unsqueeze(2).to_broadcast([T, 4, HD3]),
                                ALU.mult).then_inc(K.on3_done, 1)

    def squares(s):
        wait(dve, K.sq_ready, s.n + 1)
        nc.vector.reduce_sum(K.ss[:, :], K.sq3[:, :, :].rearrange("p w (h d) -> p (w h) d", d=HD3),
                             AX.X).then_inc(K.ss_ready, 1)

    def head_norm(s, which):
        if which == 0:
            wait(dve, K.rh_ready, s.n + 1)
        op = nc.vector.tensor_tensor(K.qk3n[:, which, :].rearrange("p (h d) -> p h d", h=H),
                                     K.qk3[:, which, :].rearrange("p (h d) -> p h d", h=H),
                                     K.rh[:, which * H:(which + 1) * H].unsqueeze(2).to_broadcast([T, H, HD3]), ALU.mult)
        op.then_inc((K.q3n_ready, K.k3n_ready)[which], 1)

    def residual(s):
        wait(dve, K.a_done, uses.at["y"] + 1)
        c = Chain(dve, K.l3_res_step, s.n, 1)
        c.link(nc.vector.tensor_tensor(K.y3[:, :], K.yb[:, :], K.row("bu3"), ALU.add))
        nc.vector.tensor_tensor(batch(K.x, s.n), batch(K.x, s.n), K.y3[:, :], ALU.add).then_inc(K.x3_done, 1)

    dve.wait_ge(K.x_done, K.x_before_attn[3])

    def body(s):
        uses.of(s)
        a, nx, pr, st = s + 1, s + 2, s + -1, s + 3
        if nx.exists():
            normalise(nx)
        for u in range(4):
            if a.exists():
                row_max(a, u)
            if u >= 1 and s.exists():
                normalise_o(s, u - 1)
            if u == 2 and pr.exists():
                residual(pr)
        if a.exists():
            split_max(a)
        if s.exists():
            normalise_o(s, 3)
        if nx.exists():
            squares(nx)
            head_norm(nx, 0)
            head_norm(nx, 1)
        if st.exists():
            stats(st)

    pipeline(dve, body, 3, 1)
    dve.wait_ge(K.x3_done, B)
    dve.sem_inc(K.x_done, 1)


def attn3_pool(nc, pool, K):
    uses = Uses()

    def body(s):
        uses.of(s)
        if (s + 2).exists():
            wait(pool, K.a_done, uses.at["K1"] + 1)
            nc.gpsimd.tensor_tensor(K.sq3[:, :, :], K.qk3[:, :, :], K.qk3[:, :, :], ALU.mult).then_inc(K.sq_ready, 1)

    pipeline(pool, body, 3, 1)



CONSTS = [("ident", T), ("blockmask", T), ("headmask", H), ("desc", E), ("selc", H), ("causal", T),
          ("causalT", T)]
NCONST = sum(w for _, w in CONSTS)
CONST_AT = {}
_at = 0
for _n, _w in CONSTS:
    CONST_AT[_n] = slice(_at, _at + _w)
    _at += _w


def setup_dve(nc, dve, K):
    def const(name):
        return K.consts[:, CONST_AT[name]]

    nc.vector.memset(K.eps[:, :], EPS)
    nc.vector.memset(K.one[:, :], 1.0)
    nc.vector.memset(K.vaug[:, :, :, :], 1.0)
    nc.vector.memset(K.linv[:, :, :], 1.0)
    nc.vector.memset(K.m3[:, :], 0.0)
    nc.vector.memset(K.ks[:, :], 0.0)
    nc.vector.memset(K.qs[:, :], 0.0).then_inc(K.set_step, 1)
    dve.wait_ge(K.consts_loaded, 16)
    nc.vector.tensor_copy(K.identb[:, :], const("ident"))
    nc.vector.tensor_copy(K.causal[:, :], const("causal"))
    nc.vector.tensor_copy(K.causalT[:, :], const("causalT"))
    nc.vector.tensor_copy(K.sel[:, :, :], const("selc").unsqueeze(2).to_broadcast([T, H, T]))
    dve.wait_ge(K.rows_loaded, 16)
    dve.wait_ge(K.cols_loaded, 16)
    dve.wait_ge(K.masks_loaded, 48)
    for n in (1, 2):
        nc.vector.tensor_scalar(K.bqs[:, n - 1, :], K.row(f"bq{n}"), HD ** -0.5, None, ALU.mult)
    nc.vector.tensor_scalar(K.qn8[:, 0:1], K.col("qn_w"), HD3 ** -0.5, None, ALU.mult)
    nc.vector.tensor_scalar(K.qn8[:, 1:2], K.col("qn_b"), HD3 ** -0.5, None, ALU.mult)
    nc.vector.tensor_scalar(K.pcol[1][:, :, 0], K.mcol[:, 0, :], 1.0, -NEG, ALU.subtract, ALU.mult)
    nc.vector.tensor_scalar(K.pcol[2][:, :, 0], K.mcol[:, 1, :], NEG, 2.0, ALU.mult, ALU.mult)
    dve.wait_ge(K.set_step, 1)
    nc.vector.memset(K.qs[:, :].rearrange("p (h c) -> p h c", h=H)[:, :, 6 * HD], 1.0)
    def part(out, a, b):
        K.parts += 1
        nc.vector.tensor_tensor(out, a, b, ALU.subtract).then_inc(K.part_step, 1)
        dve.wait_ge(K.part_step, K.parts)
    K.parts = 0
    for src, dst in ((K.amf[:, 0, :], K.amask), (K.amf[:, 1, :], K.amaskT)):
        for step, op in enumerate((lambda: nc.vector.tensor_scalar(src, src, NEG, None, ALU.max),
                                   lambda: nc.vector.tensor_copy(dst[:, 0, :], src))):
            K.parts += 1
            op().then_inc(K.part_step, 1)
            dve.wait_ge(K.part_step, K.parts)
        part(src, src, dst[:, 0, :])
        K.parts += 1
        nc.vector.tensor_copy(dst[:, 1, :], src).then_inc(K.part_step, 1)
        dve.wait_ge(K.part_step, K.parts)
        part(dst[:, 2, :], src, dst[:, 1, :])
    z, t = K.row("scale0"), K.sp
    c = Chain(dve, K.sp_step, 0, 11)
    c.link(nc.vector.tensor_scalar(t[:, 0, :], z, -1.0, None, ALU.mult))
    c.link(nc.vector.tensor_tensor(t[:, 0, :], t[:, 0, :], z, ALU.min))
    dve.sem_inc(K.spz_ready, 1)
    dve.wait_ge(K.spe_ready, 1)
    c.link(nc.vector.tensor_scalar(t[:, 2, :], t[:, 1, :], 1.0, None, ALU.add))
    dve.sem_inc(K.spu_ready, 1)
    c.link(nc.vector.tensor_scalar(t[:, 3, :], t[:, 2, :], 1.0, None, ALU.is_equal))
    c.link(nc.vector.scalar_tensor_tensor(t[:, 4, :], t[:, 2, :], 1.0, t[:, 3, :], ALU.subtract, ALU.add))
    c.link(nc.vector.reciprocal(t[:, 4, :], t[:, 4, :]))
    dve.wait_ge(K.spl_ready, 1)
    c.link(nc.vector.tensor_tensor(t[:, 5, :], t[:, 5, :], t[:, 3, :], ALU.add))
    c.link(nc.vector.tensor_tensor(t[:, 5, :], t[:, 5, :], t[:, 1, :], ALU.mult))
    c.link(nc.vector.tensor_tensor(t[:, 5, :], t[:, 5, :], t[:, 4, :], ALU.mult))
    c.link(nc.vector.scalar_tensor_tensor(t[:, 5, :], z, 0.0, t[:, 5, :], ALU.max, ALU.add))
    c.link(nc.vector.reciprocal(K.isp[:, :], t[:, 5, :]))
    dve.sem_inc(K.consts_ready, 1)


def setup_act(nc, act, K):
    act.preload_act_table_set(LN_EXP)
    act.wait_ge(K.spz_ready, 1)
    nc.scalar.activation(K.sp[:, 1, :], K.sp[:, 0, :], ACT.Exp).then_inc(K.spe_ready, 1)
    act.wait_ge(K.spu_ready, 1)
    nc.scalar.activation(K.sp[:, 5, :], K.sp[:, 2, :], ACT.Ln).then_inc(K.spl_ready, 1)


def before_layer3(nc, dve, K):
    for n, w in enumerate((K.w3qkv[:, 0, :], K.w3qkv[:, 1, :])):
        if n == 0:
            dve.wait_ge(K.w3_loaded, 64)
        heads = w.rearrange("p (h d) -> p h d", h=H)
        c = Chain(dve, K.centre_step, n, 2)
        c.link(nc.vector.reduce_sum(K.rec[:, :], heads, AX.X))
        c.link(nc.vector.tensor_scalar(K.rec[:, :], K.rec[:, :], -1.0 / HD3, None, ALU.mult))
        nc.vector.tensor_tensor(heads, heads, K.rec[:, :].unsqueeze(2).to_broadcast([T, H, HD3]),
                                ALU.add).then_inc(K.w3_centred, 1)
        dve.wait_ge(K.w3_centred, n + 1)
    nc.vector.memset(K.v3[:, :, :, HD3:HD3 + 1], 1.0)
    dve.wait_ge(K.int_loaded, 48)
    nc.vector.tensor_scalar(K.wint[:, :], K.wint[:, :].bitcast(I32), 1.0 / 127.0, None, ALU.mult).then_inc(K.deq_ready, 1)


def build(nc, a, out):
    ctx = ExitStack()
    with ctx:
        def sb(name, shape, dt=F32):
            return ctx.enter_context(nc.sbuf_tensor(name, shape, dt))

        K = Names()
        K.x = sb("x", [T, B, D])
        K.lin_w = sb("lin_w", [D, 3, D])
        K.wsmall = [sb(f"attn_w{n}", [D, 4, D]) for n in range(3)]
        early = sb("early", [128, 8192])
        w0_1 = early[:, 0:2048].rearrange("p (e n) -> p e n", e=E)
        w0_2 = early[:, 2048:4096].rearrange("p (e n) -> p e n", e=E)
        w0_3 = early[:, 4096:6144].rearrange("p (e h n) -> p e h n", e=E, h=2)
        K.x1 = early[:, 6144:8192].rearrange("p (b d) -> p b d", b=B)
        K.qk3 = early[:, 0:2048].rearrange("p (w n) -> p w n", w=2)
        K.qk3n = early[:, 2048:4096].rearrange("p (w n) -> p w n", w=2)
        K.sq3 = early[:, 4096:6144].rearrange("p (w n) -> p w n", w=2)
        qkT = early[:, 6144:8192].rearrange("p (c j q) -> p c j q", c=2, j=8)
        w1_1 = sb("w1_1", [128, E * 512])
        late = w1_1[:, :]
        K.q3T = qkT
        K.k3T = late[:, 0:2048].rearrange("p (c j q) -> p c j q", c=2, j=8)
        K.on3 = late[:, 2048:3072]
        K.o3T = late[:, 3072:4096].rearrange("p (j q) -> p j q", j=8)
        w1_2 = sb("w1_2", [128, E, 4, D])
        w2_1 = sb("w2_1", [128, E * 512])
        w2_2 = sb("w2_2", [128, E, 4, D])
        gates = sb("gates", [D, 3, E])
        b1s = sb("b1s", [128, 2, E * 4])
        b2s = sb("b2s", [E, 2, D])
        K.w3qkv = sb("w3qkv", [D, 3, H * HD3])
        K.wu = sb("wu", [128, 8, D])
        K.wint = sb("wint", [128, 9 * 128])
        K.v3 = sb("v3", [T, 2, H, HD3 + 1])
        K.rows, K.cols = sb("rows", [128, NROW]), sb("cols", [128, NCOL])
        K.row = lambda name: K.rows[:, ROW_AT[name][0]:ROW_AT[name][0] + ROW_AT[name][1]]
        K.row2 = lambda one, two: K.rows[:, ROW_AT[one][0]:ROW_AT[two][0] + ROW_AT[two][1]]
        K.col = lambda name: K.cols[:, COLS.index(name):COLS.index(name) + 1]
        K.consts = sb("consts", [128, NCONST])
        K.ident, K.blockmask = K.consts[:, CONST_AT["ident"]], K.consts[:, CONST_AT["blockmask"]]
        K.headmask = K.consts[:, CONST_AT["headmask"]]
        K.desc = K.consts[:, CONST_AT["desc"]]
        K.identb, K.causal = sb("identb", [T, T], BF16), sb("causalb", [T, T], BF16)
        K.causalT = sb("causalTb", [T, T], BF16)
        K.sel = sb("sel", [T, H, T], BF16)
        K.eps, K.bqs, K.qn8 = sb("eps", [128, 1]), sb("bqs", [T, 2, D]), sb("qn8", [128, 2])
        K.pcol = {1: sb("pcol1", [T, B, 1]), 2: sb("pcol2", [T, B, 1])}
        K.spare, K.one = sb("spare", [T, 1]), sb("one", [T, 1])
        K.mcol = sb("mcol", [T, 2, B], U8)
        K.amf = sb("amf", [T, 2, T])
        K.amask, K.amaskT = sb("amask", [T, 3, T], BF16), sb("amaskT", [T, 3, T], BF16)
        shared = sb("shared", [128, 2 * 4 * NT])
        K.sp, K.isp = shared[:, 2048:2816].rearrange("p (a d) -> p a d", a=6), sb("isp", [128, D])
        K.ctx, K.xT = sb("ctx", [D, 2, T]), sb("xT", [D, 2, T])
        K.xn, K.qkv = sb("xn", [T, D]), sb("qkv", [T, 3 * D])
        K.qs, K.ks = sb("qs", [T, H * 64], BF16), sb("ks", [T, H * 64], BF16)
        K.qt = shared[:, 0:1024].bitcast(BF16).rearrange("p (c j q) -> p c j q", c=2, j=8)
        K.kt = shared[:, 1024:2048].bitcast(BF16).rearrange("p (c j q) -> p c j q", c=2, j=8)
        K.vaug, K.pt = sb("vaug", [T, 2, H, HD + 1]), shared[:, 2048:3072].rearrange("p (c n) -> p c n", c=2)
        K.m, K.m3, K.mr, K.mT = sb("m", [T, H]), sb("m3", [T, T], BF16), sb("mr", [T, H]), sb("mT", [T, T], BF16)
        K.rec, K.on, K.oT, K.yb = sb("rec", [T, H]), sb("on", [T, D]), sb("oT", [D, T]), sb("yb", [T, D])
        K.y3 = sb("y3", [T, D])
        K.bn, K.mv, K.rs = sb("bn", [T, 6]), sb("mv", [T, 2, 2]), sb("rs", [T, 2, 2])
        K.lnv, K.var2, K.var2a = sb("lnv", [T, 2]), sb("var2", [T, 1]), sb("var2a", [T, 1])
        K.ss, K.lnh, K.rh = sb("ss", [T, 2 * H]), sb("lnh", [T, 2 * H]), sb("rh", [T, 2 * H])
        K.ft, K.f2, K.f3 = (shared[:, n:n + 256].rearrange("p (a d) -> p a d", a=2) for n in (0, 256, 512))
        K.fm, K.fr, K.fs, K.lnr, K.froot = sb("fm", [T, 2]), sb("fr", [T, 2]), sb("fs", [T, 4]), sb("lnr", [T, 2]), sb("froot", [T, 2])
        K.feat, K.linv = shared[:, 1024:1536].rearrange("p (c a d) -> p c a d", c=2, a=2), sb("linv", [T, 2, D + 1])
        K.lqT, K.kvblk = sb("lqT", [D, T]), sb("kvblk", [D, D + H])
        K.xg, K.xTg = sb("xg", [T, GB, D]), sb("xTg", [D, NT])
        K.hT = shared[:, :].rearrange("p (c h n) -> p c h n", c=2, h=4)
        K.silu = sb("silu", [128, 2, NT])
        K.bng, K.mvg, K.lng, K.rsg = sb("bng", [T, GB, 6]), sb("mvg", [T, GB, 2]), sb("lng", [T, GB]), sb("rsg", [T, GB])
        K.gl, K.g1, K.g2, K.wts = (sb(n, [T, GB, E]) for n in ("gl", "g1", "g2", "wts"))
        K.gm, K.gm1, K.gi, K.gs = (sb(n, [T, GB]) for n in ("gm", "gm1", "gi", "gs"))
        K.gd, K.ge = sb("gd", [T, GB * E]), sb("ge", [T, GB * E])
        K.wT = sb("wT", [E, NT])

        bank = [ctx.enter_context(nc.psum_tensor(f"bank{n}", [128, 512], F32)) for n in range(8)]
        K.pT, K.pP, K.pO, K.pM = bank[0], bank[1], bank[6], bank[7]
        K.pS, K.pC, K.pH, K.pY, K.pA, K.pO3 = bank[2:4], bank[4:6], bank[2:6], bank[6:8], bank[0:2], bank[6:8]
        K.pMb, K.pTb, K.pPb = (bank[n][:, :].bitcast(BF16) for n in (7, 0, 1))

        def sem(name):
            return ctx.enter_context(nc.semaphore(name))

        def sems(names):
            return [sem(name) for name in names.split()]

        K.a_done, K.a_ready, K.c3_ready, K.c_ready, K.centre_step = sems(
            "a_done a_ready c3_ready c_ready centre_step")
        K.cols_loaded, K.consts_loaded, K.consts_ready, K.deq_ready, K.exp3_done = sems(
            "cols_loaded consts_loaded consts_ready deq_ready exp3_done")
        K.exp_done, K.int_loaded, K.k3n_ready, K.ks_ready, K.ksplit_step = sems(
            "exp_done int_loaded k3n_ready ks_ready ksplit_step")
        K.kt_done, K.kt_ready, K.kv_done, K.l3_hr_step, K.l3_rec_step = sems(
            "kt_done kt_ready kv_done l3_hr_step l3_rec_step")
        K.l3_res_step, K.l3_rstd_ready, K.l3_rstd_step, K.l3_split_step, K.l3_stat_step = sems(
            "l3_res_step l3_rstd_ready l3_rstd_step l3_split_step l3_stat_step")
        K.l3_var_ready, K.l3_xn_ready, K.lin_f_ready, K.lin_f_step, K.lin_kv_done = sems(
            "l3_var_ready l3_xn_ready lin_f_ready lin_f_step lin_kv_done")
        K.lin_kv_ready, K.lin_o_done, K.lin_o_ready, K.lin_o_step, K.lin_p_done = sems(
            "lin_kv_ready lin_o_done lin_o_ready lin_o_step lin_p_done")
        K.lin_p_ready, K.lin_qT_done, K.lin_qT_ready, K.lin_ratio_ready, K.lin_root_ready = sems(
            "lin_p_ready lin_qT_done lin_qT_ready lin_ratio_ready lin_root_ready")
        K.lin_root_step, K.lin_rstd_ready, K.lin_rstd_step, K.lin_stat_step, K.lin_var_ready = sems(
            "lin_root_step lin_rstd_ready lin_rstd_step lin_stat_step lin_var_ready")
        K.lin_w_loaded, K.lin_xT_done, K.lin_xT_ready, K.lin_xn_ready, K.m33_ready = sems(
            "lin_w_loaded lin_xT_done lin_xT_ready lin_xn_ready m33_ready")
        K.m3_ready, K.mT_done, K.mT_ready, K.masks_loaded, K.oT_done = sems(
            "m3_ready mT_done mT_ready masks_loaded oT_done")
        K.oT_ready, K.on3_done, K.on_ready, K.out_done, K.part_step = sems(
            "oT_ready on3_done on_ready out_done part_step")
        K.pv3_done, K.pv_done, K.q3n_ready, K.q_done = sems(
            "pv3_done pv_done q3n_ready q_done")
        K.qkv_ready, K.qs_ready, K.qsplit_step, K.qt_done, K.qt_ready = sems(
            "qkv_ready qs_ready qsplit_step qt_done qt_ready")
        K.rec_step, K.res_step, K.rh_ready, K.rows_loaded, K.rstd2_ready = sems(
            "rec_step res_step rh_ready rows_loaded rstd2_ready")
        K.rstd2_step, K.rstd_ready, K.rstd_step, K.s3_done, K.s3_ready = sems(
            "rstd2_step rstd_ready rstd_step s3_done s3_ready")
        K.s_ready, K.set_step, K.smax_done, K.sp_step, K.spe_ready = sems(
            "s_ready set_step smax_done sp_step spe_ready")
        K.spl_ready, K.split_step, K.spu_ready, K.spz_ready, K.sq_ready = sems(
            "spl_ready split_step spu_ready spz_ready sq_ready")
        K.ss_ready, K.stat_step, K.v_done, K.var2_ready, K.var2_step = sems(
            "ss_ready stat_step v_done var2_ready var2_step")
        K.var_ready, K.w3_centred, K.w3_loaded, K.x1_step, K.x3_done = sems(
            "var_ready w3_centred w3_loaded x1_step x3_done")
        K.xT_done, K.xT_ready, K.x_done, K.x_loaded, K.xn_ready = sems(
            "xT_done xT_ready x_done x_loaded xn_ready")
        K.y_done, K.y_ready = sems(
            "y_done y_ready")
        K.ctx_loaded = [ctx.enter_context(nc.semaphore(f"ctx_loaded{n}")) for n in range(2)]
        K.attn_w_loaded = [ctx.enter_context(nc.semaphore(f"attn_w_loaded{n}")) for n in range(3)]
        ffn_sems = {n: ctx.enter_context(nc.semaphore(f"ffn_{n}")) for n in FFN_COUNTS}
        K.ffn = {}
        for kind in range(4):
            F = Names()
            F.scale, F.w_loaded = 1.0, sem(f"ffn_w_loaded{kind}")
            at = {n: From(h, sum(FFN_COUNTS[n][:kind])) for n, h in ffn_sems.items()}
            F.var_ready, F.rstd_step, F.rstd_ready, F.stat_step, F.xn_ready, F.xT_ready, F.xT_done = (
                at[n] for n in "var_ready rstd_step rstd_ready stat_step xn_ready xT_ready xT_done".split())
            F.l_ready, F.d_ready, F.e_ready, F.w_ready, F.wT_ready, F.wT_done, F.a_ready = (
                at[n] for n in "l_ready d_ready e_ready w_ready wT_ready wT_done a_ready".split())
            F.b_ready, F.silu_done, F.h_ready, F.h_done, F.gate_step, F.y_ready, F.acc_done = (
                at[n] for n in "b_ready silu_done h_ready h_done gate_step y_ready acc_done".split())
            F.experts, F.blocks = (E, E, E, 1)[kind], (2, 4, 4, 3)[kind]
            F.ys = F.experts + (kind in (1, 2))
            K.ffn[kind] = F
        F0, F1, F2, F3 = (K.ffn[n] for n in range(4))
        F0.w1, F0.w2, F0.w3, F0.gate = w0_1, w0_2, w0_3, gates[:, 0, :]
        for n, F, w, w2 in ((1, F1, w1_1, w1_2), (2, F2, w2_1, w2_2)):
            F.w1, F.w3 = w[:, :].rearrange("p (e n) -> p e n", e=E), w2
            F.gate, F.b1, F.b2 = gates[:, n, :], b1s[:, n - 1, :], b2s[:, n - 1, :]
        F3.w1 = K.wint[:, 0:384].unsqueeze(1)
        F3.w2 = K.wint[:, 384:768].unsqueeze(1)
        F3.w3 = K.wint[:, 768:1152].rearrange("p (e h n) -> p e h n", e=1, h=3)
        F0.loaded, F1.loaded, F2.loaded = [(F0.w_loaded, 64)], [(F1.w_loaded, 80)], [(F2.w_loaded, 80)]
        F3.loaded = [(K.deq_ready, 1)]
        K.x_before_attn = {0: 16, 1: 33, 2: 50, 3: 67}
        K.x_before_ffn = {0: 32, 1: 49, 2: 66, 3: 68}
        K.n_consts = 1

        block = ctx.enter_context(nc.Block())

        @block.sync
        def _(sp):
            sp.dma_start(K.x[:, :, :], a["x"]).then_inc(K.x_loaded, 16)
            sp.dma_start(K.consts[:, :], a["consts"]).then_inc(K.consts_loaded, 16)
            sp.dma_start(K.rows[:, :], a["rows"].partition_broadcast(128)).then_inc(K.rows_loaded, 16)
            sp.dma_start(K.cols[:, :], a["cols"]).then_inc(K.cols_loaded, 16)
            sp.dma_start(K.mcol[:, :, :].bitcast(I32), a["mcol"]).then_inc(K.masks_loaded, 16)
            sp.dma_start(K.amf[:, :, :], a["amf"]).then_inc(K.masks_loaded, 32)
            ctxT = a["ctxT"]

            def load_ctx(s):
                src = ctxT[s.n] if s.static() else ctxT[bass.ds(s.n, 1)].rearrange("a d t -> d (a t)")
                sp.dma_start(K.ctx[:, s.par, :], src).then_inc(K.ctx_loaded[s.par], 16)

            def lin(s):
                if s.c >= 2 or not s.static():
                    wait(sp, K.lin_p_ready, s.n - 1)
                load_ctx(s)

            pipeline(sp, lin, 0, 0)
            for lay in (1, 2):
                def attn(s):
                    wait(sp, K.qkv_ready, s.n + B * lay - 1)
                    load_ctx(s)
                sp.wait_ge(K.lin_p_ready, B)
                pipeline(sp, attn, 0, 0)
            sp.wait_ge(K.qkv_ready, 3 * B)
            uses = Uses()

            def attn3(s):
                uses.of(s)
                if s.exists() or s.c < 0:
                    wait(sp, K.a_ready, uses.start)
                if (s + 3).exists():
                    load_ctx(s + 3)

            pipeline(sp, attn3, 3, 1)
            for g in range(B // GB):
                wait(sp, K.ffn[3].acc_done, g + 1)
                sp.dma_start(out.rearrange("b t d -> t b d")[:, g * GB:(g + 1) * GB, :],
                             K.x[:, g * GB:(g + 1) * GB, :]).then_inc(K.out_done, 16)
            sp.wait_ge(K.out_done, 16 * (B // GB))

        @block.scalar
        def _(act):
            act.dma_start(K.lin_w[:, :, :], a["lin_w"]).then_inc(K.lin_w_loaded, 48)
            act.dma_start(K.wsmall[0][:, :, :], a["attn_w"][0]).then_inc(K.attn_w_loaded[0], 64)
            act.dma_start(gates[:, :, :], a["gates"]).then_inc(F0.w_loaded, 16)
            act.dma_start(w0_1, a["w0_1"].rearrange("e d h -> d e h")).then_inc(F0.w_loaded, 16)
            act.dma_start(w0_2, a["w0_2"].rearrange("e d h -> d e h")).then_inc(F0.w_loaded, 16)
            act.dma_start(w0_3, a["w0_3"]).then_inc(F0.w_loaded, 16)
            for n, F, w, w2, aw, aw2 in ((1, F1, w1_1, w1_2, a["w1_1"], a["w1_2"]), (2, F2, w2_1, w2_2, a["w2_1"], a["w2_2"])):
                act.dma_start(K.wsmall[n][:, :, :], a["attn_w"][n]).then_inc(K.attn_w_loaded[n], 64)
                act.dma_start(F.w1, aw.rearrange("e d h -> d e h")).then_inc(F.w_loaded, 16)
                act.dma_start(w2[:, :, :, :], aw2).then_inc(F.w_loaded, 16)
                act.dma_start(b1s[:, n - 1, :], a["b1s"][n - 1]).then_inc(F.w_loaded, 16)
                act.dma_start(b2s[:, n - 1, :], a["b2s"][n - 1]).then_inc(F.w_loaded, 32)
            act.dma_start(K.w3qkv[:, :, :], a["w3qkv"]).then_inc(K.w3_loaded, 48)
            act.dma_start(K.wu[:, :, :], a["wu"]).then_inc(K.w3_loaded, 16)
            act.dma_start(K.wint[:, :].bitcast(I32), a["wint"]).then_inc(K.int_loaded, 48)
            setup_act(nc, act, K)
            lin_act(nc, act, K)
            for lay in range(3):
                attn_act(nc, act, K, lay)
                ffn_act(nc, act, K, lay)
            attn3_act(nc, act, K)
            ffn_act(nc, act, K, 3)

        @block.vector
        def _(dve):
            setup_dve(nc, dve, K)
            lin_dve(nc, dve, K)
            for lay in range(3):
                attn_dve(nc, dve, K, lay)
                ffn_dve(nc, dve, K, lay)
            before_layer3(nc, dve, K)
            attn3_dve(nc, dve, K)
            ffn_dve(nc, dve, K, 3)

        @block.tensor
        def _(pe):
            lin_pe(nc, pe, K)
            for lay in range(3):
                attn_pe(nc, pe, K, lay)
                ffn_pe(nc, pe, K, lay)
            attn3_pe(nc, pe, K)
            ffn_pe(nc, pe, K, 3)

        @block.gpsimd
        def _(pool):
            for lay in range(3):
                attn_pool(nc, pool, K, lay)
            attn3_pool(nc, pool, K)


INPUTS = ["x", "ctxT", "lin_w", "attn_w", "gates", "w0_1", "w0_2", "w0_3", "w1_1", "w1_2", "w2_1", "w2_2", "b1s", "b2s",
          "w3qkv", "wu", "wint", "rows", "cols", "consts", "mcol", "amf"]


def constants(np):
    p, c = np.arange(128)[:, None], np.arange(128)[None, :]
    r16 = np.arange(16)[None, :]
    parts = {
        "ident": p == c, "blockmask": p // HD == c // HD, "headmask": p // HD == r16,
        "desc": np.zeros((128, 1)) + (E - np.arange(E)[None, :]),
        "selc": (p % H == r16) & (p < 3 * H), "causal": (c > p) * NEG, "causalT": (p > c) * NEG
    }
    return np.concatenate([np.asarray(parts[n], np.float32) for n, _ in CONSTS], axis=1)


def lay_out(np, v):
    f = {n: np.ascontiguousarray(a) for n, a in v.items()}
    d = {"x": f["x"].transpose(1, 0, 2), "ctxT": f["ctx_1024"].transpose(0, 2, 1)}
    d["lin_w"] = np.stack([f[f"L0_xattn_W{n}"] for n in "qkv"], 1)
    kv = f["L1_xattn_Wkv"]
    d["attn_w"] = np.stack([
        np.stack([f["L0_ffn_wq"], f["L0_ffn_wk"], f["L0_ffn_wv"], f["L0_ffn_wo"]], 1),
        np.stack([f["L1_xattn_Wq"], kv[:, :D], kv[:, D:], f["L1_xattn_Wp"]], 1),
        np.stack([f[f"L2_xattn_W{n}"].T for n in ("q", "k", "v", "out")], 1)])
    d["gates"] = np.stack([f["L0_ffn_gate_w"], f["L1_ffn_w_gate"], f["L2_ffn_Wr"]], 1)
    d["w0_1"], d["w0_2"], d["w0_3"] = f["L0_ffn_w1"], f["L0_ffn_w2"], f["L0_ffn_w3"]
    d["w1_1"], d["w1_2"], d["w2_1"], d["w2_2"] = f["L1_ffn_W1"], f["L1_ffn_W2"], f["L2_ffn_W1"], f["L2_ffn_W2"]
    for n in ("w0_3", "w1_2", "w2_2"):
        d[n] = d[n].reshape(E, -1, 128, D).transpose(2, 0, 1, 3)
    d["b1s"] = np.stack([f[f"L{n}_ffn_b1"].reshape(E * 4, 128).T for n in (1, 2)])
    d["b2s"] = np.stack([f[f"L{n}_ffn_b2"] for n in (1, 2)])
    d["w3qkv"] = np.stack([f[f"L3_xattn_W{n}"].T for n in "qkv"], 1)
    d["wu"] = f["L3_xattn_Wu"].T.reshape(8, 128, D).transpose(1, 0, 2)
    down = f["L3_ffn_w_down"].T.reshape(3, 128, D).transpose(1, 0, 2).reshape(128, 3 * D)
    d["wint"] = np.concatenate([f["L3_ffn_w_gate"].T, f["L3_ffn_w_up"].T, down], 1)
    bkv = f["L1_xattn_bkv"]
    rows = {"bq0": "L0_xattn_bq", "bk0": "L0_xattn_bk", "bv0": "L0_xattn_bv", "scale0": "L0_xattn_scale", "bo": "L0_ffn_bo",
            "bq1": "L1_xattn_bq", "bq2": "L2_xattn_bq", "bk2": "L2_xattn_bk", "bp1": "L1_xattn_bp", "bv2": "L2_xattn_bv", "bout2": "L2_xattn_bout", "bu3": "L3_xattn_bu",
            "bg1": "L1_ffn_b_gate", "br2": "L2_ffn_br"}
    d["rows"] = np.concatenate([bkv[:D] if n == "bk1" else bkv[D:] if n == "bv1" else f[rows[n]].reshape(-1) for n, _ in ROWS])
    twice = lambda n: np.concatenate([f[n], f[n]])
    d["cols"] = np.stack([f["L0_ffn_ln1_scale"], f["L0_ffn_ln1_shift"], f["L0_ffn_ln2_scale"], f["L0_ffn_ln2_shift"],
                          twice("L3_xattn_qn_w"),
                          twice("L3_xattn_qn_b"), twice("L3_xattn_kn_w"), twice("L3_xattn_kn_b")], 1)
    d["consts"] = constants(np)
    m1, m2 = (f[n].view(np.uint8) for n in ("mask_BxS2_bf1", "mask_BxS2_bf0"))
    d["mcol"] = np.ascontiguousarray(np.stack([m1.T, m2.T], 1)).view(np.int32)
    d["amf"] = np.stack([f["mask_SxS2_ff0"], f["mask_SxS2_ff0"].T], 1)
    return {n: np.ascontiguousarray(d[n]) for n in INPUTS}


def kernel(**inputs):
    import numpy as np
    import concourse.bacc as bacc
    from concourse.bass_utils import run_bass_kernel_spmd

    nc = bacc.Bacc("TRN2", target_bir_lowering=False, num_devices=1)
    arrays = lay_out(np, inputs)
    a = {n: nc.dram_tensor(f"in_{n}", v.shape, mybir.dt.from_np(v.dtype), kind="ExternalInput").ap()
         for n, v in arrays.items()}
    out = nc.dram_tensor("out_x", (B, T, D), F32, kind="ExternalOutput").ap()
    build(nc, a, out)
    r = run_bass_kernel_spmd(nc, [{f"in_{n}": v for n, v in arrays.items()}], core_ids=[0])
    return r.results[0]["out_x"]
```

```python
from contextlib import ExitStack

import concourse.bass as bass
from concourse import mybir

F32 = mybir.dt.float32
BF16 = mybir.dt.bfloat16
F32R = mybir.dt.float32r
I32 = mybir.dt.int32
U8 = mybir.dt.uint8
ALU = mybir.AluOpType
ACT = mybir.ActivationFunctionType
AX = mybir.AxisListType

B, T, D = 16, 128, 128
H, HD = 16, 8
G = 4
NG = H // G
HD3 = 64
E = 8
GB = 4
NT = GB * T
LN_EXP = "natural_log_exp_and_others"
NEG = -1.5 * 2.0 ** 127
EPS = 1e-5

COLS = ["ln1_s", "ln1_b", "ln2_s", "ln2_b", "qn_w", "qn_b", "kn_w", "kn_b"]
ROWS = [("bq0", D), ("bk0", D), ("bv0", D), ("scale0", D), ("bo", D), ("bq1", D), ("bk1", D), ("bv1", D), ("bp1", D),
        ("bq2", D), ("bk2", D), ("bv2", D),
        ("bout2", D), ("bu3", D), ("bg1", E), ("br2", E)]
ROW_AT = {}
_at = 0
for _n, _w in ROWS:
    ROW_AT[_n] = (_at, _w)
    _at += _w
NROW = _at
NCOL = len(COLS)


NGR = B // GB
FFN_COUNTS = {n: [NGR] * 4 for n in ("var_ready", "rstd_step", "rstd_ready", "stat_step", "xn_ready", "xT_ready", "xT_done",
                                 "xh_ready", "xl_ready")}
FFN_COUNTS.update({n: [NGR] * 3 + [0] for n in ("l_ready", "d_ready", "e_ready", "w_ready")})
FFN_COUNTS.update({n: [0, NGR, NGR, 0] for n in ("wT_ready", "wT_done")})
FFN_COUNTS.update({n: [NGR * 16, 0, 0, NGR * 3] for n in ("a_ready", "b_ready", "silu_done")})
FFN_COUNTS.update({"h_ready": [0, NGR * 32, NGR * 32, 0], "h_done": [NGR * 16, NGR * 32, NGR * 32, NGR * 3],
                   "gate_step": [NGR * 17, NGR * 8, NGR * 8, 0]})
FFN_COUNTS.update({n: [NGR * 8, NGR * 9, NGR * 9, NGR] for n in ("y_ready", "acc_done")})


class Names:
    pass


class From:

    def __init__(self, sem, base):
        self.sem, self.base = sem, base


def wait(eng, sem, value):
    if isinstance(sem, From):
        sem, value = sem.sem, value + sem.base
    if not (isinstance(value, int) and value <= 0):
        eng.wait_ge(sem, value)


class Chain:

    def __init__(self, eng, sem, k, per):
        self.eng, self.sem, self.base, self.per, self.n = eng, sem, k * per, per, 0
        if isinstance(sem, From):
            self.sem, self.base = sem.sem, k * per + sem.base

    def link(self, ins):
        self.n += 1
        ins.then_inc(self.sem, 1)
        self.eng.wait_ge(self.sem, self.base + self.n)

    def done(self):
        assert self.n == self.per, (self.n, self.per)


class Step:

    def __init__(self, i, c):
        self.i, self.c = i, c
        self.n, self.par, self.half = i * 2 + c, c % 2, i + c // 2

    def __add__(self, d):
        return Step(self.i, self.c + d)

    def static(self):
        return isinstance(self.i, int)

    def exists(self, count=B):
        return not self.static() or 0 <= self.c < count

    def within(self, count=B):
        return min(max(self.c, 0), count) if self.static() else self.n


def pipeline(eng, body, before, after):
    first = 2
    pairs = (B - before - first) // 2
    for c in range(-before, first):
        body(Step(0, c))
    with eng.Fori(0, pairs) as i:
        body(Step(i, first))
        body(Step(i, first + 1))
    for c in range(first + 2 * pairs, B + after):
        body(Step(0, c))


def batch(t, n):
    return t[:, n, :] if isinstance(n, int) else t[:, bass.ds(n, 1), :].rearrange("p a d -> p (a d)")



def unit_head(u, a):
    return 2 * (4 * (u // 2) + a) + u % 2


def unit_max(K, u):
    return K.m[:, :].rearrange("p (j a b) -> p j a b", j=2, a=4)[:, u // 2, :, u % 2]


def attn_pe(nc, pe, K, lay):
    W, Wo = K.wsmall[lay], K.wsmall[lay][:, 3, :]
    k0 = B * lay

    def transpose_x(s):
        k = s.n + k0
        wait(pe, K.xn_ready, k + 1)
        wait(pe, K.kt_done, k)
        wait(pe, K.oT_done, k0 + (s + -3).within())
        nc.tensor.transpose(K.pT[:, 0:T], K.xn[:, :], K.ident[:, :]).then_inc(K.xT_ready, 1)

    def project(s):
        k = s.n + k0
        wait(pe, K.xT_done, k + 1)
        wait(pe, K.qt_done, k)
        x = K.xT[:, s.par, :]
        if lay == 0:
            mm = nc.tensor.matmul(K.pP[:, 0:3 * D], x, W[:, 0:3, :].rearrange("p a d -> p (a d)"), start=True, stop=True)
        else:
            pe.wait_ge(K.ctx_loaded[s.par], 16 * (s.half + 1 + (B // 2) * lay))
            nc.tensor.matmul(K.pP[:, 0:D], x, W[:, 0, :], start=True, stop=True)
            mm = nc.tensor.matmul(K.pP[:, D:3 * D], K.ctx[:, s.par, :], W[:, 1:3, :].rearrange("p a d -> p (a d)"),
                                  start=True, stop=True)
        mm.then_inc(K.qkv_ready, 1)

    def transpose_q(s):
        wait(pe, K.qs_ready, s.n + k0 + 1)
        for j in range(H // 2):
            mm = nc.tensor.transpose(K.pPb[:, j * T:(j + 1) * T], K.qs[:, j * 128:(j + 1) * 128], K.identb[:, :])
        mm.then_inc(K.qt_ready, 1)

    def transpose_k(s):
        wait(pe, K.ks_ready, s.n + k0 + 1)
        for j in range(H // 2):
            mm = nc.tensor.transpose(K.pTb[:, j * T:(j + 1) * T], K.ks[:, j * 128:(j + 1) * 128], K.identb[:, :])
        mm.then_inc(K.kt_ready, 1)

    def mask(bank, causal, parts):
        masks = [[causal[:, :]], [K.zeros[:, :]], [parts[:, part, :] for part in range(2)]][lay]
        ident = K.identr if lay == 2 else K.identb
        for n, m in enumerate(masks):
            nc.tensor.matmul(bank[:, :], ident[:, :], m.unsqueeze(1).to_broadcast([T, G, T]), start=(n == 0),
                             stop=False, skip_group_check=True)

    def row_scores(s, u):
        k = s.n + k0
        if u == 0:
            wait(pe, K.qt_done, k + 1)
            wait(pe, K.kt_done, k + 1)
        wait(pe, K.smax_done, 4 * k + u - 1)
        bank, r = K.pS[u % 2], slice(64 * (u % 2), 64 * (u % 2) + 64)
        if lay != 1:
            mask(bank, K.causal, K.amask)
        for a in range(G):
            j = G * (u // 2) + a
            mm = nc.tensor.matmul(bank[:, a * T:(a + 1) * T], K.qt[r, s.par, j, :], K.kt[r, s.par, j, :],
                                  start=(lay == 1 and a == 0), stop=(a == G - 1), skip_group_check=True)
        mm.then_inc(K.s_ready, 1)

    def transpose_max(s):
        k = s.n + k0
        wait(pe, K.m3_ready, k + 1)
        wait(pe, K.mT_done, k)
        wait(pe, K.y_done, k0 + (s + -1).within())
        nc.tensor.transpose(K.pMb[:, 0:T], K.m3[:, :], K.identb[:, :]).then_inc(K.mT_ready, 1)

    def col_scores(s, u):
        k = s.n + k0
        wait(pe, K.exp_done, 4 * k + u - 1)
        bank, r = K.pC[u % 2], slice(64 * (u % 2), 64 * (u % 2) + 64)
        mask(bank, K.causalT, K.amaskT)
        for a in range(G):
            j = G * (u // 2) + a
            nc.tensor.matmul(bank[:, a * T:(a + 1) * T], K.kt[r, s.par, j, :], K.qt[r, s.par, j, :],
                             start=False, stop=False, skip_group_check=True)
        if u == 0:
            wait(pe, K.mT_done, k + 1)
        for a in range(G):
            mm = nc.tensor.matmul(bank[:, a * T:(a + 1) * T], K.sel[:, unit_head(u, a), :], K.mT[:, :],
                                  start=False, stop=(a == G - 1), skip_group_check=True)
        mm.then_inc(K.c_ready, 1)

    def probs_v(s, u):
        k = s.n + k0
        if u == 0:
            wait(pe, K.v_done, k + 1)
            wait(pe, K.heads_done, k)
        wait(pe, K.exp_done, 4 * k + u + 1)
        for a in range(G):
            mm = nc.tensor.matmul(K.pO[32 * a:32 * a + 32, u * T:(u + 1) * T], K.vaug[:, s.par, unit_head(u, a), :],
                                  K.pt[:, u % 2, a * T:(a + 1) * T], start=True, stop=True)
        mm.then_inc(K.pv_done, 1)

    def transpose_heads(s):
        k = s.n + k0
        wait(pe, K.heads_done, k + 1)
        wait(pe, K.mT_done, k0 + (s + 2).within())
        wait(pe, K.y_done, k)
        for u in range(4):
            mm = nc.tensor.transpose(K.pM[:, u * T:(u + 1) * T], K.heads[:, u * T:(u + 1) * T], K.ident[:, :])
        mm.then_inc(K.hT_ready, 1)

    def transpose_o(s):
        k = s.n + k0
        wait(pe, K.on_ready, k + 1)
        wait(pe, K.kt_done, k0 + (s + 3).within())
        wait(pe, K.xT_done, k0 + (s + 4).within())
        nc.tensor.transpose(K.pT[:, 0:T], K.on[:, :], K.ident[:, :]).then_inc(K.oT_ready, 1)

    def out_project(s):
        k = s.n + k0
        wait(pe, K.oT_done, k + 1)
        wait(pe, K.mT_done, k0 + (s + 2).within())
        wait(pe, K.y_done, k)
        nc.tensor.matmul(K.pM[:, 0:D], K.oT[:, :], Wo, start=True, stop=True).then_inc(K.y_ready, 1)

    pe.wait_ge(K.attn_w_loaded[lay], 64)

    def body(s):
        a, nx, pr = s + 1, s + 2, s + -1
        for u in range(4):
            if s.exists():
                col_scores(s, u)
            if u == 2 and pr.exists():
                transpose_o(pr)
            if a.exists():
                row_scores(a, u)
            if u == 0 and pr.exists():
                transpose_heads(pr)
            if u == 0 and nx.exists():
                transpose_x(nx)
            if u == 1 and nx.exists():
                project(nx)
            if u >= 1 and s.exists():
                probs_v(s, u - 1)
            if u == 2 and pr.exists():
                out_project(pr)
        if nx.exists():
            transpose_q(nx)
            transpose_k(nx)
        if s.exists():
            probs_v(s, 3)
        if a.exists():
            transpose_max(a)

    pipeline(pe, body, 3, 1)


def attn_act(nc, act, K, lay):
    k0 = B * lay

    def rstd(s):
        k = s.n + k0
        wait(act, K.var_ready, k + 1)
        c = Chain(act, K.rstd_step, k, 1)
        c.link(nc.scalar.activation(K.lnv[:, 0:1], K.mv[:, s.par, 1:2], ACT.Ln, bias=K.eps[:, :]))
        c.done()
        nc.scalar.activation(K.rs[:, s.par, 0:1], K.lnv[:, 0:1], ACT.Exp, scale=-0.5).then_inc(K.rstd_ready, 1)

    def rstd2(s):
        wait(act, K.var2_ready, s.n + 1)
        c = Chain(act, K.rstd2_step, s.n, 1)
        c.link(nc.scalar.activation(K.lnv[:, 1:2], K.var2[:, :], ACT.Ln, bias=K.eps[:, :]))
        nc.scalar.activation(K.rs[:, s.par, 1:2], K.lnv[:, 1:2], ACT.Exp, scale=-0.5).then_inc(K.rstd2_ready, 1)

    def keep_xT(s):
        wait(act, K.xT_ready, s.n + k0 + 1)
        if lay == 0:
            op = nc.scalar.activation(K.xT[:, s.par, :], K.pT[:, 0:T], ACT.Identity, scale=K.col("ln1_s"),
                                      bias=K.col("ln1_b"))
        else:
            op = nc.scalar.copy(K.xT[:, s.par, :], K.pT[:, 0:T])
        op.then_inc(K.xT_done, 1)

    def keep_qT(s):
        wait(act, K.qt_ready, s.n + k0 + 1)
        nc.scalar.copy(K.qt[:, s.par, :, :].rearrange("p j q -> p (j q)"), K.pPb[:, 0:8 * T]).then_inc(K.qt_done, 1)

    def keep_mT(s):
        wait(act, K.mT_ready, s.n + k0 + 1)
        nc.scalar.copy(K.mT[:, :], K.pMb[:, 0:T]).then_inc(K.mT_done, 1)

    def exp(s, u):
        k = s.n + k0
        wait(act, K.c_ready, 4 * k + u + 1)
        wait(act, K.pv_done, 4 * k + u - 1)
        nc.scalar.activation(K.pt[:, u % 2, :], K.pC[u % 2][:, :], ACT.Exp).then_inc(K.exp_done, 1)

    def keep_heads(s):
        wait(act, K.pv_done, 4 * (s.n + k0 + 1))
        nc.scalar.copy(K.heads[:, :], K.pO[:, :]).then_inc(K.heads_done, 1)

    def keep_oT(s):
        wait(act, K.oT_ready, s.n + k0 + 1)
        nc.scalar.copy(K.oT[:, :], K.pT[:, 0:T]).then_inc(K.oT_done, 1)

    def body(s):
        a, nx, pr, st = s + 1, s + 2, s + -1, s + 3
        for u in range(4):
            if u == 0 and pr.exists():
                keep_heads(pr)
            if u == 2 and pr.exists():
                keep_oT(pr)
            if s.exists():
                exp(s, u)
            if u == 0 and nx.exists():
                keep_xT(nx)
            if u == 2 and st.exists():
                rstd(st)
        if lay == 0 and st.exists():
            rstd2(st)
        if nx.exists():
            keep_qT(nx)
        if a.exists():
            keep_mT(a)

    pipeline(act, body, 3, 1)


def split(c, engine, copy, parts, x, first, second, third):
    heads = x.rearrange("p (h d) -> p h d", h=H)
    c.link(copy(first, heads.unsqueeze(2).to_broadcast([T, H, 3, HD])))
    c.link(engine.tensor_tensor(heads, heads, first[:, :, 0, :], ALU.subtract))
    c.link(copy(second, heads.unsqueeze(2).to_broadcast([T, H, 2, HD])))
    engine.tensor_tensor(third, heads, second[:, :, 0, :], ALU.subtract).then_inc(parts, 1)


def attn_dve(nc, dve, K, lay):
    k0 = B * lay

    def stats(s):
        k = s.n + k0
        c = Chain(dve, K.stat_step, k, 1)
        c.link(nc.vector.bn_stats(K.bn[:, :], batch(K.x, s.n)))
        nc.vector.memset(K.spare[:, :], 0.0)
        nc.vector.bn_aggr(K.mv[:, s.par, :], K.bn[:, :]).then_inc(K.var_ready, 1)

    def stats2(s):
        wait(dve, K.rstd_ready, s.n + 1)
        c = Chain(dve, K.var2_step, s.n, 1)
        c.link(nc.vector.tensor_tensor(K.var2a[:, :], K.mv[:, s.par, 1:2], K.rs[:, s.par, 0:1], ALU.mult))
        nc.vector.tensor_tensor(K.var2[:, :], K.var2a[:, :], K.rs[:, s.par, 0:1], ALU.mult).then_inc(K.var2_ready, 1)

    def normalise(s):
        k = s.n + k0
        wait(dve, K.rstd_ready, k + 1)
        wait(dve, K.xT_ready, k)
        if lay == 0:
            nc.vector.tensor_scalar(batch(K.x1, s.n), batch(K.x, s.n), K.mv[:, s.par, 0:1], K.rs[:, s.par, 0:1],
                                    ALU.subtract, ALU.mult).then_inc(K.x1_step, 1)
            wait(dve, K.rstd2_ready, s.n + 1)
            dve.wait_ge(K.x1_step, s.n + 1)
            nc.vector.tensor_scalar(K.xn[:, :], batch(K.x1, s.n), K.rs[:, s.par, 1:2], None,
                                    ALU.mult).then_inc(K.xn_ready, 1)
        else:
            nc.vector.tensor_scalar(K.xn[:, :], batch(K.x, s.n), K.mv[:, s.par, 0:1], K.rs[:, s.par, 0:1],
                                    ALU.subtract, ALU.mult).then_inc(K.xn_ready, 1)

    def keep_qkv(s):
        k = s.n + k0
        wait(dve, K.qkv_ready, k + 1)
        wait(dve, K.v_done, k)
        if lay == 0:
            nc.vector.tensor_copy(K.qkv[:, D:3 * D], K.pP[:, D:3 * D]).then_inc(K.kv_done, 1)
            nc.vector.tensor_scalar(K.qkv[:, 0:D], K.pP[:, 0:D], HD ** -0.5, None, ALU.mult).then_inc(K.q_done, 1)
        else:
            nc.vector.tensor_tensor(K.qkv[:, D:3 * D], K.pP[:, D:3 * D], K.row2(f"bk{lay}", f"bv{lay}"),
                                    ALU.add).then_inc(K.kv_done, 1)
            nc.vector.scalar_tensor_tensor(K.qkv[:, 0:D], K.pP[:, 0:D], HD ** -0.5, K.bqs[:, lay - 1, :], ALU.mult,
                                           ALU.add).then_inc(K.q_done, 1)

    def split_q(s):
        k = s.n + k0
        dve.wait_ge(K.q_done, k + 1)
        wait(dve, K.qt_ready, k)
        q = K.qs[:, :].rearrange("p (h b d) -> p h b d", h=H, b=8)
        c = Chain(dve, K.qsplit_step, k, 3)
        split(c, nc.vector, nc.vector.tensor_copy, K.qs_ready, K.qkv[:, 0:D], q[:, :, 3:6, :], q[:, :, 0:2, :], q[:, :, 2, :])
        c.done()

    def keep_kT(s):
        wait(dve, K.kt_ready, s.n + k0 + 1)
        nc.vector.tensor_copy(K.kt[:, s.par, :, :].rearrange("p j q -> p (j q)"), K.pTb[:, 0:8 * T]).then_inc(K.kt_done, 1)

    def row_max(s, u):
        wait(dve, K.s_ready, 4 * (s.n + k0) + u + 1)
        nc.vector.reduce_max(unit_max(K, u), K.pS[u % 2][:, :].rearrange("p (a k) -> p a k", a=G),
                             AX.X).then_inc(K.smax_done, 1)

    def split_max(s):
        k = s.n + k0
        dve.wait_ge(K.smax_done, 4 * k + 4)
        c = Chain(dve, K.split_step, k, 3)
        c.link(nc.vector.tensor_scalar(K.m3[:, 0:H], K.m[:, :], -1.0, None, ALU.mult))
        c.link(nc.vector.scalar_tensor_tensor(K.mr[:, :], K.m[:, :], -1.0, K.m3[:, 0:H], ALU.mult, ALU.subtract))
        c.link(nc.vector.tensor_copy(K.m3[:, H:2 * H], K.mr[:, :]))
        c.done()
        nc.vector.tensor_tensor(K.m3[:, 2 * H:3 * H], K.mr[:, :], K.m3[:, H:2 * H],
                                ALU.subtract).then_inc(K.m3_ready, 1)

    def normalise_o(s):
        k = s.n + k0
        dve.wait_ge(K.hT_ready, k + 1)
        wait(dve, K.oT_ready, k)
        po = K.pM[:, :].rearrange("p (g d) -> p g d", d=32)
        c = Chain(dve, K.rec_step, k, 1)
        c.link(nc.vector.reciprocal(K.rec[:, :], po[:, :, HD]))
        nc.vector.tensor_tensor(K.on[:, :].rearrange("p (g d) -> p g d", d=HD), po[:, :, 0:HD],
                                K.rec[:, :].unsqueeze(2).to_broadcast([T, H, HD]),
                                ALU.mult).then_inc(K.on_ready, 1)

    def residual(s):
        k = s.n + k0
        wait(dve, K.y_ready, k + 1)
        bias = K.row({0: "bo", 1: "bp1", 2: "bout2"}[lay])
        nc.vector.tensor_tensor(K.yb[:, :], K.pM[:, 0:D], bias, ALU.add).then_inc(K.y_done, 1)
        dve.wait_ge(K.y_done, k + 1)
        if lay == 0:
            c = Chain(dve, K.res_step, s.n, 1)
            c.link(nc.vector.tensor_tensor(batch(K.x1, s.n), batch(K.x1, s.n), K.yb[:, :], ALU.add))
            nc.vector.tensor_tensor(batch(K.x, s.n), batch(K.x, s.n), batch(K.x1, s.n), ALU.add).then_inc(K.x_done, 1)
        else:
            nc.vector.tensor_tensor(batch(K.x, s.n), batch(K.x, s.n), K.yb[:, :], ALU.add).then_inc(K.x_done, 1)

    def body(s):
        a, nx, pr, st = s + 1, s + 2, s + -1, s + 3
        for u in range(4):
            if a.exists():
                row_max(a, u)
            if u == 1 and nx.exists():
                keep_qkv(nx)
                split_q(nx)
            if u == 0 and pr.exists():
                normalise_o(pr)
            if u == 1 and st.exists():
                stats(st)
            if u == 2 and pr.exists():
                residual(pr)
        if lay == 0 and st.exists():
            stats2(st)
        if a.exists():
            split_max(a)
        if nx.exists():
            keep_kT(nx)
        if st.exists():
            normalise(st)

    dve.wait_ge(K.x_done, K.x_before_attn[lay])
    pipeline(dve, body, 3, 1)


def split_weights(nc, pool, K, kind, first, count):
    F = K.ffn[kind]
    if first == 0:
        for sem, n in F.raw:
            pool.wait_ge(sem, n)
    for n in range(first, first + count):
        cut = slice(n * F.chunk, (n + 1) * F.chunk)
        w, hi, lo = F.flat[:, cut], K.w_hi[:, cut], K.w_lo[:, cut]
        nc.gpsimd.tensor_tensor(hi, w, K.one[:, :].to_broadcast([D, F.chunk]), ALU.mult).then_inc(K.w_hi_step, 1)
        pool.wait_ge(K.w_hi_step, 8 * kind + n + 1)
        nc.gpsimd.tensor_tensor(lo, w, hi, ALU.subtract).then_inc(K.w_split, 1)


def attn_pool(nc, pool, K, lay):
    k0 = B * lay

    def copy(out, x):
        one = K.one[:, :]
        while len(one.shape) < len(x.shape):
            one = one.unsqueeze(1)
        return nc.gpsimd.tensor_tensor(out, x, one.to_broadcast(list(x.shape)), ALU.mult)

    def body(s):
        nx = s + 2
        if s.static() and B - 4 <= s.c < B:
            split_weights(nc, pool, K, lay, 2 * (s.c - (B - 4)), 2)
        if not nx.exists():
            return
        k = nx.n + k0
        wait(pool, K.kv_done, k + 1)
        wait(pool, K.kt_ready, k)
        if lay:
            nc.gpsimd.tensor_copy(K.ks[:, :].rearrange("p (h c) -> p h c", h=H)[:, :, 6 * HD],
                                  batch(K.pcol[lay], nx.n).to_broadcast([T, H]))
        kb = K.ks[:, :].rearrange("p (h b w d) -> p h b w d", h=H, b=4, w=2)
        c = Chain(pool, K.ksplit_step, k, 3)
        split(c, nc.gpsimd, copy, K.ks_ready, K.qkv[:, D:2 * D], kb[:, :, 0:3, 0, :], kb[:, :, 0:2, 1, :], kb[:, :, 2, 1, :])
        wait(pool, K.pv_done, 4 * (k - 1))
        copy(K.vaug[:, nx.par, :, 0:HD], K.qkv[:, 2 * D:3 * D].rearrange("p (h d) -> p h d", h=H)).then_inc(K.v_done, 1)

    pipeline(pool, body, 3, 1)



def lin_pe(nc, pe, K):
    def transpose_x(s):
        wait(pe, K.lin_xn_ready, s.n + 1)
        wait(pe, K.lin_xT_done, s.n)
        nc.tensor.transpose(K.pT[:, 0:T], K.xn[:, :], K.ident[:, :]).then_inc(K.lin_xT_ready, 1)

    def project(s):
        wait(pe, K.lin_xT_done, s.n + 1)
        pe.wait_ge(K.ctx_loaded[s.par], 16 * (s.half + 1))
        wait(pe, K.lin_p_done, s.n)
        c = K.ctx[:, s.par, :]
        nc.tensor.matmul(K.pP[:, 0:D], K.xT[:, s.par, :], K.lin_w[:, 0, :], start=True, stop=True)
        nc.tensor.matmul(K.pP[:, D:2 * D], c, K.lin_w[:, 1, :], start=True, stop=True)
        nc.tensor.matmul(K.pP[:, 2 * D:3 * D], c, K.lin_w[:, 2, :], start=True, stop=True).then_inc(K.lin_p_ready, 1)

    def kv(s):
        wait(pe, K.lin_f_ready, s.n + 1)
        wait(pe, K.lin_qT_done, s.n)
        nc.tensor.transpose(K.pC[0][:, 0:T], K.feat[:, s.par, 0, :], K.ident[:, :]).then_inc(K.lin_qT_ready, 1)
        wait(pe, K.lin_kv_done, s.n)
        nc.tensor.matmul(K.pM[:, 0:D + 1], K.feat[:, s.par, 1, :], K.linv[:, s.par, :], start=True,
                         stop=True).then_inc(K.lin_kv_ready, 1)

    def out(s):
        wait(pe, K.lin_qT_done, s.n + 1)
        wait(pe, K.lin_kv_done, s.n + 1)
        wait(pe, K.lin_o_done, s.n)
        nc.tensor.matmul(K.pO[:, 0:D + H], K.lqT[:, :], K.kvblk[:, :], start=True, stop=True).then_inc(K.lin_o_ready, 1)

    pe.wait_ge(K.consts_ready, 1)
    pe.wait_ge(K.consts_loaded, 16)

    def body(s):
        nx = s + 2
        if s.exists():
            kv(s)
        if nx.exists():
            transpose_x(nx)
            project(nx)
        if s.exists():
            out(s)

    pipeline(pe, body, 3, 0)


def lin_act(nc, act, K):
    def rstd(s):
        wait(act, K.lin_var_ready, s.n + 1)
        c = Chain(act, K.lin_rstd_step, s.n, 1)
        c.link(nc.scalar.activation(K.lnv[:, 0:1], K.mv[:, s.par, 1:2], ACT.Ln, bias=K.eps[:, :]))
        nc.scalar.activation(K.rs[:, s.par, 0:1], K.lnv[:, 0:1], ACT.Exp, scale=-0.5).then_inc(K.lin_rstd_ready, 1)

    def keep_xT(s):
        wait(act, K.lin_xT_ready, s.n + 1)
        nc.scalar.copy(K.xT[:, s.par, :], K.pT[:, 0:T]).then_inc(K.lin_xT_done, 1)

    def keep_qT(s):
        wait(act, K.lin_qT_ready, s.n + 1)
        nc.scalar.copy(K.lqT[:, :], K.pC[0][:, 0:T]).then_inc(K.lin_qT_done, 1)

    def ratio(s):
        wait(act, K.lin_ratio_ready, s.n + 1)
        c = Chain(act, K.lin_root_step, s.n, 1)
        c.link(nc.scalar.activation(K.lnr[:, :], K.fr[:, :], ACT.Ln))
        nc.scalar.activation(K.froot[:, :], K.lnr[:, :], ACT.Exp, scale=0.5).then_inc(K.lin_root_ready, 1)
        act.wait_ge(K.lin_root_ready, s.n + 1)
        for n in range(2):
            op = nc.scalar.activation(K.feat[:, s.par, n, :], K.f3[:, n, :], ACT.Identity, scale=K.froot[:, n:n + 1])
        op.then_inc(K.lin_f_ready, 1)

    def body(s):
        a, nx, st = s + 1, s + 2, s + 3
        if s.exists():
            keep_qT(s)
        if nx.exists():
            keep_xT(nx)
        if a.exists():
            ratio(a)
        if st.exists():
            rstd(st)

    pipeline(act, body, 3, 0)


def lin_dve(nc, dve, K):
    def stats(s):
        if s.static() and s.c in (0, GB):
            dve.wait_ge(K.x_loaded[s.c // GB], 16)
        c = Chain(dve, K.lin_stat_step, s.n, 1)
        c.link(nc.vector.bn_stats(K.bn[:, :], batch(K.x, s.n)))
        nc.vector.memset(K.spare[:, :], 0.0)
        nc.vector.bn_aggr(K.mv[:, s.par, :], K.bn[:, :]).then_inc(K.lin_var_ready, 1)

    def normalise(s):
        wait(dve, K.lin_rstd_ready, s.n + 1)
        wait(dve, K.lin_xT_ready, s.n)
        nc.vector.tensor_scalar(K.xn[:, :], batch(K.x, s.n), K.mv[:, s.par, 0:1], K.rs[:, s.par, 0:1],
                                ALU.subtract, ALU.mult).then_inc(K.lin_xn_ready, 1)

    def features(s):
        wait(dve, K.lin_p_ready, s.n + 1)
        qk = K.pP[:, 0:2 * D].rearrange("p (a d) -> p a d", a=2)
        c = Chain(dve, K.lin_f_step, s.n, 5)
        two = [T, 2, D]
        c.link(nc.vector.tensor_tensor(K.ft[:, :, :], qk, K.row2("bq0", "bk0").rearrange("p (a d) -> p a d", a=2), ALU.add))
        nc.vector.tensor_tensor(K.linv[:, s.par, 0:D], K.pP[:, 2 * D:3 * D], K.row("bv0"), ALU.add).then_inc(K.lin_p_done, 1)
        c.link(nc.vector.scalar_tensor_tensor(K.ft[:, :, :], K.ft[:, :, :], 0.0,
                                              K.epsr[:, :].unsqueeze(1).to_broadcast(two), ALU.max, ALU.add))
        for n in range(2):
            op = nc.vector.scalar_tensor_tensor(K.f2[:, n, :], K.ft[:, n, :], 1.0, K.ft[:, n, :], ALU.mult, ALU.mult,
                                                accum_out=K.fs[:, n:n + 1])
        c.link(op)
        wait(dve, K.lin_f_ready, s.n)
        c.link(nc.vector.tensor_tensor(K.f3[:, :, :], K.f2[:, :, :], K.ft[:, :, :], ALU.mult))
        for n in range(2):
            op = nc.vector.scalar_tensor_tensor(K.ft[:, n, :], K.f3[:, n, :], 1.0, K.f3[:, n, :], ALU.mult, ALU.mult,
                                                accum_out=K.fs[:, 2 + n:3 + n])
        c.link(op)
        c.done()
        c = Chain(dve, K.lin_r_step, s.n, 1)
        c.link(nc.vector.reciprocal(K.fs[:, 2:4], K.fs[:, 2:4]))
        nc.vector.tensor_tensor(K.fr[:, :], K.fs[:, 0:2], K.fs[:, 2:4], ALU.mult).then_inc(K.lin_ratio_ready, 1)

    def within_heads(s):
        wait(dve, K.lin_kv_ready, s.n + 1)
        nc.vector.tensor_tensor(K.kvblk[:, 0:D], K.pM[:, 0:D], K.blockmask[:, :], ALU.mult)
        nc.vector.tensor_scalar(K.kvblk[:, D:D + H], K.headmask[:, :], K.pM[:, D:D + 1], None,
                                ALU.mult).then_inc(K.lin_kv_done, 1)

    def residual(s):
        wait(dve, K.lin_o_ready, s.n + 1)
        c = Chain(dve, K.lin_o_step, s.n, 2)
        c.link(nc.vector.tensor_scalar(K.rec[:, :], K.pO[:, D:D + H], 1e-6, None, ALU.add))
        c.link(nc.vector.reciprocal(K.rec[:, :], K.rec[:, :]))
        nc.vector.tensor_tensor(K.yb[:, :].rearrange("p (h d) -> p h d", h=H),
                                K.pO[:, 0:D].rearrange("p (h d) -> p h d", h=H),
                                K.rec[:, :].unsqueeze(2).to_broadcast([T, H, HD]), ALU.mult).then_inc(K.lin_o_done, 1)
        dve.wait_ge(K.lin_o_done, s.n + 1)
        nc.vector.tensor_tensor(batch(K.x, s.n), batch(K.x, s.n), K.yb[:, :], ALU.add).then_inc(K.x_done, 1)


    def body(s):
        a, nx, st = s + 1, s + 2, s + 3
        if nx.exists():
            normalise(nx)
        if a.exists():
            features(a)
        if s.exists():
            within_heads(s)
        if st.exists():
            stats(st)
        if s.exists():
            residual(s)

    pipeline(dve, body, 3, 0)



def groups(eng, body):
    body(0, True)
    with eng.Fori(1, B // GB - 1) as g:
        body(g, True)
    body(B // GB - 1, False)


def ffn_pe(nc, pe, K, kind):
    F = K.ffn[kind]
    NE, HB = F.experts, F.blocks

    def transpose_x(g):
        wait(pe, F.xn_ready, g + 1)
        wait(pe, F.xh_ready, g)
        for b in range(GB):
            mm = nc.tensor.transpose(K.pT[:, b * T:(b + 1) * T], K.xg[:, b, :], K.ident[:, :])
        mm.then_inc(F.xT_ready.sem, 1)

    def logits(g):
        wait(pe, F.xT_done, g + 1)
        if NE == 1:
            return
        wait(pe, F.w_ready, g)
        if kind:
            wait(pe, F.wT_done, g)
        for b in range(GB):
            mm = nc.tensor.matmul(K.pP[:, b * E:(b + 1) * E], K.xTg[:, b * T:(b + 1) * T], F.gate, start=True, stop=True)
        mm.then_inc(F.l_ready.sem, 1)

    def product(bank, w_hi, w_lo, e, hb):
        cut = slice(hb * T, (hb + 1) * T)
        nc.tensor.matmul(bank[:, :], w_lo[:, e, cut], K.xh[:, :], start=True, stop=False)
        nc.tensor.matmul(bank[:, :], w_hi[:, e, cut], K.xh[:, :], start=False, stop=False)
        return nc.tensor.matmul(bank[:, :], w_hi[:, e, cut], K.xl[:, :], start=False, stop=True)

    def hidden(g, e):
        if e == 0:
            wait(pe, F.xl_ready, g + 1)
        for hb in range(HB):
            v = e * HB + hb
            if kind in (1, 2):
                wait(pe, F.h_done, g * (NE * HB) + max(v - 3, 0))
                product(K.pH[v % 4], F.w1_hi, F.w1_lo, e, hb).then_inc(F.h_ready.sem, 1)
            else:
                for q, w_hi, w_lo, free in ((0, F.w1_hi, F.w1_lo, F.silu_done), (1, F.w2_hi, F.w2_lo, F.h_done)):
                    wait(pe, free, g * (NE * HB) + max(v - 1, 0))
                    product(K.pH[2 * (v % 2) + q], w_hi, w_lo, e, hb).then_inc((F.a_ready, F.b_ready)[q].sem, 1)

    def weights_T(g):
        wait(pe, F.w_ready, g + 1)
        for b in range(GB):
            mm = nc.tensor.transpose(K.pP[0:E, b * T:(b + 1) * T], K.wts[:, b, :], K.ident[:, :])
        mm.then_inc(F.wT_ready.sem, 1)

    def down(g, e):
        wait(pe, F.h_done, g * (NE * HB) + (e + 1) * HB)
        wait(pe, F.acc_done, g * F.ys + max(e - 1, 0))
        bank = K.pY[e % 2]
        for b in range(GB):
            for hb in range(HB):
                mm = nc.tensor.matmul(bank[:, b * T:(b + 1) * T], K.hT[:, e % 2, hb, b * T:(b + 1) * T],
                                      F.w3[:, e, hb, :], start=(hb == 0), stop=(hb == HB - 1))
        mm.then_inc(F.y_ready.sem, 1)

    def down_bias(g):
        wait(pe, F.wT_done, g + 1)
        wait(pe, F.acc_done, g * F.ys + NE - 1)
        for b in range(GB):
            mm = nc.tensor.matmul(K.pY[0][:, b * T:(b + 1) * T], K.wT[:, b * T:(b + 1) * T], F.b2, start=True, stop=True)
        mm.then_inc(F.y_ready.sem, 1)

    for sem, count in F.loaded:
        pe.wait_ge(sem, count)
    transpose_x(0)
    logits(0)

    def body(g, more):
        hidden(g, 0)
        for e in range(NE):
            if e + 1 < NE:
                hidden(g, e + 1)
            if e == 0 and kind in (1, 2):
                weights_T(g)
            if e == NE - 1 and more:
                transpose_x(g + 1)
            down(g, e)
        if kind in (1, 2):
            down_bias(g)
        if more:
            logits(g + 1)

    groups(pe, body)


def ffn_act(nc, act, K, kind):
    F = K.ffn[kind]
    NE, HB = F.experts, F.blocks

    def rstd(g):
        wait(act, F.var_ready, g + 1)
        c = Chain(act, F.rstd_step, g, 1)
        c.link(nc.scalar.activation(K.lng[:, :], K.mvg[:, :, 1], ACT.Ln, bias=K.eps[:, :]))
        nc.scalar.activation(K.rsg[:, :], K.lng[:, :], ACT.Exp, scale=-0.5).then_inc(F.rstd_ready.sem, 1)

    def keep_xT(g):
        wait(act, F.xT_ready, g + 1)
        for dst, done in ((K.xTg, F.xT_done), (K.xh, F.xh_ready)):
            if kind == 0:
                op = nc.scalar.activation(dst[:, :], K.pT[:, :], ACT.Identity, scale=K.col("ln2_s"), bias=K.col("ln2_b"))
            else:
                op = nc.scalar.copy(dst[:, :], K.pT[:, :])
            op.then_inc(done.sem, 1)

    def gate_exp(g):
        wait(act, F.d_ready, g + 1)
        n = GB if kind == 0 else GB * E
        nc.scalar.activation(K.ge[:, 0:n], K.gd[:, 0:n], ACT.Exp).then_inc(F.e_ready.sem, 1)

    def keep_wT(g):
        wait(act, F.wT_ready, g + 1)
        nc.scalar.copy(K.wT[:, :], K.pP[0:E, :]).then_inc(F.wT_done.sem, 1)

    def hidden(g, e):
        for hb in range(HB):
            v = e * HB + hb
            u = g * (NE * HB) + v
            if kind in (1, 2):
                wait(act, F.h_ready, u + 1)
                if hb == 0:
                    wait(act, F.y_ready, g * F.ys + max(e - 1, 0))
                nc.scalar.activation(K.hT[:, e % 2, hb, :], K.pH[v % 4][:, :], ACT.Relu,
                                     bias=F.b1[:, v:v + 1]).then_inc(F.h_done.sem, 1)
            else:
                wait(act, F.a_ready, u + 1)
                wait(act, F.h_done, g * (NE * HB) + max(v - 1, 0))
                nc.scalar.activation(K.silu[:, v % 2, :], K.pH[2 * (v % 2)][:, :], ACT.Silu,
                                     scale=F.scale).then_inc(F.silu_done.sem, 1)

    act.preload_act_table_set(LN_EXP)
    rstd(0)
    keep_xT(0)

    def body(g, more):
        if NE > 1:
            gate_exp(g)
        for e in range(NE):
            hidden(g, e)
            if e == 1 and kind in (1, 2):
                keep_wT(g)
        if more:
            if kind in (0, 3):
                act.preload_act_table_set(LN_EXP)
            rstd(g + 1)
            keep_xT(g + 1)

    groups(act, body)
    if kind in (0, 3):
        act.preload_act_table_set(LN_EXP)


def ffn_dve(nc, dve, K, kind):
    F = K.ffn[kind]
    NE, HB = F.experts, F.blocks
    src = K.x1 if kind == 0 else K.x
    f4 = [T, GB, E]

    def stats(g):
        c = Chain(dve, F.stat_step, g, 1)
        for b in range(GB):
            op = nc.vector.bn_stats(K.bng[:, b, :], batch(src, g * GB + b))
        c.link(op)
        nc.vector.memset(K.spare[:, :], 0.0)
        for b in range(GB):
            op = nc.vector.bn_aggr(K.mvg[:, b, :], K.bng[:, b, :])
        op.then_inc(F.var_ready.sem, 1)

    def normalise(g):
        wait(dve, F.rstd_ready, g + 1)
        wait(dve, F.xT_ready, g)
        for b in range(GB):
            op = nc.vector.tensor_scalar(K.xg[:, b, :], batch(src, g * GB + b), K.mvg[:, b, 0:1], K.rsg[:, b:b + 1],
                                         ALU.subtract, ALU.mult)
        op.then_inc(F.xn_ready.sem, 1)

    def split_x(g):
        wait(dve, F.xh_ready, g + 1)
        nc.vector.tensor_tensor(K.xl[:, :], K.xTg[:, :], K.xh[:, :], ALU.subtract).then_inc(F.xl_ready.sem, 1)

    def first_max(c, onehot):
        c.link(nc.vector.reduce_max(K.gm[:, :], K.gl[:, :, :], AX.X))
        c.link(nc.vector.tensor_tensor(onehot, K.gl[:, :, :], K.gm[:, :].unsqueeze(2).to_broadcast(f4), ALU.is_equal))
        c.link(nc.vector.tensor_tensor(onehot, onehot, K.desc[:, :].unsqueeze(1).to_broadcast(f4), ALU.mult))
        c.link(nc.vector.reduce_max(K.gi[:, :], onehot, AX.X))
        c.link(nc.vector.tensor_tensor(onehot, onehot, K.gi[:, :].unsqueeze(2).to_broadcast(f4), ALU.is_equal))

    def gating(g):
        wait(dve, F.l_ready, g + 1)
        pl = K.pP[:, 0:GB * E].rearrange("p (b e) -> p b e", b=GB)
        c = Chain(dve, F.gate_step, g, 17 if kind == 0 else 8)
        if kind == 0:
            c.link(nc.vector.tensor_copy(K.gl[:, :, :], pl))
            first_max(c, K.g1[:, :, :])
            c.link(nc.vector.tensor_copy(K.gm1[:, :], K.gm[:, :]))
            c.link(nc.vector.scalar_tensor_tensor(K.gl[:, :, :], K.g1[:, :, :], NEG, K.gl[:, :, :], ALU.mult, ALU.add))
            first_max(c, K.g2[:, :, :])
            nc.vector.tensor_tensor(K.gd[:, 0:GB], K.gm[:, :], K.gm1[:, :], ALU.subtract).then_inc(F.d_ready.sem, 1)
            wait(dve, F.e_ready, g + 1)
            c.link(nc.vector.tensor_scalar(K.gs[:, :], K.ge[:, 0:GB], 1.0, None, ALU.add))
            c.link(nc.vector.reciprocal(K.gs[:, :], K.gs[:, :]))
            c.link(nc.vector.tensor_tensor(K.g2[:, :, :], K.g2[:, :, :], K.ge[:, 0:GB].unsqueeze(2).to_broadcast(f4), ALU.mult))
            c.link(nc.vector.tensor_tensor(K.g2[:, :, :], K.g2[:, :, :], K.g1[:, :, :], ALU.add))
            nc.vector.tensor_tensor(K.wts[:, :, :], K.g2[:, :, :], K.gs[:, :].unsqueeze(2).to_broadcast(f4),
                                    ALU.mult).then_inc(F.w_ready.sem, 1)
        else:
            bg = K.row({1: "bg1", 2: "br2"}[kind]).unsqueeze(1).to_broadcast(f4)
            c.link(nc.vector.tensor_tensor(K.gl[:, :, :], pl, bg, ALU.add))
            first_max(c, K.g1[:, :, :])
            nc.vector.tensor_tensor(K.gd[:, :].rearrange("p (b e) -> p b e", b=GB), K.gl[:, :, :],
                                    K.gm[:, :].unsqueeze(2).to_broadcast(f4), ALU.subtract).then_inc(F.d_ready.sem, 1)
            wait(dve, F.e_ready, g + 1)
            c.link(nc.vector.reduce_sum(K.gs[:, :], K.ge[:, :].rearrange("p (b e) -> p b e", b=GB), AX.X))
            c.link(nc.vector.reciprocal(K.gs[:, :], K.gs[:, :]))
            nc.vector.tensor_tensor(K.wts[:, :, :], K.g1[:, :, :], K.gs[:, :].unsqueeze(2).to_broadcast(f4),
                                    ALU.mult).then_inc(F.w_ready.sem, 1)
        c.done()
        wait(dve, F.w_ready, g + 1)

    def product(g, e):
        for hb in range(HB):
            v = e * HB + hb
            u = g * (NE * HB) + v
            wait(dve, F.silu_done, u + 1)
            wait(dve, F.b_ready, u + 1)
            if hb == 0:
                wait(dve, F.y_ready, g * F.ys + max(e - 1, 0))
            if F.scale == 1.0:
                op = nc.vector.tensor_tensor(K.hT[:, e % 2, hb, :], K.silu[:, v % 2, :], K.pH[2 * (v % 2) + 1][:, :],
                                             ALU.mult)
            else:
                op = nc.vector.scalar_tensor_tensor(K.hT[:, e % 2, hb, :], K.pH[2 * (v % 2) + 1][:, :], F.scale,
                                                    K.silu[:, v % 2, :], ALU.mult, ALU.mult)
            op.then_inc(F.h_done.sem, 1)

    def add_up(g, e):
        y = g * F.ys + e
        wait(dve, F.y_ready, y + 1)
        wait(dve, F.acc_done, y)
        bank = K.pY[e % 2]
        for b in range(GB):
            xb = batch(K.x, g * GB + b)
            if NE > 1 and e < NE:
                op = nc.vector.scalar_tensor_tensor(xb, bank[:, b * T:(b + 1) * T], K.wts[:, b, e:e + 1], xb,
                                                    ALU.mult, ALU.add)
            else:
                op = nc.vector.tensor_tensor(xb, bank[:, b * T:(b + 1) * T], xb, ALU.add)
        op.then_inc(F.acc_done.sem, 1)

    dve.wait_ge(K.x_done, K.x_before_ffn[kind])
    stats(0)
    normalise(0)

    def body(g, more):
        split_x(g)
        if NE > 1:
            gating(g)
        for e in range(NE):
            if kind in (0, 3):
                product(g, e)
            if e == max(NE - 2, 0) and more:
                stats(g + 1)
            if e == NE - 1 and more:
                normalise(g + 1)
            if e:
                add_up(g, e - 1)
        add_up(g, NE - 1)
        if kind in (1, 2):
            add_up(g, NE)

    groups(dve, body)
    wait(dve, F.acc_done, (B // GB) * F.ys)
    dve.sem_inc(K.x_done, 1)



class Uses:

    ORDER = [("xT", 2), ("oT0", -1), ("oT1", -1), ("Q0", 2), ("Q1", 2), ("K0", 2), ("K1", 2), ("y", -1),
             ("QT0", 2), ("QT1", 2), ("V0", 1), ("V1", 1), ("m", 1), ("KT0", 2), ("KT1", 2)]

    def __init__(self):
        self.total, self.looped = 0, None

    def of(self, s):
        n = len(self.ORDER)
        if s.static():
            if self.looped is not None:
                self.total, self.looped = self.looped + n * 2 * ((B - 3 - 2) // 2), None
            start = self.total
        else:
            if self.looped is None:
                self.looped = self.total
            base = self.looped + n * (s.c - 2)
            start = s.i * (2 * n) + base
        names = [name for name, d in self.ORDER if (s + d).exists()]
        at = {name: start + j for j, name in enumerate(names)}
        even = self.total if s.static() else base
        self.bank = {name: (even + j) % 2 for j, name in enumerate(names)}
        if s.static():
            self.total += len(names)
        self.at, self.start = at, start
        return at


def attn3_pe(nc, pe, K):
    uses = Uses()

    def free(name):
        wait(pe, K.a_done, uses.at[name] - 1)
        return K.pA[uses.bank[name]]

    def transpose_x(s):
        wait(pe, K.l3_xn_ready, s.n + 1)
        nc.tensor.transpose(free("xT")[:, 0:T], K.xn[:, :], K.ident[:, :]).then_inc(K.a_ready, 1)

    def project(s, which):
        src = (K.xT, K.ctx, K.ctx_v)[which][:, s.par, :]
        if which == 0:
            wait(pe, K.a_done, uses.at["xT"] + 1)
        if which == 1:
            pe.wait_ge(K.ctx_loaded[s.par], 16 * (s.half + 1 + (B // 2) * 3))
        if which == 2:
            pe.wait_ge(K.ctx_v_loaded[s.par], 16 * (s.half + 1))
        for half in range(2):
            op = nc.tensor.matmul(free(f"{'QKV'[which]}{half}")[:, :], src,
                                  K.w3qkv[:, which, half * 512:(half + 1) * 512], start=True, stop=True)
            op.then_inc(K.a_ready, 1)

    def transpose_qk(s, which):
        wait(pe, (K.q3n_ready, K.k3n_ready)[which], s.n + 1)
        for half in range(2):
            bank = free(f"{'QK'[which]}T{half}")
            for j in range(4):
                jj = half * 4 + j
                op = nc.tensor.transpose(bank[:, j * T:(j + 1) * T], K.qk3n[:, which, jj * T:(jj + 1) * T], K.ident[:, :])
            op.then_inc(K.a_ready, 1)

    def row_scores(s, u):
        if u == 0:
            wait(pe, K.a_done, uses.start)
        wait(pe, K.s3_done, 4 * s.n + u - 1)
        r = slice(64 * (u % 2), 64 * (u % 2) + 64)
        for a in range(4):
            j = 4 * (u // 2) + a
            op = nc.tensor.matmul(K.pS[u % 2][:, a * T:(a + 1) * T], K.q3T[r, s.par, j, :], K.k3T[r, s.par, j, :],
                                  start=True, stop=True)
        op.then_inc(K.s3_ready, 1)

    def transpose_max(s):
        wait(pe, K.m33_ready, s.n + 1)
        nc.tensor.transpose(free("m")[:, :].bitcast(BF16)[:, 0:T], K.m3[:, :], K.identb[:, :]).then_inc(K.a_ready, 1)

    def col_scores(s, u):
        if u == 0:
            wait(pe, K.a_done, uses.start - (2 if (s + 1).exists() else 0))
        wait(pe, K.exp3_done, 4 * s.n + u - 1)
        r = slice(64 * (u % 2), 64 * (u % 2) + 64)
        bank = K.pC[u % 2]
        for a in range(4):
            j = 4 * (u // 2) + a
            nc.tensor.matmul(bank[:, a * T:(a + 1) * T], K.k3T[r, s.par, j, :], K.q3T[r, s.par, j, :],
                             start=(a == 0), stop=False, skip_group_check=True)
        for a in range(4):
            h = 2 * (4 * (u // 2) + a) + u % 2
            op = nc.tensor.matmul(bank[:, a * T:(a + 1) * T], K.sel[:, h, :], K.mT[:, :], start=False, stop=(a == 3),
                                  skip_group_check=True)
        op.then_inc(K.c3_ready, 1)

    def probs_v(s, u):
        wait(pe, K.exp3_done, 4 * s.n + u + 1)
        wait(pe, K.on3_done, 4 * s.n + u - 1)
        for a in range(4):
            h = 2 * (4 * (u // 2) + a) + u % 2
            op = nc.tensor.matmul(K.pO3[u % 2][:, a * (HD3 + 1):(a + 1) * (HD3 + 1)], K.pt[:, u % 2, a * T:(a + 1) * T],
                                  K.v3[:, s.par, h, :], start=True, stop=True)
        op.then_inc(K.pv3_done, 1)

    def transpose_o(s):
        wait(pe, K.on3_done, 4 * s.n + 4)
        for half in range(2):
            bank = free(f"oT{half}")
            for j in range(4):
                jj = half * 4 + j
                op = nc.tensor.transpose(bank[:, j * T:(j + 1) * T], K.on3[:, jj * T:(jj + 1) * T], K.ident[:, :])
            op.then_inc(K.a_ready, 1)

    def out_project(s):
        wait(pe, K.a_done, uses.at["oT1"] + 1)
        bank = free("y")
        for j in range(8):
            op = nc.tensor.matmul(bank[:, 0:D], K.o3T[:, j, :], K.wu[:, j, :], start=(j == 0), stop=(j == 7))
        op.then_inc(K.a_ready, 1)

    pe.wait_ge(K.w3_loaded, 64)
    pe.wait_ge(K.w3_centred, 2)

    def body(s):
        uses.of(s)
        a, nx, pr = s + 1, s + 2, s + -1
        for u in range(4):
            if s.exists():
                col_scores(s, u)
            if u == 0 and nx.exists():
                transpose_x(nx)
            if u == 0 and pr.exists():
                transpose_o(pr)
            if a.exists():
                row_scores(a, u)
            if u == 0 and nx.exists():
                project(nx, 0)
                project(nx, 1)
            if u >= 1 and s.exists():
                probs_v(s, u - 1)
            if u == 1 and pr.exists():
                out_project(pr)
        if nx.exists():
            transpose_qk(nx, 0)
        if s.exists():
            probs_v(s, 3)
        if a.exists():
            project(a, 2)
            transpose_max(a)
        if nx.exists():
            transpose_qk(nx, 1)

    pipeline(pe, body, 3, 1)


def attn3_act(nc, act, K):
    uses = Uses()

    def taken(name):
        wait(act, K.a_ready, uses.at[name] + 1)
        return K.pA[uses.bank[name]]

    def rstd(s):
        wait(act, K.l3_var_ready, s.n + 1)
        c = Chain(act, K.l3_rstd_step, s.n, 1)
        c.link(nc.scalar.activation(K.lnv[:, 0:1], K.mv[:, s.par, 1:2], ACT.Ln, bias=K.eps[:, :]))
        nc.scalar.activation(K.rs[:, s.par, 0:1], K.lnv[:, 0:1], ACT.Exp, scale=-0.5).then_inc(K.l3_rstd_ready, 1)

    def keep_qk(s, which):
        if which == 0:
            wait(act, K.k3n_ready, s.n)
        for half in range(2):
            nc.scalar.copy(K.qk3[:, which, half * 512:(half + 1) * 512],
                           taken(f"{'QK'[which]}{half}")[:, :]).then_inc(K.a_done, 1)

    def keep_v(s):
        for half in range(2):
            nc.scalar.copy(K.v3[:, s.par, half * 8:(half + 1) * 8, 0:HD3],
                           taken(f"V{half}")[:, :].rearrange("p (h d) -> p h d", h=8)).then_inc(K.a_done, 1)

    def head_rstd(s):
        wait(act, K.ss_ready, 2 * s.n + 2)
        c = Chain(act, K.l3_hr_step, s.n, 1)
        c.link(nc.scalar.activation(K.lnh[:, :], K.ss[:, :], ACT.Ln, bias=K.eps[:, :], scale=1.0 / HD3))
        nc.scalar.activation(K.rh[:, :], K.lnh[:, :], ACT.Exp, scale=-0.5).then_inc(K.rh_ready, 1)

    def keep_qkT(s, which):
        dst = (K.q3T, K.k3T)[which]
        w, b = ((K.qn8[:, 0:1], K.qn8[:, 1:2]), (K.col("kn_w"), K.col("kn_b")))[which]
        for half in range(2):
            nc.scalar.activation(dst[:, s.par, half * 4:(half + 1) * 4, :].rearrange("p a q -> p (a q)"),
                                 taken(f"{'QK'[which]}T{half}")[:, :], ACT.Identity, scale=w, bias=b).then_inc(K.a_done, 1)

    def exp(s, u):
        wait(act, K.c3_ready, 4 * s.n + u + 1)
        wait(act, K.pv3_done, 4 * s.n + u - 1)
        nc.scalar.activation(K.pt[:, u % 2, :], K.pC[u % 2][:, :], ACT.Exp).then_inc(K.exp3_done, 1)

    def keep_oT(s):
        for half in range(2):
            nc.scalar.copy(K.o3T[:, half * 4:(half + 1) * 4, :].rearrange("p a q -> p (a q)"),
                           taken(f"oT{half}")[:, :]).then_inc(K.a_done, 1)

    def body(s):
        uses.of(s)
        a, nx, pr, st = s + 1, s + 2, s + -1, s + 3
        for u in range(4):
            if s.exists():
                exp(s, u)
            if u == 0 and nx.exists():
                nc.scalar.copy(K.xT[:, nx.par, :], taken("xT")[:, 0:T]).then_inc(K.a_done, 1)
            if u == 0 and pr.exists():
                keep_oT(pr)
            if u == 0 and nx.exists():
                keep_qk(nx, 0)
                keep_qk(nx, 1)
            if u == 1 and pr.exists():
                wait(act, K.x3_done, pr.n)
                nc.scalar.copy(K.yb[:, :], taken("y")[:, 0:D]).then_inc(K.a_done, 1)
            if u == 2 and st.exists():
                rstd(st)
            if u == 2 and nx.exists():
                head_rstd(nx)
        if nx.exists():
            keep_qkT(nx, 0)
        if a.exists():
            keep_v(a)
            nc.scalar.copy(K.mT[:, :], taken("m")[:, :].bitcast(BF16)[:, 0:T]).then_inc(K.a_done, 1)
        if nx.exists():
            keep_qkT(nx, 1)

    pipeline(act, body, 3, 1)


def attn3_dve(nc, dve, K):
    uses = Uses()

    def stats(s):
        c = Chain(dve, K.l3_stat_step, s.n, 1)
        c.link(nc.vector.bn_stats(K.bn[:, :], batch(K.x, s.n)))
        nc.vector.memset(K.spare[:, :], 0.0)
        nc.vector.bn_aggr(K.mv[:, s.par, :], K.bn[:, :]).then_inc(K.l3_var_ready, 1)

    def normalise(s):
        wait(dve, K.l3_rstd_ready, s.n + 1)
        nc.vector.tensor_scalar(K.xn[:, :], batch(K.x, s.n), K.mv[:, s.par, 0:1], K.rs[:, s.par, 0:1],
                                ALU.subtract, ALU.mult).then_inc(K.l3_xn_ready, 1)

    def row_max(s, u):
        wait(dve, K.s3_ready, 4 * s.n + u + 1)
        out = K.m[:, :].rearrange("p (j a b) -> p j a b", j=2, a=4)[:, u // 2, :, u % 2]
        nc.vector.reduce_max(out, K.pS[u % 2][:, :].rearrange("p (a k) -> p a k", a=4), AX.X).then_inc(K.s3_done, 1)

    def split_max(s):
        dve.wait_ge(K.s3_done, 4 * s.n + 4)
        c = Chain(dve, K.l3_split_step, s.n, 3)
        c.link(nc.vector.tensor_scalar(K.m3[:, 0:H], K.m[:, :], -1.0, None, ALU.mult))
        c.link(nc.vector.scalar_tensor_tensor(K.mr[:, :], K.m[:, :], -1.0, K.m3[:, 0:H], ALU.mult, ALU.subtract))
        c.link(nc.vector.tensor_copy(K.m3[:, H:2 * H], K.mr[:, :]))
        nc.vector.tensor_tensor(K.m3[:, 2 * H:3 * H], K.mr[:, :], K.m3[:, H:2 * H],
                                ALU.subtract).then_inc(K.m33_ready, 1)

    def normalise_o(s, u):
        wait(dve, K.pv3_done, 4 * s.n + u + 1)
        po = K.pO3[u % 2][:, 0:4 * (HD3 + 1)].rearrange("p (a d) -> p a d", a=4)
        out = K.on3[:, :].rearrange("p (j a b d) -> p j a b d", j=2, a=4, b=2)[:, u // 2, :, u % 2, :]
        c = Chain(dve, K.l3_rec_step, 4 * s.n + u, 1)
        rec = K.rec[:, 4 * (u % 2):4 * (u % 2) + 4]
        c.link(nc.vector.reciprocal(rec, po[:, :, HD3]))
        nc.vector.tensor_tensor(out, po[:, :, 0:HD3], rec.unsqueeze(2).to_broadcast([T, 4, HD3]),
                                ALU.mult).then_inc(K.on3_done, 1)

    def squares(s, which):
        wait(dve, K.sq_ready, 2 * s.n + which + 1)
        nc.vector.reduce_sum(K.ss[:, which * H:(which + 1) * H], K.sq3[:, which, :].rearrange("p (h d) -> p h d", d=HD3),
                             AX.X).then_inc(K.ss_ready, 1)

    def head_norm(s, which):
        if which == 0:
            wait(dve, K.rh_ready, s.n + 1)
        op = nc.vector.tensor_tensor(K.qk3n[:, which, :].rearrange("p (h d) -> p h d", h=H),
                                     K.qk3[:, which, :].rearrange("p (h d) -> p h d", h=H),
                                     K.rh[:, which * H:(which + 1) * H].unsqueeze(2).to_broadcast([T, H, HD3]), ALU.mult)
        op.then_inc((K.q3n_ready, K.k3n_ready)[which], 1)

    def residual(s):
        wait(dve, K.a_done, uses.at["y"] + 1)
        c = Chain(dve, K.l3_res_step, s.n, 1)
        c.link(nc.vector.tensor_tensor(K.y3[:, :], K.yb[:, :], K.row("bu3"), ALU.add))
        nc.vector.tensor_tensor(batch(K.x, s.n), batch(K.x, s.n), K.y3[:, :], ALU.add).then_inc(K.x3_done, 1)

    dve.wait_ge(K.x_done, K.x_before_attn[3])

    def body(s):
        uses.of(s)
        a, nx, pr, st = s + 1, s + 2, s + -1, s + 3
        if nx.exists():
            normalise(nx)
        for u in range(4):
            if u == 3 and nx.exists():
                head_norm(nx, 0)
            if a.exists():
                row_max(a, u)
            if u >= 1 and s.exists():
                normalise_o(s, u - 1)
            if u == 1 and st.exists():
                stats(st)
            if u in (1, 2) and nx.exists():
                squares(nx, u - 1)
            if u == 2 and pr.exists():
                residual(pr)
        if a.exists():
            split_max(a)
        if nx.exists():
            head_norm(nx, 1)
        if s.exists():
            normalise_o(s, 3)

    pipeline(dve, body, 3, 1)
    dve.wait_ge(K.x3_done, B)
    dve.sem_inc(K.x_done, 1)


def attn3_pool(nc, pool, K):
    uses = Uses()

    def body(s):
        uses.of(s)
        if s.static() and s.c == B - 1:
            split_weights(nc, pool, K, 3, 0, 2)
        if (s + 2).exists():
            for which in range(2):
                wait(pool, K.a_done, uses.at[("Q1", "K1")[which]] + 1)
                nc.gpsimd.tensor_tensor(K.sq3[:, which, :], K.qk3[:, which, :], K.qk3[:, which, :],
                                        ALU.mult).then_inc(K.sq_ready, 1)

    pipeline(pool, body, 3, 1)



CONSTS = [("ident", T), ("blockmask", T), ("headmask", H), ("desc", E), ("selc", H), ("causal", T),
          ("causalT", T)]
NCONST = sum(w for _, w in CONSTS)
CONST_AT = {}
_at = 0
for _n, _w in CONSTS:
    CONST_AT[_n] = slice(_at, _at + _w)
    _at += _w


def setup_dve(nc, dve, K):
    def const(name):
        return K.consts[:, CONST_AT[name]]

    nc.vector.memset(K.eps[:, :], EPS)
    nc.vector.memset(K.one[:, :], 1.0)
    nc.vector.memset(K.zeros[:, :], 0.0)
    nc.vector.memset(K.vaug[:, :, :, HD + 1:], 0.0)
    nc.vector.memset(K.vaug[:, :, :, HD:HD + 1], 1.0)
    nc.vector.memset(K.linv[:, :, :], 1.0)
    nc.vector.memset(K.m3[:, :], 0.0)
    nc.vector.memset(K.ks[:, :], 0.0)
    nc.vector.memset(K.qs[:, :], 0.0).then_inc(K.set_step, 1)
    dve.wait_ge(K.consts_loaded, 16)
    nc.vector.tensor_copy(K.identb[:, :], const("ident"))
    nc.vector.tensor_copy(K.identr[:, :], const("ident"))
    nc.vector.tensor_copy(K.causal[:, :], const("causal"))
    nc.vector.tensor_copy(K.causalT[:, :], const("causalT"))
    nc.vector.tensor_copy(K.sel[:, :, :], const("selc").unsqueeze(2).to_broadcast([T, H, T]))
    dve.wait_ge(K.rows_loaded, 16)
    dve.wait_ge(K.cols_loaded, 16)
    dve.wait_ge(K.masks_loaded, 16)
    for n in (1, 2):
        nc.vector.tensor_scalar(K.bqs[:, n - 1, :], K.row(f"bq{n}"), HD ** -0.5, None, ALU.mult)
    nc.vector.tensor_scalar(K.qn8[:, 0:1], K.col("qn_w"), HD3 ** -0.5, None, ALU.mult)
    nc.vector.tensor_scalar(K.qn8[:, 1:2], K.col("qn_b"), HD3 ** -0.5, None, ALU.mult)
    nc.vector.tensor_scalar(K.pcol[1][:, :, 0], K.mcol[:, 0, :], 1.0, -NEG, ALU.subtract, ALU.mult)
    nc.vector.tensor_scalar(K.pcol[2][:, :, 0], K.mcol[:, 1, :], NEG, 2.0, ALU.mult, ALU.mult)
    dve.wait_ge(K.set_step, 1)
    nc.vector.memset(K.qs[:, :].rearrange("p (h c) -> p h c", h=H)[:, :, 6 * HD], 1.0)
    z, t = K.row("scale0"), K.sp
    c = Chain(dve, K.sp_step, 0, 11)
    c.link(nc.vector.tensor_scalar(t[:, 0, :], z, -1.0, None, ALU.mult))
    c.link(nc.vector.tensor_tensor(t[:, 0, :], t[:, 0, :], z, ALU.min))
    dve.sem_inc(K.spz_ready, 1)
    dve.wait_ge(K.spe_ready, 1)
    c.link(nc.vector.tensor_scalar(t[:, 2, :], t[:, 1, :], 1.0, None, ALU.add))
    dve.sem_inc(K.spu_ready, 1)
    c.link(nc.vector.tensor_scalar(t[:, 3, :], t[:, 2, :], 1.0, None, ALU.is_equal))
    c.link(nc.vector.scalar_tensor_tensor(t[:, 4, :], t[:, 2, :], 1.0, t[:, 3, :], ALU.subtract, ALU.add))
    c.link(nc.vector.reciprocal(t[:, 4, :], t[:, 4, :]))
    dve.wait_ge(K.spl_ready, 1)
    c.link(nc.vector.tensor_tensor(t[:, 5, :], t[:, 5, :], t[:, 3, :], ALU.add))
    c.link(nc.vector.tensor_tensor(t[:, 5, :], t[:, 5, :], t[:, 1, :], ALU.mult))
    c.link(nc.vector.tensor_tensor(t[:, 5, :], t[:, 5, :], t[:, 4, :], ALU.mult))
    c.link(nc.vector.scalar_tensor_tensor(t[:, 5, :], z, 0.0, t[:, 5, :], ALU.max, ALU.add))
    c.link(nc.vector.reciprocal(K.isp[:, :], t[:, 5, :]))
    dve.sem_inc(K.isp_ready, 1)
    dve.wait_ge(K.isp_ready, 1)
    dve.wait_ge(K.lin_w_loaded, 48)
    isp2 = K.isp[:, :].unsqueeze(1).to_broadcast([D, 2, D])
    nc.vector.tensor_tensor(K.lin_w[:, 0:2, :], K.lin_w[:, 0:2, :], isp2, ALU.mult)
    biases = K.row2("bq0", "bk0").rearrange("p (a d) -> p a d", a=2)
    nc.vector.tensor_tensor(biases, biases, isp2, ALU.mult)
    nc.vector.tensor_scalar(K.epsr[:, :], K.isp[:, :], 1e-6, None, ALU.mult).then_inc(K.consts_ready, 1)
    dve.wait_ge(K.consts_ready, 1)


def setup_act(nc, act, K):
    act.preload_act_table_set(LN_EXP)
    act.wait_ge(K.spz_ready, 1)
    nc.scalar.activation(K.sp[:, 1, :], K.sp[:, 0, :], ACT.Exp).then_inc(K.spe_ready, 1)
    act.wait_ge(K.spu_ready, 1)
    nc.scalar.activation(K.sp[:, 5, :], K.sp[:, 2, :], ACT.Ln).then_inc(K.spl_ready, 1)


def before_layer2(nc, dve, K):
    dve.wait_ge(K.amf_loaded, 16)
    c = Chain(dve, K.part_step, 0, 4)
    for n, dst in enumerate((K.amask, K.amaskT)):
        src = K.amf[:, n, :]
        c.link(nc.vector.tensor_scalar(src, src, NEG, None, ALU.max))
        c.link(nc.vector.tensor_copy(dst[:, 0, :], src))
        nc.vector.tensor_tensor(dst[:, 1, :], src, dst[:, 0, :], ALU.subtract).then_inc(K.amask_ready, 1)


def before_layer3(nc, dve, K):
    for n, w in enumerate((K.w3qkv[:, 0, :], K.w3qkv[:, 1, :])):
        if n == 0:
            dve.wait_ge(K.w3_loaded, 64)
        heads = w.rearrange("p (h d) -> p h d", h=H)
        c = Chain(dve, K.centre_step, n, 2)
        c.link(nc.vector.reduce_sum(K.rec[:, :], heads, AX.X))
        c.link(nc.vector.tensor_scalar(K.rec[:, :], K.rec[:, :], -1.0 / HD3, None, ALU.mult))
        nc.vector.tensor_tensor(heads, heads, K.rec[:, :].unsqueeze(2).to_broadcast([T, H, HD3]),
                                ALU.add).then_inc(K.w3_centred, 1)
        dve.wait_ge(K.w3_centred, n + 1)
    nc.vector.memset(K.v3[:, :, :, HD3:HD3 + 1], 1.0)
    dve.wait_ge(K.int_loaded, 48)
    nc.vector.tensor_scalar(K.wint[:, :], K.wint[:, :].bitcast(I32), 1.0 / 127.0, None, ALU.mult).then_inc(K.deq_ready, 1)


def build(nc, a, out):
    ctx = ExitStack()
    with ctx:
        def sb(name, shape, dt=F32):
            return ctx.enter_context(nc.sbuf_tensor(name, shape, dt))

        K = Names()
        K.x = sb("x", [T, B, D])
        K.lin_w = sb("lin_w", [D, 3, D])
        K.x_loaded = [ctx.enter_context(nc.semaphore(f"x_loaded{n}")) for n in range(2)]
        K.wsmall = [sb(f"attn_w{n}", [D, 4, D]) for n in range(3)]
        early = sb("early", [128, 8192])
        w0_1 = early[:, 0:2048].rearrange("p (e n) -> p e n", e=E)
        w0_2 = early[:, 2048:4096].rearrange("p (e n) -> p e n", e=E)
        w0_3 = early[:, 4096:6144].rearrange("p (e h n) -> p e h n", e=E, h=2)
        K.x1 = early[:, 6144:8192].rearrange("p (b d) -> p b d", b=B)
        K.qk3 = early[:, 0:2048].rearrange("p (w n) -> p w n", w=2)
        K.qk3n = early[:, 2048:4096].rearrange("p (w n) -> p w n", w=2)
        K.sq3 = early[:, 4096:6144].rearrange("p (w n) -> p w n", w=2)
        qkT = early[:, 6144:8192].rearrange("p (c j q) -> p c j q", c=2, j=8)
        w1_2 = sb("w1_2", [128, E * 512])
        late = w1_2[:, :]
        K.q3T = qkT
        K.k3T = late[:, 0:2048].rearrange("p (c j q) -> p c j q", c=2, j=8)
        K.on3 = late[:, 2048:3072]
        K.o3T = late[:, 3072:4096].rearrange("p (j q) -> p j q", j=8)
        w1_2 = w1_2[:, :].rearrange("p (e h n) -> p e h n", e=E, h=4)
        w2_2 = early[:, 4096:8192].rearrange("p (e h n) -> p e h n", e=E, h=4)
        K.w_hi, K.w_lo = sb("w_hi", [128, E * 512], F32R), sb("w_lo", [128, E * 512], F32R)
        gates = sb("gates", [D, 3, E])
        b1s = sb("b1s", [128, 2, E * 4])
        b2s = sb("b2s", [E, 2, D])
        K.w3qkv = sb("w3qkv", [D, 3, H * HD3])
        K.wu = sb("wu", [128, 8, D])
        K.wint = sb("wint", [128, 9 * 128])
        K.v3 = sb("v3", [T, 2, H, HD3 + 1])
        K.rows, K.cols = sb("rows", [128, NROW]), sb("cols", [128, NCOL])
        K.row = lambda name: K.rows[:, ROW_AT[name][0]:ROW_AT[name][0] + ROW_AT[name][1]]
        K.row2 = lambda one, two: K.rows[:, ROW_AT[one][0]:ROW_AT[two][0] + ROW_AT[two][1]]
        K.col = lambda name: K.cols[:, COLS.index(name):COLS.index(name) + 1]
        K.consts = sb("consts", [128, NCONST])
        K.ident, K.blockmask = K.consts[:, CONST_AT["ident"]], K.consts[:, CONST_AT["blockmask"]]
        K.headmask = K.consts[:, CONST_AT["headmask"]]
        K.desc = K.consts[:, CONST_AT["desc"]]
        K.identb, K.causal = sb("identb", [T, T], BF16), sb("causalb", [T, T], BF16)
        K.causalT = sb("causalTb", [T, T], BF16)
        K.sel = sb("sel", [T, H, T], BF16)
        K.eps, K.bqs, K.qn8 = sb("eps", [128, 1]), sb("bqs", [T, 2, D]), sb("qn8", [128, 2])
        K.pcol = {1: sb("pcol1", [T, B, 1]), 2: sb("pcol2", [T, B, 1])}
        K.zeros = sb("zeros", [T, T], BF16)
        K.spare, K.one = sb("spare", [T, 1]), sb("one", [T, 1])
        K.mcol = sb("mcol", [T, 2, B], U8)
        K.amf = sb("amf", [T, 2, T])
        K.amask, K.amaskT, K.identr = sb("amask", [T, 2, T], F32R), sb("amaskT", [T, 2, T], F32R), sb("identr", [T, T], F32R)
        shared = sb("shared", [128, 2 * 4 * NT])
        K.sp, K.isp = shared[:, 2048:2816].rearrange("p (a d) -> p a d", a=6), sb("isp", [128, D])
        K.epsr = sb("epsr", [128, D])
        K.ctx, K.ctx_v, K.xT = sb("ctx", [D, 2, T]), sb("ctx_v", [D, 2, T]), sb("xT", [D, 2, T])
        K.xn, K.qkv = sb("xn", [T, D]), sb("qkv", [T, 3 * D])
        K.qs, K.ks = sb("qs", [T, H * 64], BF16), sb("ks", [T, H * 64], BF16)
        K.qt = shared[:, 0:1024].bitcast(BF16).rearrange("p (c j q) -> p c j q", c=2, j=8)
        K.kt = shared[:, 1024:2048].bitcast(BF16).rearrange("p (c j q) -> p c j q", c=2, j=8)
        K.heads, K.vaug, K.pt = sb("heads", [128, 4 * T]), sb("vaug", [T, 2, H, 32]), shared[:, 2048:3072].rearrange("p (c n) -> p c n", c=2)
        K.m, K.m3, K.mr, K.mT = sb("m", [T, H]), sb("m3", [T, T], BF16), sb("mr", [T, H]), sb("mT", [T, T], BF16)
        K.rec, K.on, K.oT, K.yb = sb("rec", [T, H]), sb("on", [T, D]), sb("oT", [D, T]), sb("yb", [T, D])
        K.y3 = sb("y3", [T, D])
        K.bn, K.mv, K.rs = sb("bn", [T, 6]), sb("mv", [T, 2, 2]), sb("rs", [T, 2, 2])
        K.lnv, K.var2, K.var2a = sb("lnv", [T, 2]), sb("var2", [T, 1]), sb("var2a", [T, 1])
        K.ss, K.lnh, K.rh = sb("ss", [T, 2 * H]), sb("lnh", [T, 2 * H]), sb("rh", [T, 2 * H])
        K.ft, K.f2, K.f3 = (shared[:, n:n + 256].rearrange("p (a d) -> p a d", a=2) for n in (0, 256, 512))
        K.fr, K.fs, K.lnr, K.froot = sb("fr", [T, 2]), sb("fs", [T, 4]), sb("lnr", [T, 2]), sb("froot", [T, 2])
        K.feat, K.linv = shared[:, 1024:1536].rearrange("p (c a d) -> p c a d", c=2, a=2), sb("linv", [T, 2, D + 1])
        K.lqT, K.kvblk = sb("lqT", [D, T]), sb("kvblk", [D, D + H])
        K.xg, K.xTg = sb("xg", [T, GB, D]), sb("xTg", [D, NT])
        K.xh, K.xl = sb("xh", [D, NT], F32R), sb("xl", [D, NT], F32R)
        K.hT = shared[:, :].rearrange("p (c h n) -> p c h n", c=2, h=4)
        K.silu = sb("silu", [128, 2, NT])
        K.bng, K.mvg, K.lng, K.rsg = sb("bng", [T, GB, 6]), sb("mvg", [T, GB, 2]), sb("lng", [T, GB]), sb("rsg", [T, GB])
        K.gl, K.g1, K.g2, K.wts = (sb(n, [T, GB, E]) for n in ("gl", "g1", "g2", "wts"))
        K.gm, K.gm1, K.gi, K.gs = (sb(n, [T, GB]) for n in ("gm", "gm1", "gi", "gs"))
        K.gd, K.ge = sb("gd", [T, GB * E]), sb("ge", [T, GB * E])
        K.wT = sb("wT", [E, NT])

        bank = [ctx.enter_context(nc.psum_tensor(f"bank{n}", [128, 512], F32)) for n in range(8)]
        K.pT, K.pP, K.pO, K.pM = bank[0], bank[1], bank[6], bank[7]
        K.pS, K.pC, K.pH, K.pY, K.pA, K.pO3 = bank[2:4], bank[4:6], bank[2:6], bank[6:8], bank[0:2], bank[6:8]
        K.pMb, K.pTb, K.pPb = (bank[n][:, :].bitcast(BF16) for n in (7, 0, 1))

        def sem(name):
            return ctx.enter_context(nc.semaphore(name))

        def sems(names):
            return [sem(name) for name in names.split()]

        K.a_done, K.a_ready, K.c3_ready, K.c_ready, K.centre_step = sems(
            "a_done a_ready c3_ready c_ready centre_step")
        K.cols_loaded, K.consts_loaded, K.consts_ready, K.deq_ready, K.exp3_done = sems(
            "cols_loaded consts_loaded consts_ready deq_ready exp3_done")
        K.exp_done, K.int_loaded, K.k3n_ready, K.ks_ready, K.ksplit_step = sems(
            "exp_done int_loaded k3n_ready ks_ready ksplit_step")
        K.kt_done, K.kt_ready, K.kv_done, K.l3_hr_step, K.l3_rec_step = sems(
            "kt_done kt_ready kv_done l3_hr_step l3_rec_step")
        K.l3_res_step, K.l3_rstd_ready, K.l3_rstd_step, K.l3_split_step, K.l3_stat_step = sems(
            "l3_res_step l3_rstd_ready l3_rstd_step l3_split_step l3_stat_step")
        K.l3_var_ready, K.l3_xn_ready, K.lin_f_ready, K.lin_f_step, K.lin_kv_done = sems(
            "l3_var_ready l3_xn_ready lin_f_ready lin_f_step lin_kv_done")
        K.lin_kv_ready, K.lin_o_done, K.lin_o_ready, K.lin_o_step, K.lin_p_done = sems(
            "lin_kv_ready lin_o_done lin_o_ready lin_o_step lin_p_done")
        K.lin_p_ready, K.lin_qT_done, K.lin_qT_ready, K.lin_ratio_ready, K.lin_root_ready = sems(
            "lin_p_ready lin_qT_done lin_qT_ready lin_ratio_ready lin_root_ready")
        K.lin_root_step, K.lin_rstd_ready, K.lin_rstd_step, K.lin_stat_step, K.lin_var_ready = sems(
            "lin_root_step lin_rstd_ready lin_rstd_step lin_stat_step lin_var_ready")
        K.isp_ready, K.lin_r_step, K.amask_ready, K.amf_loaded, K.w_hi_step, K.w_split, K.heads_done, K.hT_ready = sems(
            "isp_ready lin_r_step amask_ready amf_loaded w_hi_step w_split heads_done hT_ready")
        K.lin_w_loaded, K.lin_xT_done, K.lin_xT_ready, K.lin_xn_ready, K.m33_ready = sems(
            "lin_w_loaded lin_xT_done lin_xT_ready lin_xn_ready m33_ready")
        K.m3_ready, K.mT_done, K.mT_ready, K.masks_loaded, K.oT_done = sems(
            "m3_ready mT_done mT_ready masks_loaded oT_done")
        K.oT_ready, K.on3_done, K.on_ready, K.out_done, K.part_step = sems(
            "oT_ready on3_done on_ready out_done part_step")
        K.pv3_done, K.pv_done, K.q3n_ready, K.q_done = sems(
            "pv3_done pv_done q3n_ready q_done")
        K.qkv_ready, K.qs_ready, K.qsplit_step, K.qt_done, K.qt_ready = sems(
            "qkv_ready qs_ready qsplit_step qt_done qt_ready")
        K.rec_step, K.res_step, K.rh_ready, K.rows_loaded, K.rstd2_ready = sems(
            "rec_step res_step rh_ready rows_loaded rstd2_ready")
        K.rstd2_step, K.rstd_ready, K.rstd_step, K.s3_done, K.s3_ready = sems(
            "rstd2_step rstd_ready rstd_step s3_done s3_ready")
        K.s_ready, K.set_step, K.smax_done, K.sp_step, K.spe_ready = sems(
            "s_ready set_step smax_done sp_step spe_ready")
        K.spl_ready, K.split_step, K.spu_ready, K.spz_ready, K.sq_ready = sems(
            "spl_ready split_step spu_ready spz_ready sq_ready")
        K.ss_ready, K.stat_step, K.v_done, K.var2_ready, K.var2_step = sems(
            "ss_ready stat_step v_done var2_ready var2_step")
        K.var_ready, K.w3_centred, K.w3_loaded, K.x1_step, K.x3_done = sems(
            "var_ready w3_centred w3_loaded x1_step x3_done")
        K.xT_done, K.xT_ready, K.x_done, K.xn_ready = sems("xT_done xT_ready x_done xn_ready")
        K.y_done, K.y_ready = sems(
            "y_done y_ready")
        K.ctx_loaded = [ctx.enter_context(nc.semaphore(f"ctx_loaded{n}")) for n in range(2)]
        K.ctx_v_loaded = [ctx.enter_context(nc.semaphore(f"ctx_v_loaded{n}")) for n in range(2)]
        K.attn_w_loaded = [ctx.enter_context(nc.semaphore(f"attn_w_loaded{n}")) for n in range(3)]
        ffn_sems = {n: ctx.enter_context(nc.semaphore(f"ffn_{n}")) for n in FFN_COUNTS}
        K.ffn = {}
        for kind in range(4):
            F = Names()
            F.scale, F.w_loaded = 1.0, sem(f"ffn_w_loaded{kind}")
            at = {n: From(h, sum(FFN_COUNTS[n][:kind])) for n, h in ffn_sems.items()}
            F.var_ready, F.rstd_step, F.rstd_ready, F.stat_step, F.xn_ready, F.xT_ready, F.xT_done = (
                at[n] for n in "var_ready rstd_step rstd_ready stat_step xn_ready xT_ready xT_done".split())
            F.l_ready, F.d_ready, F.e_ready, F.w_ready, F.wT_ready, F.wT_done, F.a_ready = (
                at[n] for n in "l_ready d_ready e_ready w_ready wT_ready wT_done a_ready".split())
            F.b_ready, F.silu_done, F.h_ready, F.h_done, F.gate_step, F.y_ready, F.acc_done = (
                at[n] for n in "b_ready silu_done h_ready h_done gate_step y_ready acc_done".split())
            F.xh_ready, F.xl_ready = at["xh_ready"], at["xl_ready"]
            F.experts, F.blocks = (E, E, E, 1)[kind], (2, 4, 4, 3)[kind]
            F.ys = F.experts + (kind in (1, 2))
            K.ffn[kind] = F
        F0, F1, F2, F3 = (K.ffn[n] for n in range(4))
        F0.flat, F1.flat, F2.flat, F3.flat = early[:, 0:4096], early[:, 0:4096], early[:, 0:4096], K.wint[:, 0:768]
        for F in (F0, F1, F2, F3):
            total = F.flat.shape[1]
            F.chunk = total // (8 if F is not F3 else 2)
            both = [t.rearrange("p (m e n) -> p m e n", m=(2 if F in (F0, F3) else 1), e=F.experts)
                    for t in (K.w_hi[:, 0:total], K.w_lo[:, 0:total])]
            F.w1_hi, F.w1_lo = (t[:, 0] for t in both)
            if F in (F0, F3):
                F.w2_hi, F.w2_lo = (t[:, 1] for t in both)
        F0.w3, F0.gate = w0_3, gates[:, 0, :]
        for n, F, w2 in ((1, F1, w1_2), (2, F2, w2_2)):
            F.w3, F.gate, F.b1, F.b2 = w2, gates[:, n, :], b1s[:, n - 1, :], b2s[:, n - 1, :]
        F3.w3 = K.wint[:, 768:1152].rearrange("p (e h n) -> p e h n", e=1, h=3)
        F0.raw, F1.raw, F2.raw, F3.raw = [(F0.w_loaded, 64)], [(F1.w_loaded, 80)], [(F2.w_loaded, 80)], [(K.deq_ready, 1)]
        for n in range(4):
            K.ffn[n].loaded = K.ffn[n].raw + [(K.w_split, 8 * n + (8 if n < 3 else 2))]
        K.x_before_attn = {0: 16, 1: 33, 2: 50, 3: 67}
        K.x_before_ffn = {0: 32, 1: 49, 2: 66, 3: 68}

        block = ctx.enter_context(nc.Block())

        @block.sync
        def _(sp):
            sp.dma_start(K.rows[:, :], a["rows"].partition_broadcast(128)).then_inc(K.rows_loaded, 16)
            sp.dma_start(K.consts[:, :], a["consts"]).then_inc(K.consts_loaded, 16)
            sp.dma_start(K.x[:, 0:GB, :], a["x"][:, 0:GB, :]).then_inc(K.x_loaded[0], 16)
            sp.dma_start(K.x[:, GB:, :], a["x"][:, GB:, :]).then_inc(K.x_loaded[1], 16)
            sp.dma_start(K.cols[:, :], a["cols"]).then_inc(K.cols_loaded, 16)
            sp.dma_start(K.mcol[:, :, :].bitcast(I32), a["mcol"]).then_inc(K.masks_loaded, 16)
            ctxT = a["ctxT"]

            def load_ctx(s, to=K.ctx, loaded=K.ctx_loaded):
                src = ctxT[s.n] if s.static() else ctxT[bass.ds(s.n, 1)].rearrange("a d t -> d (a t)")
                sp.dma_start(to[:, s.par, :], src).then_inc(loaded[s.par], 16)

            def lin(s):
                if s.c >= 2 or not s.static():
                    wait(sp, K.lin_p_ready, s.n - 1)
                load_ctx(s)

            pipeline(sp, lin, 0, 0)
            sp.dma_start(K.amf[:, :, :], a["amf"]).then_inc(K.amf_loaded, 16)
            for lay in (1, 2):
                def attn(s):
                    wait(sp, K.qkv_ready, s.n + B * lay - 1)
                    load_ctx(s)
                sp.wait_ge(K.lin_p_ready, B)
                pipeline(sp, attn, 0, 0)
            sp.wait_ge(K.qkv_ready, 3 * B)
            uses = Uses()

            def attn3(s):
                uses.of(s)
                if s.exists() or s.c < 0:
                    wait(sp, K.a_ready, uses.start)
                if (s + 3).exists():
                    load_ctx(s + 3)
                if (s + 2).exists():
                    load_ctx(s + 2, K.ctx_v, K.ctx_v_loaded)

            pipeline(sp, attn3, 3, 1)
            for g in range(B // GB):
                wait(sp, K.ffn[3].acc_done, g + 1)
                sp.dma_start(out.rearrange("b t d -> t b d")[:, g * GB:(g + 1) * GB, :],
                             K.x[:, g * GB:(g + 1) * GB, :]).then_inc(K.out_done, 16)
            sp.wait_ge(K.out_done, 16 * (B // GB))

        @block.scalar
        def _(act):
            def load_layer(n):
                F, w2 = K.ffn[n], (w1_2, w2_2)[n - 1]
                act.dma_start(K.wsmall[n][:, :, :], a["attn_w"][n]).then_inc(K.attn_w_loaded[n], 64)
                act.dma_start(F.flat.rearrange("p (e n) -> p e n", e=E), a[f"w{n}_1"].rearrange("e d h -> d e h")).then_inc(F.w_loaded, 16)
                act.dma_start(w2, a[f"w{n}_2"]).then_inc(F.w_loaded, 16)
                act.dma_start(b1s[:, n - 1, :], a["b1s"][n - 1]).then_inc(F.w_loaded, 16)
                act.dma_start(b2s[:, n - 1, :], a["b2s"][n - 1]).then_inc(F.w_loaded, 32)

            act.dma_start(K.lin_w[:, :, :], a["lin_w"]).then_inc(K.lin_w_loaded, 48)
            setup_act(nc, act, K)
            act.dma_start(K.wsmall[0][:, :, :], a["attn_w"][0]).then_inc(K.attn_w_loaded[0], 64)
            act.dma_start(gates[:, :, :], a["gates"]).then_inc(F0.w_loaded, 16)
            lin_act(nc, act, K)
            act.dma_start(w0_1, a["w0_1"].rearrange("e d h -> d e h")).then_inc(F0.w_loaded, 16)
            act.dma_start(w0_2, a["w0_2"].rearrange("e d h -> d e h")).then_inc(F0.w_loaded, 16)
            act.dma_start(w0_3, a["w0_3"]).then_inc(F0.w_loaded, 16)
            attn_act(nc, act, K, 0)
            act.wait_ge(K.w_split, 8)
            load_layer(1)
            ffn_act(nc, act, K, 0)
            attn_act(nc, act, K, 1)
            act.wait_ge(K.w_split, 16)
            load_layer(2)
            ffn_act(nc, act, K, 1)
            act.dma_start(K.w3qkv[:, :, :], a["w3qkv"]).then_inc(K.w3_loaded, 48)
            act.dma_start(K.wu[:, :, :], a["wu"]).then_inc(K.w3_loaded, 16)
            act.dma_start(K.wint[:, :].bitcast(I32), a["wint"]).then_inc(K.int_loaded, 48)
            attn_act(nc, act, K, 2)
            ffn_act(nc, act, K, 2)
            attn3_act(nc, act, K)
            ffn_act(nc, act, K, 3)

        @block.vector
        def _(dve):
            setup_dve(nc, dve, K)
            lin_dve(nc, dve, K)
            for lay in range(3):
                if lay == 2:
                    before_layer2(nc, dve, K)
                attn_dve(nc, dve, K, lay)
                ffn_dve(nc, dve, K, lay)
            before_layer3(nc, dve, K)
            attn3_dve(nc, dve, K)
            ffn_dve(nc, dve, K, 3)

        @block.tensor
        def _(pe):
            lin_pe(nc, pe, K)
            for lay in range(3):
                if lay == 2:
                    pe.wait_ge(K.amask_ready, 2)
                attn_pe(nc, pe, K, lay)
                ffn_pe(nc, pe, K, lay)
            attn3_pe(nc, pe, K)
            ffn_pe(nc, pe, K, 3)

        @block.gpsimd
        def _(pool):
            for lay in range(3):
                attn_pool(nc, pool, K, lay)
            attn3_pool(nc, pool, K)


INPUTS = ["x", "ctxT", "lin_w", "attn_w", "gates", "w0_1", "w0_2", "w0_3", "w1_1", "w1_2", "w2_1", "w2_2", "b1s", "b2s",
          "w3qkv", "wu", "wint", "rows", "cols", "consts", "mcol", "amf"]


def constants(np):
    p, c = np.arange(128)[:, None], np.arange(128)[None, :]
    r16 = np.arange(16)[None, :]
    parts = {
        "ident": p == c, "blockmask": p // HD == c // HD, "headmask": p // HD == r16,
        "desc": np.zeros((128, 1)) + (E - np.arange(E)[None, :]),
        "selc": (p % H == r16) & (p < 3 * H), "causal": (c > p) * NEG, "causalT": (p > c) * NEG
    }
    return np.concatenate([np.asarray(parts[n], np.float32) for n, _ in CONSTS], axis=1)


def lay_out(np, v):
    f = {n: np.ascontiguousarray(a) for n, a in v.items()}
    d = {"x": f["x"].transpose(1, 0, 2), "ctxT": f["ctx_1024"].transpose(0, 2, 1)}
    d["lin_w"] = np.stack([f[f"L0_xattn_W{n}"] for n in "qkv"], 1)
    kv = f["L1_xattn_Wkv"]
    d["attn_w"] = np.stack([
        np.stack([f["L0_ffn_wq"], f["L0_ffn_wk"], f["L0_ffn_wv"], f["L0_ffn_wo"]], 1),
        np.stack([f["L1_xattn_Wq"], kv[:, :D], kv[:, D:], f["L1_xattn_Wp"]], 1),
        np.stack([f[f"L2_xattn_W{n}"].T for n in ("q", "k", "v", "out")], 1)])
    order = [unit_head(u, a) * HD + n for u in range(4) for a in range(G) for n in range(HD)]
    d["attn_w"][:, :, 3, :] = d["attn_w"][:, order, 3, :]
    d["gates"] = np.stack([f["L0_ffn_gate_w"], f["L1_ffn_w_gate"], f["L2_ffn_Wr"]], 1)
    d["w0_1"], d["w0_2"], d["w0_3"] = f["L0_ffn_w1"], f["L0_ffn_w2"], f["L0_ffn_w3"]
    d["w1_1"], d["w1_2"], d["w2_1"], d["w2_2"] = f["L1_ffn_W1"], f["L1_ffn_W2"], f["L2_ffn_W1"], f["L2_ffn_W2"]
    for n in ("w0_3", "w1_2", "w2_2"):
        d[n] = d[n].reshape(E, -1, 128, D).transpose(2, 0, 1, 3)
    d["b1s"] = np.stack([f[f"L{n}_ffn_b1"].reshape(E * 4, 128).T for n in (1, 2)])
    d["b2s"] = np.stack([f[f"L{n}_ffn_b2"] for n in (1, 2)])
    d["w3qkv"] = np.stack([f[f"L3_xattn_W{n}"].T for n in "qkv"], 1)
    d["wu"] = f["L3_xattn_Wu"].T.reshape(8, 128, D).transpose(1, 0, 2)
    down = f["L3_ffn_w_down"].T.reshape(3, 128, D).transpose(1, 0, 2).reshape(128, 3 * D)
    d["wint"] = np.concatenate([f["L3_ffn_w_gate"].T, f["L3_ffn_w_up"].T, down], 1)
    bkv = f["L1_xattn_bkv"]
    rows = {"bq0": "L0_xattn_bq", "bk0": "L0_xattn_bk", "bv0": "L0_xattn_bv", "scale0": "L0_xattn_scale", "bo": "L0_ffn_bo",
            "bq1": "L1_xattn_bq", "bq2": "L2_xattn_bq", "bk2": "L2_xattn_bk", "bp1": "L1_xattn_bp", "bv2": "L2_xattn_bv", "bout2": "L2_xattn_bout", "bu3": "L3_xattn_bu",
            "bg1": "L1_ffn_b_gate", "br2": "L2_ffn_br"}
    d["rows"] = np.concatenate([bkv[:D] if n == "bk1" else bkv[D:] if n == "bv1" else f[rows[n]].reshape(-1) for n, _ in ROWS])
    twice = lambda n: np.concatenate([f[n], f[n]])
    d["cols"] = np.stack([f["L0_ffn_ln1_scale"], f["L0_ffn_ln1_shift"], f["L0_ffn_ln2_scale"], f["L0_ffn_ln2_shift"],
                          twice("L3_xattn_qn_w"),
                          twice("L3_xattn_qn_b"), twice("L3_xattn_kn_w"), twice("L3_xattn_kn_b")], 1)
    d["consts"] = constants(np)
    m1, m2 = (f[n].view(np.uint8) for n in ("mask_BxS2_bf1", "mask_BxS2_bf0"))
    d["mcol"] = np.ascontiguousarray(np.stack([m1.T, m2.T], 1)).view(np.int32)
    d["amf"] = np.stack([f["mask_SxS2_ff0"], f["mask_SxS2_ff0"].T], 1)
    return {n: np.ascontiguousarray(d[n]) for n in INPUTS}


def kernel(**inputs):
    import numpy as np
    import concourse.bacc as bacc
    from concourse.bass_utils import run_bass_kernel_spmd

    nc = bacc.Bacc("TRN2", target_bir_lowering=False, num_devices=1)
    arrays = lay_out(np, inputs)
    a = {n: nc.dram_tensor(f"in_{n}", v.shape, mybir.dt.from_np(v.dtype), kind="ExternalInput").ap()
         for n, v in arrays.items()}
    out = nc.dram_tensor("out_x", (B, T, D), F32, kind="ExternalOutput").ap()
    build(nc, a, out)
    r = run_bass_kernel_spmd(nc, [{f"in_{n}": v for n, v in arrays.items()}], core_ids=[0])
    return r.results[0]["out_x"]
```
